# Optimizing a Trainium2 kernel written in Bass

```python
import numpy as np
import jax
import jax.numpy as jnp

def _softmax(x, axis=-1):
    return jax.nn.softmax(x, axis=axis)

def _gelu(x):
    return jax.nn.gelu(x, approximate=True)

def _silu(x):
    return jax.nn.silu(x)

def _sigmoid(x):
    return jax.nn.sigmoid(x)

def _layernorm(x, axis=-1, eps=1e-05):
    m = jnp.mean(x, axis=axis, keepdims=True)
    v = jnp.var(x, axis=axis, keepdims=True)
    return (x - m) / jnp.sqrt(v + eps)

def _scatter_add(tgt, idx, src, axis=0):
    return tgt.at[idx].add(src)

def _segment_sum(src, seg, n):
    return jax.ops.segment_sum(src, seg, n)
kernel_name = 'mk_audio_tower_d2_tok_audfeat768_r4_478e80'

def setup_inputs(seed: int=0):
    np.random.seed(seed)
    _w = jnp.asarray

    def _rec_inputs():
        import jax
        import jax.numpy as jnp
        _rk = jax.random.key(seed)
        x = 0.000106427 + 1.00001 * jax.random.normal(jax.random.fold_in(_rk, 1), (32, 125, 192), jnp.float32)
        return x
    x = _rec_inputs()

    def _L0_tok_setup():
        import jax, jax.numpy as jnp
        import numpy as np
        D_MODEL = 192
        SEGMENT_SIZE = 128
        DILATION_RATE = 2
        key = jax.random.key(seed)
        x = jax.random.normal(key, (4, 4096, D_MODEL), dtype=jnp.float32)
        return {'x': x}
    _L0_tok_all = _L0_tok_setup()
    _L0_tok_in = {k: v for k, v in _L0_tok_all.items() if k in ()}
    del _L0_tok_all

    def _L0_attn_setup():
        import math
        import jax, jax.numpy as jnp
        import numpy as np
        NUM_HEADS = 12
        EPS = 0.0001

        def softmax_kernel_features(data, proj, is_query):
            d = data.shape[-1]
            data_normalizer = 1.0 / math.sqrt(math.sqrt(d))
            ratio = 1.0 / math.sqrt(proj.shape[0])
            data_dash = jnp.einsum('bhnd,md->bhnm', data_normalizer * data, proj)
            diag_data = jnp.sum(jnp.square(data), axis=-1, keepdims=True) * 0.5 * data_normalizer * data_normalizer
            if is_query:
                stab = jnp.max(data_dash, axis=-1, keepdims=True)
            else:
                stab = jnp.max(data_dash)
            return ratio * (jnp.exp(data_dash - diag_data - stab) + EPS)
        key = jax.random.key(seed)
        k0, k1, k2, k3, k4 = jax.random.split(key, 5)
        B, N, C, H = (8, 1024, 192, NUM_HEADS)
        hd = C // H
        m = int(hd * math.log(hd))
        x = jax.random.normal(k0, (B, N, C), dtype=jnp.float32)
        W_qkv = jax.random.normal(k1, (C, 3 * C), dtype=jnp.float32) / math.sqrt(C)
        W_proj = jax.random.normal(k2, (C, C), dtype=jnp.float32) / math.sqrt(C)
        b_proj = jnp.zeros((C,), dtype=jnp.float32)
        proj_mat = jax.random.normal(k3, (m, hd), dtype=jnp.float32)
        return {'x': x, 'W_qkv': W_qkv, 'W_proj': W_proj, 'b_proj': b_proj, 'proj_mat': proj_mat}
    _L0_attn_all = _L0_attn_setup()
    _L0_attn_in = {k: v for k, v in _L0_attn_all.items() if k in ('W_qkv', 'W_proj', 'b_proj', 'proj_mat')}
    del _L0_attn_all

    def _L0_ffn_setup():
        import jax, jax.numpy as jnp
        import numpy as np
        import math
        B, T, C = (8, 512, 192)
        E = 3
        HD = C // E
        TOPK = 2
        NGLOB = 4

        def _masked_softmax(att, mask):
            att = jnp.where(mask, -jnp.inf, att)
            return jax.nn.softmax(att, axis=-1)
        key = jax.random.key(seed)
        ks = jax.random.split(key, 16)
        s = 0.02
        return {'x': jax.random.normal(ks[0], (B, T, C), jnp.float32), 'Wqk': jax.random.normal(ks[1], (C, 2 * C), jnp.float32) * s, 'bqk': jnp.zeros((2 * C,), jnp.float32), 'Wv': jax.random.normal(ks[2], (E, C, HD), jnp.float32) * s, 'bv': jnp.zeros((E, HD), jnp.float32), 'conv_w': jax.random.normal(ks[3], (HD, 1, 3), jnp.float32) * s, 'conv_b': jnp.zeros((HD,), jnp.float32), 'glob': jax.random.normal(ks[4], (NGLOB, HD), jnp.float32) * 0.02, 'pos_bias': jnp.zeros((64, 64), jnp.float32), 'Wg1': jax.random.normal(ks[5], (C, 32), jnp.float32) * s, 'bg1': jnp.zeros((32,), jnp.float32), 'Wg2': jax.random.normal(ks[6], (32, E), jnp.float32) * s, 'bg2': jnp.zeros((E,), jnp.float32), 'Wp': jax.random.normal(ks[7], (C, C), jnp.float32) * s, 'bp': jnp.zeros((C,), jnp.float32)}
    _L0_ffn_all = _L0_ffn_setup()
    _L0_ffn_in = {k: v for k, v in _L0_ffn_all.items() if k in ('Wqk', 'bqk', 'Wv', 'bv', 'conv_w', 'conv_b', 'glob', 'pos_bias', 'Wg1', 'bg1', 'Wg2', 'bg2', 'Wp', 'bp')}
    del _L0_ffn_all

    def _L1_attn_setup():
        import jax, jax.numpy as jnp
        import numpy as np
        B, N, C = (2, 1024, 192)
        H = 12
        HD = C // H
        THETA = 10000.0

        def _rope_tables(n, hd, dtype):
            inv = 1.0 / THETA ** (jnp.arange(0, hd, 2, dtype=jnp.float32) / hd)
            freqs = jnp.arange(n, dtype=jnp.float32)[:, None] * inv[None, :]
            cos = jnp.concatenate([jnp.cos(freqs), jnp.cos(freqs)], axis=-1).astype(dtype)
            sin = jnp.concatenate([jnp.sin(freqs), jnp.sin(freqs)], axis=-1).astype(dtype)
            return (cos, sin)

        def _rotate_half(x):
            x1, x2 = (x[..., :x.shape[-1] // 2], x[..., x.shape[-1] // 2:])
            return jnp.concatenate([-x2, x1], axis=-1)
        key = jax.random.key(seed)
        k1, k2, k3 = jax.random.split(key, 3)
        x = jax.random.normal(k1, (B, N, C), dtype=jnp.float32)
        w_qkv = jax.random.normal(k2, (3 * C, C), dtype=jnp.float32) * C ** (-0.5)
        b_qkv = jnp.zeros((3 * C,), dtype=jnp.float32)
        w_proj = jax.random.normal(k3, (C, C), dtype=jnp.float32) * C ** (-0.5)
        b_proj = jnp.zeros((C,), dtype=jnp.float32)
        return {'x': x, 'w_qkv': w_qkv, 'b_qkv': b_qkv, 'w_proj': w_proj, 'b_proj': b_proj}
    _L1_attn_all = _L1_attn_setup()
    _L1_attn_in = {k: v for k, v in _L1_attn_all.items() if k in ('w_qkv', 'b_qkv', 'w_proj', 'b_proj')}
    del _L1_attn_all

    def _L1_ffn_setup():
        import jax, jax.numpy as jnp
        import numpy as np
        B, S, D, F, E = (2, 256, 192, 768, 8)
        key = jax.random.key(seed)
        k0, k1, k2, k3, k4, k5 = jax.random.split(key, 6)
        scale = 0.02
        return {'hidden_states': jax.random.normal(k0, (B, S, D), dtype=jnp.float32), 'Wg': jax.random.normal(k1, (D, E), dtype=jnp.float32) * scale, 'W1': jax.random.normal(k2, (E, D, F), dtype=jnp.float32) * scale, 'b1': jnp.zeros((E, F), dtype=jnp.float32), 'W2': jax.random.normal(k3, (E, F, D), dtype=jnp.float32) * scale, 'b2': jnp.zeros((E, D), dtype=jnp.float32)}
    _L1_ffn_all = _L1_ffn_setup()
    _L1_ffn_in = {k: v for k, v in _L1_ffn_all.items() if k in ('Wg', 'W1', 'b1', 'W2', 'b2')}
    del _L1_ffn_all
    return {'x': x, 'L0_attn_W_qkv': _L0_attn_in['W_qkv'], 'L0_attn_W_proj': _L0_attn_in['W_proj'], 'L0_attn_b_proj': _L0_attn_in['b_proj'], 'L0_attn_proj_mat': _L0_attn_in['proj_mat'], 'L0_ffn_Wqk': _L0_ffn_in['Wqk'], 'L0_ffn_bqk': _L0_ffn_in['bqk'], 'L0_ffn_Wv': _L0_ffn_in['Wv'], 'L0_ffn_bv': _L0_ffn_in['bv'], 'L0_ffn_conv_w': _L0_ffn_in['conv_w'], 'L0_ffn_conv_b': _L0_ffn_in['conv_b'], 'L0_ffn_glob': _L0_ffn_in['glob'], 'L0_ffn_pos_bias': _L0_ffn_in['pos_bias'], 'L0_ffn_Wg1': _L0_ffn_in['Wg1'], 'L0_ffn_bg1': _L0_ffn_in['bg1'], 'L0_ffn_Wg2': _L0_ffn_in['Wg2'], 'L0_ffn_bg2': _L0_ffn_in['bg2'], 'L0_ffn_Wp': _L0_ffn_in['Wp'], 'L0_ffn_bp': _L0_ffn_in['bp'], 'L1_attn_w_qkv': _L1_attn_in['w_qkv'], 'L1_attn_b_qkv': _L1_attn_in['b_qkv'], 'L1_attn_w_proj': _L1_attn_in['w_proj'], 'L1_attn_b_proj': _L1_attn_in['b_proj'], 'L1_ffn_Wg': _L1_ffn_in['Wg'], 'L1_ffn_W1': _L1_ffn_in['W1'], 'L1_ffn_b1': _L1_ffn_in['b1'], 'L1_ffn_W2': _L1_ffn_in['W2'], 'L1_ffn_b2': _L1_ffn_in['b2']}

def reference(x, L0_attn_W_qkv, L0_attn_W_proj, L0_attn_b_proj, L0_attn_proj_mat, L0_ffn_Wqk, L0_ffn_bqk, L0_ffn_Wv, L0_ffn_bv, L0_ffn_conv_w, L0_ffn_conv_b, L0_ffn_glob, L0_ffn_pos_bias, L0_ffn_Wg1, L0_ffn_bg1, L0_ffn_Wg2, L0_ffn_bg2, L0_ffn_Wp, L0_ffn_bp, L1_attn_w_qkv, L1_attn_b_qkv, L1_attn_w_proj, L1_attn_b_proj, L1_ffn_Wg, L1_ffn_W1, L1_ffn_b1, L1_ffn_W2, L1_ffn_b2):
    import jax
    import jax.numpy as jnp

    def _L0_tok_ref(x):
        import jax, jax.numpy as jnp
        import numpy as np
        D_MODEL = 192
        SEGMENT_SIZE = 128
        DILATION_RATE = 2
        B, S, D = x.shape
        pad = -S % SEGMENT_SIZE
        if pad:
            x = jnp.pad(x, ((0, 0), (0, pad), (0, 0)))
        xs = x.reshape(B, -1, SEGMENT_SIZE, D)[:, :, ::DILATION_RATE, :]
        scale = 1.0 / jnp.sqrt(jnp.asarray(D, dtype=x.dtype))
        scores = jnp.einsum('bnqd,bnkd->bnqk', xs, xs) * scale
        attn = jax.nn.softmax(scores, axis=-1)
        out = jnp.einsum('bnqk,bnkd->bnqd', attn, xs)
        return out.reshape(B, -1, D)

    def _L0_attn_ref(x, W_qkv, W_proj, b_proj, proj_mat):
        import math
        import jax, jax.numpy as jnp
        import numpy as np
        NUM_HEADS = 12
        EPS = 0.0001

        def softmax_kernel_features(data, proj, is_query):
            d = data.shape[-1]
            data_normalizer = 1.0 / math.sqrt(math.sqrt(d))
            ratio = 1.0 / math.sqrt(proj.shape[0])
            data_dash = jnp.einsum('bhnd,md->bhnm', data_normalizer * data, proj)
            diag_data = jnp.sum(jnp.square(data), axis=-1, keepdims=True) * 0.5 * data_normalizer * data_normalizer
            if is_query:
                stab = jnp.max(data_dash, axis=-1, keepdims=True)
            else:
                stab = jnp.max(data_dash)
            return ratio * (jnp.exp(data_dash - diag_data - stab) + EPS)
        B, N, C = x.shape
        H = NUM_HEADS
        hd = C // H
        qkv = (x @ W_qkv).reshape(B, N, 3, H, hd)
        qkv = jnp.transpose(qkv, (2, 0, 3, 1, 4))
        q, k, v = (qkv[0], qkv[1], qkv[2])
        q1 = softmax_kernel_features(q, proj_mat, is_query=True)
        k1 = softmax_kernel_features(k, proj_mat, is_query=False)
        kv = jnp.einsum('bhnm,bhnd->bhmd', k1, v)
        ksum = jnp.sum(k1, axis=2)
        z = 1.0 / jnp.einsum('bhnm,bhm->bhn', q1, ksum)
        out = jnp.einsum('bhnm,bhmd->bhnd', q1, kv) * z[..., None]
        out = jnp.transpose(out, (0, 2, 1, 3)).reshape(B, N, C)
        return out @ W_proj + b_proj

    def _L0_ffn_ref(x, Wqk, bqk, Wv, bv, conv_w, conv_b, glob, pos_bias, Wg1, bg1, Wg2, bg2, Wp, bp):
        import jax, jax.numpy as jnp
        import numpy as np
        import math
        B, T, C = (8, 512, 192)
        E = 3
        HD = C // E
        TOPK = 2
        NGLOB = 4

        def _masked_softmax(att, mask):
            att = jnp.where(mask, -jnp.inf, att)
            return jax.nn.softmax(att, axis=-1)
        Bx, Tx, Cx = x.shape
        scale = 1.0 / math.sqrt(HD)
        gate = jax.nn.softmax(jax.nn.relu(x @ Wg1 + bg1) @ Wg2 + bg2, axis=-1)
        top_w, top_i = jax.lax.top_k(gate, TOPK)
        top_w = jax.nn.softmax(top_w, axis=-1)
        qk = x @ Wqk + bqk
        q, k = (qk[..., :Cx], qk[..., Cx:])
        q = q.reshape(Bx, Tx, E, HD)
        k = k.reshape(Bx, Tx, E, HD)
        rows = jnp.arange(Tx)[:, None]
        ys = []
        for e in range(E):
            qe = q[:, :, e]
            ke = k[:, :, e]
            ve = x @ Wv[e] + bv[e]
            if e == 0:
                qc = jnp.transpose(qe, (0, 2, 1))
                qc = jax.lax.conv_general_dilated(qc, conv_w, window_strides=(1,), padding=((1, 1),), feature_group_count=HD, dimension_numbers=('NCH', 'OIH', 'NCH'))
                qe = jnp.transpose(qc + conv_b[None, :, None], (0, 2, 1))
            elif e == 1:
                gb = jnp.broadcast_to(glob[None], (Bx, NGLOB, HD))
                ke = jnp.concatenate([ke, gb], axis=1)
                ve = jnp.concatenate([ve, gb], axis=1)
            att = jnp.einsum('btd,bsd->bts', qe, ke) * scale
            if e == 2 and Tx <= 64:
                att = att + pos_bias[:Tx, :Tx][None]
            S = att.shape[-1]
            mask = jnp.arange(S)[None, :] > rows
            att = _masked_softmax(att, mask[None])
            ys.append(jnp.einsum('bts,bsd->btd', att, ve))
        ys = jnp.stack(ys, axis=2)
        w_e = jnp.sum(jax.nn.one_hot(top_i, E, dtype=x.dtype) * top_w[..., None], axis=-2)
        combined = (ys * w_e[..., None]).reshape(Bx, Tx, Cx)
        return combined @ Wp + bp

    def _L1_attn_ref(x, w_qkv, b_qkv, w_proj, b_proj):
        import jax, jax.numpy as jnp
        import numpy as np
        B, N, C = (2, 1024, 192)
        H = 12
        HD = C // H
        THETA = 10000.0

        def _rope_tables(n, hd, dtype):
            inv = 1.0 / THETA ** (jnp.arange(0, hd, 2, dtype=jnp.float32) / hd)
            freqs = jnp.arange(n, dtype=jnp.float32)[:, None] * inv[None, :]
            cos = jnp.concatenate([jnp.cos(freqs), jnp.cos(freqs)], axis=-1).astype(dtype)
            sin = jnp.concatenate([jnp.sin(freqs), jnp.sin(freqs)], axis=-1).astype(dtype)
            return (cos, sin)

        def _rotate_half(x):
            x1, x2 = (x[..., :x.shape[-1] // 2], x[..., x.shape[-1] // 2:])
            return jnp.concatenate([-x2, x1], axis=-1)
        b, n, c = x.shape
        scale = HD ** (-0.5)
        qkv = jnp.einsum('bnc,dc->bnd', x, w_qkv) + b_qkv
        qkv = qkv.reshape(b, n, 3, H, HD).transpose(2, 0, 3, 1, 4)
        q, k, v = (qkv[0], qkv[1], qkv[2])
        cos, sin = _rope_tables(n, HD, x.dtype)
        q = q * cos + _rotate_half(q) * sin
        k = k * cos + _rotate_half(k) * sin
        attn = jnp.einsum('bhqd,bhkd->bhqk', q, k) * scale
        attn = jax.nn.softmax(attn, axis=-1)
        out = jnp.einsum('bhqk,bhkd->bhqd', attn, v)
        out = out.transpose(0, 2, 1, 3).reshape(b, n, c)
        return jnp.einsum('bnc,dc->bnd', out, w_proj) + b_proj

    def _L1_ffn_ref(hidden_states, Wg, W1, b1, W2, b2):
        import jax, jax.numpy as jnp
        import numpy as np
        B, S, D, F, E = (2, 256, 192, 768, 8)
        b, s, d = hidden_states.shape
        e = W1.shape[0]
        x = hidden_states.reshape(-1, d)
        logits = x @ Wg
        probs = jax.nn.softmax(logits, axis=-1)
        gate = jnp.max(probs, axis=-1)
        expert_idx = jnp.argmax(probs, axis=-1)
        h = jax.nn.silu(jnp.einsum('td,edf->etf', x, W1) + b1[:, None, :])
        y = jnp.einsum('etf,efd->etd', h, W2) + b2[:, None, :]
        combine = jax.nn.one_hot(expert_idx, e, dtype=x.dtype) * gate[:, None]
        out = jnp.einsum('te,etd->td', combine, y)
        return out.reshape(b, s, d)
    h = _L0_tok_ref(x)
    h = h + _L0_attn_ref(_layernorm(h, axis=-1), L0_attn_W_qkv, L0_attn_W_proj, L0_attn_b_proj, L0_attn_proj_mat)
    h = h + _L0_ffn_ref(_layernorm(h, axis=-1), L0_ffn_Wqk, L0_ffn_bqk, L0_ffn_Wv, L0_ffn_bv, L0_ffn_conv_w, L0_ffn_conv_b, L0_ffn_glob, L0_ffn_pos_bias, L0_ffn_Wg1, L0_ffn_bg1, L0_ffn_Wg2, L0_ffn_bg2, L0_ffn_Wp, L0_ffn_bp)
    h = h + _L1_attn_ref(_layernorm(h, axis=-1), L1_attn_w_qkv, L1_attn_b_qkv, L1_attn_w_proj, L1_attn_b_proj)
    h = h + _L1_ffn_ref(_layernorm(h, axis=-1), L1_ffn_Wg, L1_ffn_W1, L1_ffn_b1, L1_ffn_W2, L1_ffn_b2)
    return h

_drawn_inputs = setup_inputs


def setup_inputs(seed=0):
    import zlib

    import numpy as np

    out = dict(_drawn_inputs(seed))
    spreads = {'L0_attn_b_proj': (0.0, 0.1),
     'L0_ffn_bqk': (0.0, 0.8),
     'L0_ffn_bv': (0.0, 0.496),
     'L0_ffn_conv_b': (0.0, 0.8),
     'L0_ffn_pos_bias': (0.0, 0.8),
     'L0_ffn_bg1': (0.0, 0.8),
     'L0_ffn_bg2': (0.0, 0.435),
     'L0_ffn_bp': (0.0, 0.1),
     'L1_attn_b_qkv': (0.0, 0.1),
     'L1_attn_b_proj': (0.0, 0.1),
     'L1_ffn_b1': (0.0, 0.8),
     'L1_ffn_b2': (0.0, 0.457)}
    factors = {'L0_ffn_Wqk': 8.0,
     'L0_ffn_Wv': 4.47,
     'L0_ffn_conv_w': 8.0,
     'L0_ffn_Wg1': 8.0,
     'L0_ffn_Wg2': 8.0,
     'L0_ffn_Wp': 2.917,
     'L1_ffn_W1': 4.142,
     'L1_ffn_W2': 3.842}
    for name, (base, spread) in spreads.items():
        noise = np.random.default_rng([zlib.crc32(name.encode()), seed]).standard_normal(out[name].shape)
        drawn = base * np.exp(spread * noise) if base else spread * noise
        out[name] = jnp.asarray(drawn.astype(out[name].dtype))
    for name, factor in factors.items():
        out[name] = (out[name] * factor).astype(out[name].dtype)
    return out
```

```python
from contextlib import ExitStack

import numpy as np
import concourse.bass as bass
from concourse import mybir

F32 = mybir.dt.float32
BF16 = mybir.dt.bfloat16
I32 = mybir.dt.int32
U32 = mybir.dt.uint32
ALU = mybir.AluOpType
ACT = mybir.ActivationFunctionType
AX = mybir.AxisListType.X

SEQS, SEQ_IN, D = 32, 125, 192
T = 64
P = 128
TOKENS = SEQS * T
TILES = TOKENS // P
TURNS = TILES // 2
C = D // 2
H, HD = 12, 16
HC = H // 2
M = 44
FEPS = 1e-4
LNEPS = 1e-5
E3, HD3 = 3, 64
EX, FF = 8, 768
FT = FF // P
SLOT_TILES = (TOKENS + EX * (P - 1)) // P
SLOT_TILES += SLOT_TILES % 2
BIG = -1e30

_W = {}
_n = 0
for _name, _cols in (("a_qkv", 2 * 3 * D), ("feat", HC * M), ("a_out", 2 * D), ("f_qk", 2 * 2 * D), ("f_v", 2 * D),
                     ("f_g1", 2 * 32), ("f_g2", E3), ("f_out", 2 * D), ("conv", 4), ("l_qkv", 2 * 3 * D),
                     ("l_out", 2 * D), ("m_g", 2 * EX)):
    _W[_name] = (_n, _n + _cols)
    _n += _cols
NW = _n
NW_A = _W["feat"][1]

_K = {}
_n = 0
for _name, _cols in (("ident", P), ("half", P), ("split", P), ("block", HC * M), ("diag", HC), ("causal", P),
                     ("kvmask", 68), ("cos", 2 * D), ("sin", 2 * D), ("triu", P), ("eidx", E3), ("eord", EX),
                     ("thr", TILES), ("slot", SLOT_TILES), ("eps", 3)):
    _K[_name] = (_n, _n + _cols)
    _n += _cols
NK = _n


def shape_constants():
    k = np.zeros((P, NK), np.float32)

    def put(name, rows, value):
        a, b = _K[name]
        k[:rows, a:b] = value

    put("ident", P, np.eye(P))
    seq = np.arange(P) // T
    put("half", 2, np.stack([seq == 0, seq == 1]))
    put("split", 2, BIG * np.stack([seq == 1, seq == 0]))
    blk = np.zeros((C, HC, M))
    for h in range(HC):
        blk[16 * h:16 * h + 16, h] = HD ** -0.25
    put("block", C, blk.reshape(C, -1))
    dg = np.zeros((C, HC))
    for h in range(HC):
        dg[16 * h:16 * h + 16, h] = 0.5 * HD ** -0.5
    put("diag", C, dg)
    q, s = np.arange(P)[:, None], np.arange(P)[None, :]
    put("causal", P, np.where((q // T == s // T) & (s <= q), 0.0, BIG))
    kv = np.zeros((2 * M, 2, 2, 17))
    for par in range(2):
        kv[M * par:M * par + M, :, par] = 1.0
    put("kvmask", 2 * M, kv.reshape(2 * M, -1))
    inv = (1.0 / np.float32(10000.0) ** (np.arange(0, HD, 2, dtype=np.float32) / np.float32(HD))).astype(np.float32)
    fr = (np.arange(T, dtype=np.float32)[:, None] * inv[None, :]).astype(np.float32)
    cos, sin = np.cos(fr.astype(np.float64)), np.sin(fr.astype(np.float64))
    cos, sin = np.tile(cos, (2, 1)), np.tile(sin, (2, 1))
    cos = np.concatenate([cos, cos], -1)
    sin = np.concatenate([-sin, sin], -1)
    scale = np.array([HD ** -0.5, 1.0])[None, :, None, None]
    put("cos", P, (cos[:, None, None, :] * scale * np.ones((1, 1, H, 1))).reshape(P, -1))
    put("sin", P, (sin[:, None, None, :] * scale * np.ones((1, 1, H, 1))).reshape(P, -1))
    put("triu", P, (q < s).astype(np.float32))
    put("eidx", P, np.arange(1, E3 + 1))
    put("eord", P, EX - np.arange(EX))
    put("thr", P, P * np.arange(TILES))
    put("slot", P, np.arange(SLOT_TILES))
    put("eps", P, np.array([LNEPS, -0.5, FEPS]))
    return k


def audio_tower(nc, x, weights, consts, pos_bias, w1, w2, b2, out):
    ctx = ExitStack()
    with ctx:
        def sb(name, shape, dt=F32):
            return ctx.enter_context(nc.sbuf_tensor(name, shape, dt))

        def two(name, shape, dt=F32):
            return [sb(f"{name}{u}", shape, dt) for u in range(2)]

        def sem(name):
            return ctx.enter_context(nc.semaphore(name))

        def ev(name):
            return [sem(name)] * 2

        def ev_dma(name):
            return [sem(f"{name}_{u}") for u in range(2)]

        xs_dram = nc.dram_tensor("sorted_x", (SLOT_TILES * P, D), F32, kind="Internal").ap()
        ys_dram = nc.dram_tensor("sorted_y", (SLOT_TILES * P, D), F32, kind="Internal").ap()

        W = sb("weights_sb", [C + 1, NW])
        K = sb("consts_sb", [P, NK])

        def wv(name, c=None, rows=C):
            a, b = _W[name]
            if c is not None:
                n = (b - a) // 2
                a, b = a + c * n, a + c * n + n
            return W[0:rows, a:b]

        def kc(name, rows=P):
            return K[0:rows, _K[name][0]:_K[name][1]]

        ident = kc("ident")
        bf_ident = sb("bf_ident", [P, P], BF16)
        bf_causal = sb("bf_causal", [P, P], BF16)
        bf_half = sb("bf_half", [2, P], BF16)
        bf_split = sb("bf_split", [2, P], BF16)
        feat = sb("feat_blocks", [C, HC * M])
        bias_mask = sb("bias_mask", [P, P])
        ones_row = sb("ones_row", [1, P])
        ones_sq = sb("ones_sq", [P, P])

        h_all = sb("h_all", [P, TILES, D])
        x_all = sb("x_all", [P, TILES, 2 * P])
        stash = sb("stash", [P, TILES * (H * M + HC * 68)])
        kd_all = stash[:, 0:TILES * H * M].rearrange("p (t n) -> p t n", t=TILES)
        vbd_all = stash[:, TILES * H * M:].rearrange("p (t n) -> p t n", t=TILES)
        w1_sb = stash[:, 0:EX * 2 * FF]
        w2_sb = sb("w2_sb", [P, EX * FT * D])
        b2_sb = sb("b2_sb", [1, EX * D])
        kmx_all = sb("kmx_all", [P, TILES])
        kmax = sb("kmax", [P, 4])
        lg_all = sb("lg_all", [P, TILES, EX])

        actT = two("actT", [C + 1, 2 * P])
        xnT = two("xnT", [C + 1, 2 * P])
        hs = two("hs", [P, D])
        xn = two("xn", [P, D])
        att = two("att", [P, D])
        stats = two("stats", [P, 16])
        small = two("small", [P, 64])
        big_a = two("big_a", [P, FF])
        big_b = two("big_b", [P, FF])
        big_c = two("big_c", [P, FF])
        xin = [b[:, 0:D] for b in big_c]
        qe = [b[:, 0:H * M] for b in big_c]
        qkT = [b[0:C, 0:2 * P] for b in big_b]
        qksq = [b[0:C, 2 * P:4 * P] for b in big_b]
        k1 = two("k1", [P, H * M])
        kvs = two("kvs", [2 * M, HC * 68])
        pad = two("pad", [P, 2 * 3 * 4 * 32])
        zeros = pad[0][:, 0:D]
        vl = two("vl", [P, 2 * HC * 34])
        vf = two("vf", [P, E3 * (HD3 + 1)])
        g1T = two("g1T", [33, P])
        qc = two("qc", [HD3, P])

        rsm = sb("router_small", [P, 192])
        gate = sb("gate", [P, TILES])
        slots = sb("slots", [P, TILES], U32)
        tile_ex = sb("tile_ex", [P, SLOT_TILES], I32)

        ps = ctx.enter_context(nc.psum_tensor("ps", [P, 8, 512], F32))

        consts_in, wa_in, wb_in, moe_in = sem("consts_in"), sem("wa_in"), sem("wb_in"), sem("moe_in")
        w1_in, zero_out = sem("w1_in"), sem("zero_out")
        setup_v, setup_pe, ready, ready_p = sem("setup_v"), sem("setup_pe"), sem("ready"), sem("ready_p")
        x_in = ev_dma("x_in")
        S = {n: ev(n) for n in """
            xT_ps xT_sb sc_ps nmx p_sb pT_ps pT_sb px_ps hstore xstore kT_ps v_ps k_sb vbd dash_ps kd
            hrow mv var_eps rstd xnr xnT_ps xnT_sb attr attT_ps attT_sb pr_ps
            k1e k1 qT_ps q_sb kv_ps qd_ps kv_sb qe qx q1T_ps q1T_sb num_ps
            g1_ps fqk_ps fv_ps g1_sb qf_sb vf_sb kf_sb conv gl_ps gs ge gp gep fs_ps nf fp_sb fpT_ps fpT_sb fo_ps
            lqk_ps lv_ps lqk_sb lv_a lv_d rope lT_ps lT_sb ls_ps pl px lpT_ps lpT_sb lo_ps store lg_ps lg
            """.split()}
        k_max, k_maxall, k_negmax = sem("k_max"), sem("k_maxall"), sem("k_negmax")
        vstep, pstep = sem("vstep"), sem("pstep")
        r_diff, r_exp, r_onehot, r_count, r_slots = (sem(n) for n in ("r_diff", "r_exp", "r_onehot", "r_count", "r_slots"))
        scattered, gathered, out_row, out_done = sem("scattered"), [sem(f"gathered{j}") for j in range(4)], sem("out_row"), sem("out_done")
        Z = {n: ev("m_" + n) for n in "xT_ps xT_sb h_ps h_sb hT_ps hT_sb y_ps y_sb".split()}
        Z.update({n: ev_dma("m_" + n) for n in ("x_in", "y_out")})
        block = ctx.enter_context(nc.Block())

        def bank(u, b):
            return ps[:, 4 * u + b, :]

        def banks(u, a, b):
            return ps[:, 4 * u + a:4 * u + b, :]

        def turn(eng, i):
            return [eng.snap(i * 2 + u + 1) for u in range(2)]

        CREDIT = 1

        def give_credit(eng, sems):
            for s in sems:
                eng.sem_inc(s, CREDIT)

        def stage_counts(eng, i):
            return [[[eng.snap(i * 6 + (before + 2 * r + u + 1)) for u in range(2)] for r in range(3)] for before in (0, TILES)]

        def v_rows(u, b, par):
            return bank(u, 2)[T * b:T * b + T, 0:D].rearrange("p (c r d) -> p c r d", c=HC, r=2)[:, :, par, :]

        def v_place(u, b, par):
            return vl[u][T * par:T * par + T, :].rearrange("p (b c r d) -> p b c r d", b=2, c=HC, r=2)[:, b, :, par, 0:HD]

        def features(pe, u):
            for half in range(2):
                pe.matmul(bank(u, 2 + half)[:, 0:HC * M], qkT[u][:, half * P:half * P + P], feat[:, :], start=True, stop=True)
            for half in range(2):
                last = pe.matmul(bank(u, 3)[:, 264 + HC * half:264 + HC * half + HC], qksq[u][:, half * P:half * P + P], kc("diag", C),
                                 start=True, stop=True)
            return last

        def y_rows(t):
            return [qe, k1][t % 2][t // 2 % 2][:, 0:D]

        def conv_w(k):
            return wv("conv", rows=HD3)[:, k:k + 1]

        @block.sync
        def _(sp):
            sp.dma_start(K[:, :], consts).then_inc(consts_in, 16)
            sp.dma_start(W[:, 0:NW_A], weights[:, 0:NW_A]).then_inc(wa_in, 16)
            xt = x.rearrange("(t p) d -> t p d", p=P)
            with sp.Fori(0, TURNS) as i:
                n1 = turn(sp, i)
                for u in range(2):
                    sp.wait_ge(S["px_ps"][u], n1[0])
                    sp.dma_start(xin[u][:, :], xt[bass.ds(2 * i + u, 1)].rearrange("o p d -> (o p) d")).then_inc(x_in[u], 16)
            sp.wait_ge(S["kv_ps"][0], CREDIT + TILES)
            sp.wait_ge(S["kv_ps"][1], CREDIT + TILES)
            sp.dma_start(w1_sb[0:C + 1, :], w1).then_inc(w1_in, 16)
            sp.wait_ge(scattered, 16 * TILES)
            xst, yst = (a.rearrange("(t p) d -> t p d", p=P) for a in (xs_dram, ys_dram))
            for u in range(2):
                sp.dma_start(xn[u][:, :], xst[u]).then_inc(Z["x_in"][u], 16)
            with sp.Fori(0, SLOT_TILES // 2 - 1) as i:
                n1 = turn(sp, i)
                for u in range(2):
                    sp.wait_ge(Z["xT_ps"][u], n1[u])
                    sp.dma_start(xn[u][:, :], xst[bass.ds(2 * i + u + 2, 1)].rearrange("o p d -> (o p) d")).then_inc(Z["x_in"][u], 16)
                for u in range(2):
                    sp.wait_ge(Z["y_sb"][u], n1[u] + CREDIT)
                    sp.dma_start(yst[bass.ds(2 * i + u, 1)].rearrange("o p d -> (o p) d"), att[u][:, :]).then_inc(Z["y_out"][u], 16)
            for u in range(2):
                sp.wait_ge(Z["y_sb"][u], CREDIT + SLOT_TILES - 1 + u)
                sp.dma_start(yst[SLOT_TILES - 2 + u], att[u][:, :]).then_inc(Z["y_out"][u], 16)
            ot = out.rearrange("(t p) d -> t p d", p=P)
            for t in range(0, TILES, 4):
                sp.wait_ge(out_row, t + 4)
                sp.dma_start(ot[t:t + 4].rearrange("t p d -> p t d"), h_all[:, t:t + 4, :]).then_inc(out_done, 16)
            sp.wait_ge(out_done, 16 * (TILES // 4))

        @block.scalar
        def _(act):
            act.dma_start(W[:, NW_A:NW], weights[:, NW_A:NW]).then_inc(wb_in, 16)
            act.dma_start(bias_mask[:, :], pos_bias).then_inc(wb_in, 16)
            act.dma_start(w2_sb[:, :], w2).then_inc(moe_in, 16)
            act.dma_start(b2_sb[:, :], b2).then_inc(moe_in, 16)
            act.wait_ge(ready, 1)
            act.wait_ge(ready_p, 1)
            act.dma_start(xs_dram.rearrange("(t p) d -> p t d", p=P),
                          zeros[:, :].unsqueeze(1).broadcast_to([P, SLOT_TILES, D])).then_inc(zero_out, 16)

            with act.Fori(0, TURNS) as i:
                n1 = turn(act, i)
                for u in range(2):
                    act.wait_ge(S["xT_ps"][u], n1[u])
                    act.activation(big_a[u][0:C, 0:2 * P], bank(u, 0)[0:C, 0:2 * P], ACT.Copy).then_inc(S["xT_sb"][u], 1)
                for u in range(2):
                    act.wait_ge(S["nmx"][u], n1[u])
                    act.activation(att[u][:, 0:P], bank(u, 1)[:, 0:P], ACT.Exp, scale=D ** -0.5, bias=small[u][:, 1:2],
                                   accum_out=small[u][:, 2:3]).then_inc(S["p_sb"][u], 1)
                for u in range(2):
                    act.wait_ge(S["xnT_ps"][u], n1[u])
                    act.wait_ge(S["xstore"][u], n1[0])
                    act.activation(xnT[u][0:C, :], bank(u, 0)[0:C, 0:2 * P], ACT.Copy).then_inc(S["xnT_sb"][u], 1)
                for u in range(2):
                    act.wait_ge(S["kT_ps"][u], n1[u])
                    act.activation(qkT[u][:, :], bank(u, 2)[0:C, 0:2 * P], ACT.Copy)
                    act.activation(qksq[u][:, :], bank(u, 2)[0:C, 0:2 * P], ACT.Square).then_inc(S["k_sb"][u], 1)

            act.wait_ge(k_negmax, 1)
            for u in range(2):
                act.wait_ge(S["xstore"][u], CREDIT + TILES)
            with act.Fori(0, TURNS) as i:
                n1 = turn(act, i)
                m, l = stage_counts(act, i)
                for u in range(2):
                    act.wait_ge(S["kv_ps"][u], n1[0])
                    act.activation(k1[u][:, :], kd_all[:, bass.ds(2 * i + u, 1), :].rearrange("p o n -> p (o n)"),
                                   ACT.Exp, bias=kmax[:, 2:3]).then_inc(S["k1e"][u], 1)
                for u in range(2):
                    act.wait_ge(S["qT_ps"][u], n1[u])
                    act.activation(qkT[u][:, :], bank(u, 0)[0:C, 0:2 * P], ACT.Copy)
                    act.activation(qksq[u][:, :], bank(u, 0)[0:C, 0:2 * P], ACT.Square).then_inc(S["q_sb"][u], 1)
                for u in range(2):
                    act.wait_ge(S["qe"][u], n1[u])
                    act.activation(qe[u][:, :], qe[u][:, :], ACT.Exp).then_inc(S["qx"][u], 1)
                for u in range(2):
                    act.wait_ge(S["q1T_ps"][u], n1[u])
                    act.activation(big_a[u][0:2 * M, :].rearrange("p (b n) -> p b n", b=2), banks(u, 2, 4)[0:2 * M, :, 0:3 * P],
                                   ACT.Copy, bias=FEPS).then_inc(S["q1T_sb"][u], 1)

                def output_stage(r):
                    for u in range(2):
                        act.wait_ge(S["attT_ps"][u], m[r][u])
                        act.activation(actT[u][0:C, :], bank(u, 0)[0:C, 0:2 * P], ACT.Copy).then_inc(S["attT_sb"][u], 1)
                    for u in range(2):
                        act.wait_ge(S["xnT_ps"][u], l[r][u])
                        act.activation(xnT[u][0:C, :], bank(u, 0)[0:C, 0:2 * P], ACT.Copy).then_inc(S["xnT_sb"][u], 1)

                output_stage(0)
                for u in range(2):
                    act.wait_ge(S["g1_ps"][u], n1[u])
                    act.activation(g1T[u][0:32, :], bank(u, 1)[0:32, 0:P], ACT.Relu).then_inc(S["g1_sb"][u], 1)
                    act.wait_ge(S["fqk_ps"][u], n1[u])
                    act.activation(big_a[u][0:HD3, 0:3 * P], bank(u, 2)[0:HD3, 0:3 * P], ACT.Copy).then_inc(S["qf_sb"][u], 1)
                    act.wait_ge(S["fv_ps"][u], n1[u])
                    act.activation(vf[u][:, :].rearrange("p (e n) -> p e n", e=E3)[:, :, 0:HD3],
                                   bank(u, 3)[:, 0:D].rearrange("p (e n) -> p e n", e=E3), ACT.Copy).then_inc(S["vf_sb"][u], 1)
                for u in range(2):
                    act.wait_ge(S["gs"][u], n1[u])
                    act.activation(small[u][:, 8:11], small[u][:, 4:7], ACT.Exp, accum_out=small[u][:, 11:12]).then_inc(S["ge"][u], 1)
                for u in range(2):
                    act.wait_ge(S["gp"][u], n1[u])
                    act.activation(small[u][:, 16:19], small[u][:, 12:15], ACT.Exp).then_inc(S["gep"][u], 1)
                for u in range(2):
                    act.wait_ge(S["nf"][u], n1[u])
                    for e in range(E3):
                        last = act.activation(big_b[u][:, e * P:e * P + P], bank(u, 2)[:, e * P:e * P + P], ACT.Exp,
                                              scale=HD3 ** -0.5, bias=small[u][:, 36 + e:37 + e])
                    last.then_inc(S["fp_sb"][u], 1)
                output_stage(1)
                for u in range(2):
                    act.wait_ge(S["lqk_ps"][u], n1[u])
                    act.activation(big_a[u][:, 0:2 * D], bank(u, 1)[:, 0:2 * D], ACT.Copy).then_inc(S["lqk_sb"][u], 1)
                    act.wait_ge(S["lv_ps"][u], n1[u])
                    for par in range(2):
                        last = act.activation(v_place(u, 0, par), v_rows(u, 0, par), ACT.Copy)
                    last.then_inc(S["lv_a"][u], 1)
                for u in range(2):
                    act.wait_ge(S["lT_ps"][u], n1[u])
                    act.activation(big_b[u][:, :].rearrange("p (b n) -> p b n", b=2), banks(u, 2, 4)[:, :, 0:3 * P],
                                   ACT.Copy).then_inc(S["lT_sb"][u], 1)
                for u in range(2):
                    act.wait_ge(S["pl"][u], n1[u])
                    act.activation(big_c[u][:, :], big_c[u][:, :], ACT.Exp).then_inc(S["px"][u], 1)
                for u in range(2):
                    act.wait_ge(S["lpT_ps"][u], n1[u])
                    act.activation(big_a[u][:, :].rearrange("p (b n) -> p b n", b=2), banks(u, 0, 2)[:, :, 0:3 * P],
                                   ACT.Copy).then_inc(S["lpT_sb"][u], 1)
                output_stage(2)

            act.wait_ge(r_diff, 1)
            act.activation(big_a[0][:, P:2 * P], big_a[0][:, 0:P], ACT.Exp).then_inc(r_exp, 1)

            with act.Fori(0, SLOT_TILES // 2) as i:
                n1 = turn(act, i)
                for u in range(2):
                    act.wait_ge(Z["h_ps"][u], n1[u])
                    act.activation(big_b[u][:, :].rearrange("p (b n) -> p b n", b=2), banks(u, 1, 3)[:, :, 0:FF // 2],
                                   ACT.Silu).then_inc(Z["h_sb"][u], 1)

        @block.tensor
        def _(pe):
            pe.wait_ge(consts_in, 16)
            pe.wait_ge(wa_in, 16)
            pe.wait_ge(ready, 1)
            pe.wait_ge(ready_p, 1)

            def transposes(dst_bank, rows, src, cols, n, at=0, stride=P):
                for c in range(n):
                    last = pe.transpose(dst_bank[0:cols, at + stride * c:at + stride * c + rows], src[:, c * cols:(c + 1) * cols], ident)
                return last

            def project(dst, lhs, w, bias):
                pe.matmul(dst, lhs[0:C, 0:P], wv(w, 0), start=True, stop=False)
                k = C + 1 if bias else C
                return pe.matmul(dst, lhs[0:k, P:2 * P], wv(w, 1, k), start=False, stop=True)

            with pe.Fori(0, TURNS) as i:
                n1 = turn(pe, i)
                x_n = pe.snap(i * 16 + 16)
                for u in range(2):
                    pe.wait_ge(x_in[u], x_n)
                    transposes(bank(u, 0), P, xin[u], C, 2).then_inc(S["xT_ps"][u], 1)
                for u in range(2):
                    pe.wait_ge(S["xT_sb"][u], n1[u])
                    pe.wait_ge(S["vbd"][u], n1[0])
                    for c in range(2):
                        xT = big_a[u][0:C, c * P:c * P + P]
                        pe.matmul(bank(u, 1)[:, 0:P], xT, xT, start=c == 0, stop=False)
                    pe.matmul(bank(u, 1)[:, 0:P], bf_half[:, :], bf_split[:, :], start=False, stop=True).then_inc(S["sc_ps"][u], 1)
                for u in range(2):
                    pe.wait_ge(S["p_sb"][u], n1[u])
                    pe.transpose(bank(u, 0)[:, 2 * P:3 * P], att[u][:, 0:P], ident).then_inc(S["pT_ps"][u], 1)
                for u in range(2):
                    pe.wait_ge(S["pT_sb"][u], n1[u])
                    pe.matmul(bank(u, 1)[:, P:P + D], big_b[u][:, 0:P], xin[u][:, :], start=True, stop=True).then_inc(S["px_ps"][u], 1)
                for u in range(2):
                    pe.wait_ge(S["xnr"][u], n1[u])
                    transposes(bank(u, 0), P, xn[u], C, 2).then_inc(S["xnT_ps"][u], 1)
                for u in range(2):
                    pe.wait_ge(S["xnT_sb"][u], n1[u])
                    pe.wait_ge(S["kd"][u], n1[0])
                    for half in range(2):
                        for c in range(2):
                            last = pe.matmul(bank(u, 2)[0:C, half * P:half * P + P], wv("a_qkv", c)[:, D + half * C:D + half * C + C],
                                             xnT[u][0:C, c * P:c * P + P], start=c == 0, stop=c == 1)
                    last.then_inc(S["kT_ps"][u], 1)
                    for c in range(2):
                        last = pe.matmul(bank(u, 1)[:, 320:512], xnT[u][0:C, c * P:c * P + P], wv("a_qkv", c)[:, 2 * D:3 * D],
                                         start=c == 0, stop=c == 1)
                    last.then_inc(S["v_ps"][u], 1)
                for u in range(2):
                    pe.wait_ge(S["k_sb"][u], n1[u])
                    features(pe, u).then_inc(S["dash_ps"][u], 1)

            pe.wait_ge(wb_in, 32)
            pe.wait_ge(ready, 2)
            for u in range(2):
                pe.wait_ge(S["xstore"][u], CREDIT + TILES)
            with pe.Fori(0, TURNS) as i:
                n1 = turn(pe, i)
                m, l = stage_counts(pe, i)
                for u in range(2):
                    pe.wait_ge(S["lg"][u], n1[0])
                    for half in range(2):
                        for c in range(2):
                            last = pe.matmul(bank(u, 0)[0:C, half * P:half * P + P], wv("a_qkv", c)[:, half * C:half * C + C],
                                             x_all[0:C, bass.ds(2 * i + u, 1), c * P:c * P + P].rearrange("p o n -> p (o n)"),
                                             start=c == 0, stop=c == 1)
                    last.then_inc(S["qT_ps"][u], 1)
                for u in range(2):
                    pe.wait_ge(S["k1"][u], n1[u])
                    for c in range(HC):
                        last = pe.matmul(bank(u, 1)[0:2 * M, c * 68:c * 68 + 68], k1[u][:, c * 2 * M:(c + 1) * 2 * M],
                                         vbd_all[:, bass.ds(2 * i + u, 1), c * 68:c * 68 + 68].rearrange("p o n -> p (o n)"),
                                         start=True, stop=True)
                    last.then_inc(S["kv_ps"][u], 1)
                for u in range(2):
                    pe.wait_ge(S["q_sb"][u], n1[u])
                    features(pe, u).then_inc(S["qd_ps"][u], 1)
                for u in range(2):
                    pe.wait_ge(S["qx"][u], n1[u])
                    for b in range(2):
                        last = transposes(bank(u, 2 + b), P, qe[u][:, b * 6 * M:(b + 1) * 6 * M], 2 * M, 3)
                    last.then_inc(S["q1T_ps"][u], 1)
                for u in range(2):
                    pe.wait_ge(S["q1T_sb"][u], n1[u])
                    pe.wait_ge(S["kv_sb"][u], n1[u])
                    for c in range(HC):
                        last = pe.matmul(bank(u, 1)[:, c * 68:c * 68 + 68], big_a[u][0:2 * M, c * P:c * P + P],
                                         kvs[u][:, c * 68:c * 68 + 68], start=True, stop=True)
                    last.then_inc(S["num_ps"][u], 1)

                def output_stage(r, w):
                    for u in range(2):
                        pe.wait_ge(S["attr"][u], m[r][u])
                        transposes(bank(u, 0), P, att[u], C, 2).then_inc(S["attT_ps"][u], 1)
                    for u in range(2):
                        pe.wait_ge(S["attT_sb"][u], m[r][u])
                        project(bank(u, 0)[:, 2 * P:2 * P + D], actT[u], w, True).then_inc(S["pr_ps"][u], 1)
                    for u in range(2):
                        pe.wait_ge(S["xnr"][u], l[r][u])
                        transposes(bank(u, 0), P, xn[u], C, 2).then_inc(S["xnT_ps"][u], 1)

                output_stage(0, "a_out")
                for u in range(2):
                    pe.wait_ge(S["xnT_sb"][u], l[0][u])
                    for c in range(2):
                        k = C + c
                        last = pe.matmul(bank(u, 1)[0:32, 0:P], wv("f_g1", c, k), xnT[u][0:k, c * P:c * P + P], start=c == 0, stop=c == 1)
                    last.then_inc(S["g1_ps"][u], 1)
                    for e in range(E3):
                        for c in range(2):
                            k = C + c
                            last = pe.matmul(bank(u, 2)[:, e * P:e * P + P], wv("f_qk", c, k)[:, e * P:e * P + P],
                                             xnT[u][0:k, c * P:c * P + P], start=c == 0, stop=c == 1)
                    last.then_inc(S["fqk_ps"][u], 1)
                    project(bank(u, 3)[:, 0:D], xnT[u], "f_v", True).then_inc(S["fv_ps"][u], 1)
                for u in range(2):
                    pe.wait_ge(S["g1_sb"][u], n1[u])
                    pe.matmul(bank(u, 1)[:, P:P + E3], g1T[u][:, :], wv("f_g2", rows=33), start=True, stop=True).then_inc(S["gl_ps"][u], 1)
                for u in range(2):
                    pe.wait_ge(S["qf_sb"][u], n1[u])
                    pe.wait_ge(S["kf_sb"][u], n1[u])
                    for e in (1, 2, 0):
                        if e == 0:
                            pe.wait_ge(S["conv"][u], n1[u])
                        q = qc[u][:, :] if e == 0 else big_a[u][0:HD3, e * P:e * P + P]
                        dst = bank(u, 2)[:, e * P:e * P + P]
                        pe.matmul(dst, q, big_a[u][0:HD3, (3 + e) * P:(4 + e) * P], start=True, stop=False)
                        if e == 2:
                            last = pe.matmul(dst, ident, bias_mask[:, :], start=False, stop=True)
                        else:
                            last = pe.matmul(dst, bf_ident[:, :], bf_causal[:, :], start=False, stop=True)
                    last.then_inc(S["fs_ps"][u], 1)
                for u in range(2):
                    pe.wait_ge(S["fp_sb"][u], n1[u])
                    pe.wait_ge(S["vf_sb"][u], n1[u])
                    transposes(bank(u, 3), P, big_b[u], P, 3).then_inc(S["fpT_ps"][u], 1)
                for u in range(2):
                    pe.wait_ge(S["fpT_sb"][u], n1[u])
                    for e in range(E3):
                        last = pe.matmul(bank(u, 1)[:, 160 + 65 * e:225 + 65 * e], big_c[u][:, e * P:e * P + P], vf[u][:, 65 * e:65 * e + 65],
                                         start=True, stop=True)
                    last.then_inc(S["fo_ps"][u], 1)
                output_stage(1, "f_out")
                for u in range(2):
                    pe.wait_ge(S["xnT_sb"][u], l[1][u])
                    for c in range(2):
                        k = C + c
                        last = pe.matmul(bank(u, 1)[:, 0:2 * D], xnT[u][0:k, c * P:c * P + P], wv("l_qkv", c, k)[:, 0:2 * D], start=c == 0, stop=c == 1)
                    last.then_inc(S["lqk_ps"][u], 1)
                    for c in range(2):
                        k = C + c
                        last = pe.matmul(bank(u, 2)[:, 0:D], xnT[u][0:k, c * P:c * P + P], wv("l_qkv", c, k)[:, 2 * D:3 * D], start=c == 0, stop=c == 1)
                    last.then_inc(S["lv_ps"][u], 1)
                for u in range(2):
                    pe.wait_ge(S["rope"][u], n1[u])
                    pe.wait_ge(S["lv_a"][u], n1[u])
                    pe.wait_ge(S["lv_d"][u], n1[u])
                    for s in range(2):
                        last = transposes(bank(u, 2 + s), P, pad[u][:, s * 3 * P:(s + 1) * 3 * P], P, 3)
                    last.then_inc(S["lT_ps"][u], 1)
                for u in range(2):
                    pe.wait_ge(S["lT_sb"][u], n1[u])
                    for g in range(3):
                        for b in range(2):
                            for j in range(4):
                                q = big_b[u][32 * j:32 * j + 32, g * P + b * T:g * P + b * T + T]
                                k = big_b[u][32 * j:32 * j + 32, (3 + g) * P + b * T:(3 + g) * P + b * T + T]
                                last = pe.matmul(bank(u, j)[b * T:b * T + T, g * T:g * T + T], q, k, start=True, stop=True)
                    last.then_inc(S["ls_ps"][u], 1)
                for u in range(2):
                    pe.wait_ge(S["px"][u], n1[u])
                    for b in range(2):
                        last = transposes(bank(u, b), P, big_c[u][:, b * 3 * P:(b + 1) * 3 * P], P, 3)
                    last.then_inc(S["lpT_ps"][u], 1)
                for u in range(2):
                    pe.wait_ge(S["lpT_sb"][u], n1[u])
                    for c in range(HC):
                        for b in range(2):
                            last = pe.matmul(bank(u, 2)[b * T:b * T + T, c * 34:c * 34 + 34], big_a[u][:, c * P + b * T:c * P + b * T + T],
                                             vl[u][:, (b * HC + c) * 34:(b * HC + c) * 34 + 34], start=True, stop=True)
                    last.then_inc(S["lo_ps"][u], 1)
                output_stage(2, "l_out")
                for u in range(2):
                    pe.wait_ge(S["xnT_sb"][u], l[2][u])
                    project(bank(u, 0)[:, 448:448 + EX], xnT[u], "m_g", False).then_inc(S["lg_ps"][u], 1)

            pe.wait_ge(r_onehot, 1)
            pe.matmul(bank(0, 0)[:, 0:P], kc("triu"), big_a[0][:, 4 * P:5 * P], start=True, stop=True)
            pe.matmul(bank(0, 1)[:, 0:P], ones_sq[:, :], big_a[0][:, 4 * P:5 * P], start=True, stop=True).then_inc(r_count, 1)

            pe.wait_ge(r_slots, 2)
            pe.wait_ge(w1_in, 16)
            pe.wait_ge(moe_in, 32)
            with pe.Fori(0, SLOT_TILES // 2) as i:
                n1 = turn(pe, i)
                x_n = pe.snap(i * 16 + 16)
                expert = [pe.value_load(tile_ex[0:1, bass.ds(2 * i + u, 1)], min_val=0, max_val=EX - 1) for u in range(2)]
                for u in range(2):
                    pe.wait_ge(Z["x_in"][u], x_n)
                    transposes(bank(u, 0), P, xn[u], C, 2).then_inc(Z["xT_ps"][u], 1)
                for u in range(2):
                    pe.wait_ge(Z["xT_sb"][u], n1[u])
                    for f in range(2):
                        for c in range(2):
                            k = C + c
                            last = pe.matmul(bank(u, 1 + f)[:, 0:FF // 2], xnT[u][0:k, c * P:c * P + P],
                                             w1_sb[0:k, bass.ds(expert[u] * (2 * FF) + (c * FF + f * (FF // 2)), FF // 2)], start=c == 0, stop=c == 1)
                    last.then_inc(Z["h_ps"][u], 1)
                for u in range(2):
                    pe.wait_ge(Z["h_sb"][u], n1[u])
                    for b in range(2):
                        last = transposes(bank(u, 1 + b), P, big_b[u][:, b * 3 * P:(b + 1) * 3 * P], P, 3)
                    last.then_inc(Z["hT_ps"][u], 1)
                for u in range(2):
                    pe.wait_ge(Z["hT_sb"][u], n1[u])
                    pe.wait_ge(Z["y_sb"][u], n1[0])
                    pe.matmul(bank(u, 3)[:, 0:D], ones_row[:, :], b2_sb[0:1, bass.ds(expert[u] * D, D)], start=True, stop=False)
                    for f in range(FT):
                        last = pe.matmul(bank(u, 3)[:, 0:D], big_c[u][:, f * P:f * P + P], w2_sb[:, bass.ds(expert[u] * (FT * D) + f * D, D)],
                                         start=False, stop=f == FT - 1)
                    last.then_inc(Z["y_ps"][u], 1)

        @block.vector
        def _(dve):
            count = [0]
            base = [0]

            def mark(ins):
                count[0] += 1
                ins.then_inc(vstep, 1)
                return count[0]

            def after(step):
                dve.wait_ge(vstep, base[0] + step)

            def loop_base(eng_i, before, per_turn):
                base[0] = dve.snap(eng_i * per_turn + before)
                count[0] = 0

            give_credit(dve, [S[n][0] for n in ("vbd", "kd", "hstore", "xstore", "store", "lg", "px_ps", "kv_ps")])
            give_credit(dve, [Z["y_sb"][0], *Z["y_out"]])
            dve.memset(ones_row[:, :], 1.0)
            dve.memset(ones_sq[:, :], 1.0)
            for u in range(2):
                dve.memset(actT[u][C:C + 1, :], 1.0)
                dve.memset(xnT[u][C:C + 1, :], 1.0)
                dve.memset(g1T[u][32:33, :], 1.0)
                dve.memset(vf[u][:, :], 1.0)
            dve.wait_ge(consts_in, 16)
            dve.tensor_copy(bf_ident[:, :], ident)
            dve.tensor_copy(bf_causal[:, :], kc("causal"))
            dve.tensor_copy(bf_half[:, :], kc("half", 2))
            dve.tensor_copy(bf_split[:, :], kc("split", 2))
            dve.wait_ge(wa_in, 16)
            dve.tensor_tensor(feat[:, :], wv("feat"), kc("block", C), ALU.mult).then_inc(ready, 1)

            def layernorm(value):
                st = []
                for u in range(2):
                    st.append(mark(dve.bn_stats(stats[u][:, 0:6], hs[u][:, :])))
                after(st[1])
                mark(dve.memset(stats[0][:, 15:16], 0.0))
                for u in range(2):
                    dve.bn_aggr(stats[u][:, 8:10], stats[u][:, 0:6]).then_inc(S["mv"][u], 1)
                for u in range(2):
                    dve.wait_ge(S["rstd"][u], value[u])
                    dve.tensor_scalar(xn[u][:, :], hs[u][:, :], stats[u][:, 8:9], stats[u][:, 10:11], ALU.subtract, ALU.mult).then_inc(S["xnr"][u], 1)

            def minus_norms(u, dst, shift):
                return dve.tensor_tensor(dst.rearrange("p (b h n) -> p b h n", b=2, h=HC), dash(u),
                                         shift.rearrange("p (b h) -> p b h", b=2).unsqueeze(3).broadcast_to([P, 2, HC, M]), ALU.subtract)

            def dash(u):
                return banks(u, 2, 4)[:, :, 0:HC * M].rearrange("p b (h n) -> p b h n", h=HC)

            STEPS_A = 11
            with dve.Fori(0, TURNS) as i:
                n1 = turn(dve, i)
                loop_base(i, 0, STEPS_A)
                for u in range(2):
                    dve.wait_ge(S["sc_ps"][u], n1[u])
                    a = mark(dve.reduce_max(small[u][:, 0:1], bank(u, 1)[:, 0:P], AX))
                    after(a)
                    dve.tensor_scalar(small[u][:, 1:2], small[u][:, 0:1], -D ** -0.5, None, ALU.mult).then_inc(S["nmx"][u], 1)
                for u in range(2):
                    dve.wait_ge(S["pT_ps"][u], n1[u])
                    dve.tensor_copy(big_b[u][:, 0:P], bank(u, 0)[:, 2 * P:3 * P]).then_inc(S["pT_sb"][u], 1)
                r = []
                for u in range(2):
                    dve.wait_ge(S["p_sb"][u], n1[u])
                    r.append(mark(dve.reciprocal(small[u][:, 3:4], small[u][:, 2:3])))
                for u in range(2):
                    dve.wait_ge(S["px_ps"][u], n1[u] + CREDIT)
                    dve.wait_ge(S["hstore"][u], n1[0])
                    after(r[u])
                    dve.tensor_scalar(hs[u][:, :], bank(u, 1)[:, P:P + D], small[u][:, 3:4], None, ALU.mult).then_inc(S["hrow"][u], 1)
                for u in range(2):
                    dve.wait_ge(S["hrow"][u], n1[u])
                layernorm(n1)
                for u in range(2):
                    dve.wait_ge(S["v_ps"][u], n1[u])
                    for b in range(2):
                        dst = vbd_all[T * b:T * b + T, bass.ds(2 * i + u, 1), :].rearrange("p o (c b r d) -> p (o c) b r d", c=HC, b=2, r=2)
                        last = dve.tensor_copy(dst[:, :, b, :, 0:HD], bank(u, 1)[T * b:T * b + T, 320:512].rearrange("p (c r d) -> p c r d", c=HC, r=2))
                    last.then_inc(S["vbd"][u], 1)
                for u in range(2):
                    dve.wait_ge(S["dash_ps"][u], n1[u])
                    a = mark(dve.tensor_copy(small[u][:, 20:32], bank(u, 3)[:, 264:264 + H]))
                    b = mark(dve.tensor_reduce(kmx_all[:, bass.ds(2 * i + u, 1)], banks(u, 2, 4)[:, :, 0:HC * M], mybir.AxisListType.XY, ALU.max))
                    after(a)
                    minus_norms(u, kd_all[:, bass.ds(2 * i + u, 1), :].rearrange("p o n -> p (o n)"), small[u][:, 20:32]).then_inc(S["kd"][u], 1)
                assert count[0] == STEPS_A, count
            before = TURNS * STEPS_A
            base[0] = 0
            dve.wait_ge(vstep, before)
            dve.reduce_max(kmax[:, 0:1], kmx_all[:, :], AX).then_inc(k_max, 1)
            dve.wait_ge(k_maxall, 1)
            dve.tensor_scalar(kmax[:, 2:3], kmax[:, 1:2], -1.0, None, ALU.mult).then_inc(k_negmax, 1)
            dve.wait_ge(wb_in, 32)
            dve.scalar_tensor_tensor(out=bias_mask[:, :], in0=bias_mask[:, :], scalar=HD3 ** 0.5, in1=kc("causal"),
                                     op0=ALU.mult, op1=ALU.add).then_inc(ready, 1)

            for u in range(2):
                dve.wait_ge(S["hstore"][u], CREDIT + TILES)
            STEPS_B = 47
            with dve.Fori(0, TURNS) as i:
                n1 = turn(dve, i)
                m, l = stage_counts(dve, i)
                loop_base(i, before, STEPS_B)
                for u in range(2):
                    dve.wait_ge(S["kv_ps"][u], n1[u] + CREDIT)
                    dve.tensor_tensor(kvs[u][:, :].rearrange("p (c n) -> p c n", c=HC), bank(u, 1)[0:2 * M, 0:408].rearrange("p (c n) -> p c n", c=HC),
                                      kc("kvmask", 2 * M).unsqueeze(1).broadcast_to([2 * M, HC, 68]), ALU.mult).then_inc(S["kv_sb"][u], 1)
                for u in range(2):
                    dve.wait_ge(S["qd_ps"][u], n1[u])
                    a = mark(dve.tensor_reduce(small[u][:, 20:32].rearrange("p (b h) -> p b h", b=2), dash(u), AX, ALU.max))
                    after(a)
                    a = mark(dve.tensor_tensor(small[u][:, 32:44], small[u][:, 20:32], bank(u, 3)[:, 264:264 + H], ALU.add))
                    after(a)
                    minus_norms(u, qe[u][:, :], small[u][:, 32:44]).then_inc(S["qe"][u], 1)
                for u in range(2):
                    dve.wait_ge(S["num_ps"][u], n1[u])
                    num = bank(u, 1)[:, 0:408].rearrange("p (c b r d) -> p c b r d", c=HC, b=2, r=2)
                    z = small[u][:, 20:44].rearrange("p (c b r) -> p c b r", c=HC, b=2)
                    a = mark(dve.reciprocal(z, num[:, :, :, :, 16]))
                    after(a)
                    for b in range(2):
                        rows = slice(T * b, T * b + T)
                        last = dve.tensor_tensor(att[u][rows, :].rearrange("p (c r d) -> p c r d", c=HC, r=2), num[rows, :, b, :, 0:HD],
                                                 z[rows, :, b, :].unsqueeze(3).broadcast_to([T, HC, 2, HD]), ALU.mult)
                    last.then_inc(S["attr"][u], 1)

                def output_stage(r):
                    for u in range(2):
                        dve.wait_ge(S["pr_ps"][u], m[r][u])
                        if r == 0:
                            dve.wait_ge(S["store"][u], n1[0])
                            old = h_all[:, bass.ds(2 * i + u, 1), :].rearrange("p o d -> p (o d)")
                        else:
                            old = hs[u][:, :]
                        dve.tensor_tensor(hs[u][:, :], bank(u, 0)[:, 2 * P:2 * P + D], old, ALU.add).then_inc(S["hrow"][u], 1)
                    for u in range(2):
                        dve.wait_ge(S["hrow"][u], l[r][u])
                    layernorm(l[r])

                output_stage(0)
                for u in range(2):
                    dve.wait_ge(S["fqk_ps"][u], n1[u])
                    dve.tensor_copy(big_a[u][0:HD3, 3 * P:6 * P], bank(u, 2)[HD3:P, 0:3 * P]).then_inc(S["kf_sb"][u], 1)
                st = {}
                for u in range(2):
                    dve.wait_ge(S["qf_sb"][u], n1[u])
                    q = big_a[u][0:HD3, 0:P]
                    q2, y2 = (a.rearrange("p (b t) -> p b t", b=2) for a in (q, qc[u][:, :]))
                    after(mark(dve.tensor_scalar(qc[u][:, :], q, conv_w(1), conv_w(3), ALU.mult, ALU.add)))
                    after(mark(dve.scalar_tensor_tensor(out=y2[:, :, 1:T], in0=q2[:, :, 0:T - 1], scalar=conv_w(0), in1=y2[:, :, 1:T],
                                                        op0=ALU.mult, op1=ALU.add)))
                    dve.scalar_tensor_tensor(out=y2[:, :, 0:T - 1], in0=q2[:, :, 1:T], scalar=conv_w(2), in1=y2[:, :, 0:T - 1],
                                             op0=ALU.mult, op1=ALU.add).then_inc(S["conv"][u], 1)
                for u in range(2):
                    dve.wait_ge(S["gl_ps"][u], n1[u])
                    st[u] = mark(dve.reduce_max(small[u][:, 7:8], bank(u, 1)[:, P:P + E3], AX))
                for u in range(2):
                    after(st[u])
                    dve.tensor_scalar(small[u][:, 4:7], bank(u, 1)[:, P:P + E3], small[u][:, 7:8], None, ALU.subtract).then_inc(S["gs"][u], 1)
                for u in range(2):
                    dve.wait_ge(S["fs_ps"][u], n1[u])
                    st[u] = mark(dve.tensor_reduce(small[u][:, 33:36], bank(u, 2)[:, 0:3 * P].rearrange("p (e n) -> p e n", e=E3), AX, ALU.max))
                for u in range(2):
                    after(st[u])
                    dve.tensor_scalar(small[u][:, 36:39], small[u][:, 33:36], -HD3 ** -0.5, None, ALU.mult).then_inc(S["nf"][u], 1)
                for u in range(2):
                    dve.wait_ge(S["ge"][u], n1[u])
                    st[u] = mark(dve.reciprocal(small[u][:, 15:16], small[u][:, 11:12]))
                for u in range(2):
                    after(st[u])
                    dve.tensor_scalar(small[u][:, 12:15], small[u][:, 8:11], small[u][:, 15:16], None, ALU.mult).then_inc(S["gp"][u], 1)
                for u in range(2):
                    dve.wait_ge(S["gp"][u], n1[u])
                    st[u] = mark(dve.tensor_reduce(small[u][:, 40:41], small[u][:, 12:15], AX, ALU.min))
                for u in range(2):
                    after(st[u])
                    st[u] = mark(dve.scalar_tensor_tensor(out=small[u][:, 41:44], in0=small[u][:, 12:15], scalar=small[u][:, 40:41], in1=kc("eidx"),
                                                          op0=ALU.is_equal, op1=ALU.mult))
                for u in range(2):
                    after(st[u])
                    st[u] = mark(dve.reduce_max(small[u][:, 44:45], small[u][:, 41:44], AX))
                for u in range(2):
                    after(st[u])
                    dve.wait_ge(S["gep"][u], n1[u])
                    st[u] = mark(dve.scalar_tensor_tensor(out=small[u][:, 46:49], in0=small[u][:, 41:44], scalar=small[u][:, 44:45],
                                                          in1=small[u][:, 16:19], op0=ALU.not_equal, op1=ALU.mult))
                for u in range(2):
                    after(st[u])
                    st[u] = mark(dve.reduce_sum(small[u][:, 49:50], small[u][:, 46:49], AX))
                for u in range(2):
                    after(st[u])
                    st[u] = mark(dve.reciprocal(small[u][:, 50:51], small[u][:, 49:50]))
                for u in range(2):
                    after(st[u])
                    st[u] = mark(dve.tensor_scalar(small[u][:, 51:54], small[u][:, 46:49], small[u][:, 50:51], None, ALU.mult))
                weight_step = dict(st)
                for u in range(2):
                    dve.wait_ge(S["fpT_ps"][u], n1[u])
                    dve.tensor_copy(big_c[u][:, 0:3 * P], bank(u, 3)[:, 0:3 * P]).then_inc(S["fpT_sb"][u], 1)
                for u in range(2):
                    dve.wait_ge(S["fo_ps"][u], n1[u])
                    fo = bank(u, 1)[:, 160:355].rearrange("p (e n) -> p e n", e=E3)
                    a = mark(dve.reciprocal(small[u][:, 54:57], fo[:, :, HD3]))
                    after(a)
                    a = mark(dve.tensor_tensor(small[u][:, 57:60], small[u][:, 54:57], small[u][:, 51:54], ALU.mult))
                    after(a)
                    dve.tensor_tensor(att[u][:, :].rearrange("p (e n) -> p e n", e=E3), fo[:, :, 0:HD3],
                                      small[u][:, 57:60].unsqueeze(2).broadcast_to([P, E3, HD3]), ALU.mult).then_inc(S["attr"][u], 1)
                output_stage(1)
                for u in range(2):
                    dve.wait_ge(S["lv_ps"][u], n1[u])
                    for par in range(2):
                        last = dve.tensor_copy(v_place(u, 1, par), v_rows(u, 1, par))
                    last.then_inc(S["lv_d"][u], 1)
                for u in range(2):
                    dve.wait_ge(S["ls_ps"][u], n1[u])
                    sc = banks(u, 0, 4)[:, :, 0:3 * T].rearrange("p j (g n) -> p j g n", g=3)
                    mx = small[u][:, 20:32].rearrange("p (j g) -> p j g", j=4)
                    a = mark(dve.tensor_reduce(mx, sc, AX, ALU.max))
                    after(a)
                    dve.tensor_tensor(big_c[u][:, :].rearrange("p (j g n) -> p j g n", j=4, g=3), sc,
                                      mx.unsqueeze(3).broadcast_to([P, 4, 3, T]), ALU.subtract).then_inc(S["pl"][u], 1)
                for u in range(2):
                    dve.wait_ge(S["lo_ps"][u], n1[u])
                    lo = bank(u, 2)[:, 0:204].rearrange("p (h d) -> p h d", h=H)
                    a = mark(dve.reciprocal(small[u][:, 20:32], lo[:, :, HD]))
                    after(a)
                    dve.tensor_tensor(att[u][:, :].rearrange("p (h d) -> p h d", h=H), lo[:, :, 0:HD],
                                      small[u][:, 20:32].unsqueeze(2).broadcast_to([P, H, HD]), ALU.mult).then_inc(S["attr"][u], 1)
                output_stage(2)
                for u in range(2):
                    dve.wait_ge(S["lg_ps"][u], n1[u])
                    dve.tensor_copy(lg_all[:, bass.ds(2 * i + u, 1), :].rearrange("p o n -> p (o n)"), bank(u, 0)[:, 448:448 + EX]).then_inc(S["lg"][u], 1)
                assert count[0] == STEPS_B, count

            base[0] = before + TURNS * STEPS_B
            count[0] = 0

            def step(ins):
                after(mark(ins))

            def te(t, k):
                return t[:, k * P:(k + 1) * P].rearrange("p (t e) -> p t e", t=TILES)

            def over_e(v):
                return v.unsqueeze(2).broadcast_to([P, TILES, EX])

            def over_t(v):
                return v.unsqueeze(1).broadcast_to([P, TILES, EX])

            for u in range(2):
                dve.wait_ge(S["lg"][u], CREDIT + TILES)
            s16 = [rsm[:, 16 * k:16 * k + 16] for k in range(4)]
            step(dve.tensor_reduce(s16[0], lg_all[:, :, :], AX, ALU.max))
            dve.tensor_tensor(te(big_a[0], 0), lg_all[:, :, :], over_e(s16[0]), ALU.subtract).then_inc(r_diff, 1)
            dve.wait_ge(r_exp, 1)
            step(dve.tensor_reduce(s16[1], te(big_a[0], 1), AX, ALU.add))
            step(dve.reciprocal(gate[:, :], s16[1]))
            step(dve.tensor_reduce(s16[2], te(big_a[0], 1), AX, ALU.max))
            step(dve.tensor_tensor(te(big_a[0], 2), te(big_a[0], 1), over_e(s16[2]), ALU.is_equal))
            step(dve.tensor_tensor(te(big_a[0], 3), te(big_a[0], 2), over_t(kc("eord")), ALU.mult))
            step(dve.tensor_reduce(s16[3], te(big_a[0], 3), AX, ALU.max))
            dve.tensor_tensor(te(big_a[0], 4), te(big_a[0], 3), over_e(s16[3]), ALU.is_equal).then_inc(r_onehot, 1)
            dve.wait_ge(r_count, 1)
            step(dve.tensor_copy(big_b[0][:, 0:P], bank(0, 1)[:, 0:P]))
            src, k = te(big_b[0], 0), 0
            for sh in (1, 2, 4, 8):
                dst = te(big_b[0], k + 1)
                mark(dve.tensor_copy(dst[:, 0:sh, :], src[:, 0:sh, :]))
                step(dve.tensor_tensor(dst[:, sh:, :], src[:, sh:, :], src[:, :TILES - sh, :], ALU.add))
                src, k = dst, k + 1
            step(dve.tensor_tensor(te(big_b[0], 5), src, te(big_b[0], 0), ALU.subtract))
            filled = te(big_c[0], 0).rearrange("p t e -> p (t e)").rearrange("p (e t) -> p e t", e=EX)
            step(dve.tensor_tensor(filled, src[:, TILES - 1, :].unsqueeze(2).broadcast_to([P, EX, TILES]),
                                   kc("thr").unsqueeze(1).broadcast_to([P, EX, TILES]), ALU.is_gt))
            e8 = [rsm[:, 64 + 8 * k:72 + 8 * k] for k in range(8)]
            step(dve.tensor_reduce(e8[0], filled, AX, ALU.add))
            src = e8[0]
            for k, sh in enumerate((1, 2, 4)):
                mark(dve.tensor_copy(e8[k + 1][:, 0:sh], src[:, 0:sh]))
                step(dve.tensor_tensor(e8[k + 1][:, sh:], src[:, sh:], src[:, :EX - sh], ALU.add))
                src = e8[k + 1]
            step(dve.tensor_tensor(e8[4], src, e8[0], ALU.subtract))
            step(dve.tensor_scalar(e8[5], e8[4], float(P), None, ALU.mult))
            step(dve.tensor_tensor(te(big_c[0], 1), te(big_b[0], 5), bank(0, 0)[:, 0:P].rearrange("p (t e) -> p t e", t=TILES), ALU.add))
            step(dve.tensor_tensor(te(big_c[0], 2), te(big_c[0], 1), over_t(e8[5]), ALU.add))
            step(dve.tensor_tensor(te(big_c[0], 3), te(big_c[0], 2), te(big_a[0], 4), ALU.mult))
            step(dve.tensor_reduce(s16[0], te(big_c[0], 3), AX, ALU.add))
            dve.tensor_copy(slots[:, :], s16[0]).then_inc(r_slots, 1)
            past = big_b[1][:, 0:SLOT_TILES * EX].rearrange("p (s e) -> p s e", e=EX)
            step(dve.tensor_tensor(past, src.unsqueeze(1).broadcast_to([P, SLOT_TILES, EX]),
                                   kc("slot").unsqueeze(2).broadcast_to([P, SLOT_TILES, EX]), ALU.is_le))
            step(dve.tensor_reduce(rsm[:, 128:128 + SLOT_TILES], past, AX, ALU.add))
            step(dve.tensor_scalar(rsm[:, 160:160 + SLOT_TILES], rsm[:, 128:128 + SLOT_TILES], float(EX - 1), None, ALU.min))
            dve.tensor_copy(tile_ex[:, :], rsm[:, 160:160 + SLOT_TILES]).then_inc(r_slots, 1)

            with dve.Fori(0, SLOT_TILES // 2) as i:
                n1 = turn(dve, i)
                for u in range(2):
                    dve.wait_ge(Z["xT_ps"][u], n1[u])
                    dve.tensor_copy(xnT[u][0:C, :], bank(u, 0)[0:C, 0:2 * P]).then_inc(Z["xT_sb"][u], 1)
                for u in range(2):
                    dve.wait_ge(Z["hT_ps"][u], n1[u])
                    dve.tensor_copy(big_c[u][:, :].rearrange("p (b n) -> p b n", b=2), banks(u, 1, 3)[:, :, 0:3 * P]).then_inc(Z["hT_sb"][u], 1)
                for u in range(2):
                    dve.wait_ge(Z["y_ps"][u], n1[u])
                    dve.wait_ge(Z["y_out"][u], i * 16 + CREDIT)
                    dve.tensor_copy(att[u][:, :], bank(u, 3)[:, 0:D]).then_inc(Z["y_sb"][u], 1)

            for t in range(TILES):
                dve.wait_ge(gathered[t % 4], 16 * (t // 4 + 1))
                dve.scalar_tensor_tensor(out=h_all[:, t, :], in0=y_rows(t), scalar=gate[:, t:t + 1], in1=h_all[:, t, :],
                                         op0=ALU.mult, op1=ALU.add).then_inc(out_row, 1)

        @block.gpsimd
        def _(pool):
            pool.wait_ge(consts_in, 16)
            pool.memset(vbd_all, 0.0).then_inc(pstep, 1)
            for u in range(2):
                pool.memset(pad[u][:, :], 0.0).then_inc(pstep, 1)
                pool.memset(vl[u][:, :], 0.0).then_inc(pstep, 1)
            pool.wait_ge(pstep, 5)
            for b in range(2):
                v = vbd_all[T * b:T * b + T].rearrange("p t (c b r d) -> p (t c) b r d", c=HC, b=2, r=2)
                for par in range(2):
                    pool.memset(v[:, :, b, par, HD:HD + 1], 1.0)
            for u in range(2):
                for par in range(2):
                    v = vl[u][T * par:T * par + T, :].rearrange("p (c r d) -> p c r d", c=2 * HC, r=2)
                    last = pool.memset(v[:, :, par, HD:HD + 1], 1.0)
            last.then_inc(ready_p, 1)

            def rstd(u, value):
                pool.wait_ge(S["mv"][u], value[u])
                pool.tensor_tensor(stats[u][:, 11:12], stats[u][:, 9:10], kc("eps")[:, 0:1], ALU.add).then_inc(S["var_eps"][u], 1)
                pool.wait_ge(S["var_eps"][u], value[u])
                pool.tensor_tensor(stats[u][:, 10:11], stats[u][:, 11:12], kc("eps")[:, 1:2], ALU.pow).then_inc(S["rstd"][u], 1)

            with pool.Fori(0, TURNS) as i:
                n1 = turn(pool, i)
                for u in range(2):
                    rstd(u, n1)
                for u in range(2):
                    pool.wait_ge(S["hrow"][u], n1[u])
                    pool.tensor_copy(h_all[:, bass.ds(2 * i + u, 1), :].rearrange("p o d -> p (o d)"), hs[u][:, :]).then_inc(S["hstore"][u], 1)
                for u in range(2):
                    pool.wait_ge(S["xnT_sb"][u], n1[u])
                    pool.tensor_copy(x_all[0:C, bass.ds(2 * i + u, 1), :].rearrange("p o d -> p (o d)"), xnT[u][0:C, :]).then_inc(S["xstore"][u], 1)
            pool.wait_ge(k_max, 1)
            pool.partition_all_reduce(kmax[:, 1:2], kmax[:, 0:1], P, bass.bass_isa.ReduceOp.max).then_inc(k_maxall, 1)
            pool.wait_ge(zero_out, 16)
            before = 5

            ROPE_STEPS = 2
            with pool.Fori(0, TURNS) as i:
                n1 = turn(pool, i)
                m, l = stage_counts(pool, i)
                rbase = pool.snap(i * ROPE_STEPS + before)
                for u in range(2):
                    pool.wait_ge(S["k1e"][u], n1[u])
                    pool.tensor_tensor(k1[u][:, :], k1[u][:, :], kc("eps")[:, 2:3].broadcast_to([P, H * M]), ALU.add).then_inc(S["k1"][u], 1)
                for u in range(2):
                    rstd(u, l[0])
                for u in range(2):
                    rstd(u, l[1])
                for u in range(2):
                    pool.wait_ge(S["lqk_sb"][u], n1[u])
                    src = big_a[u][:, 0:2 * D].rearrange("p (h r d) -> p h r d", r=2, d=8)
                    sin = kc("sin").rearrange("p (h r d) -> p h r d", r=2, d=8)
                    sw = big_b[u][:, 0:2 * D].rearrange("p (h r d) -> p h r d", r=2, d=8)
                    for r in range(2):
                        pool.tensor_tensor(sw[:, :, r, :], src[:, :, 1 - r, :], sin[:, :, r, :], ALU.mult)
                    pool.tensor_tensor(big_b[u][:, 2 * D:4 * D], big_a[u][:, 0:2 * D], kc("cos"), ALU.mult).then_inc(pstep, 1)
                    pool.wait_ge(pstep, rbase + (1 + u))
                    for s in range(2):
                        dst = pad[u][:, s * 3 * P:(s + 1) * 3 * P].rearrange("p (g j n) -> p g j n", g=3, j=4)[:, :, :, 0:HD]
                        a, b = (big_b[u][:, o + s * D:o + (s + 1) * D].rearrange("p (j g d) -> p g j d", j=4, g=3) for o in (0, 2 * D))
                        last = pool.tensor_tensor(dst, a, b, ALU.add)
                    last.then_inc(S["rope"][u], 1)
                for u in range(2):
                    rstd(u, l[2])
                for u in range(2):
                    pool.wait_ge(S["xnr"][u], l[2][u])
                    pool.tensor_copy(h_all[:, bass.ds(2 * i + u, 1), :].rearrange("p o d -> p (o d)"), hs[u][:, :])
                    pool.tensor_copy(x_all[:, bass.ds(2 * i + u, 1), 0:D].rearrange("p o d -> p (o d)"), xn[u][:, :]).then_inc(S["store"][u], 1)

            pool.wait_ge(zero_out, 16)
            pool.wait_ge(r_slots, 1)
            pool.wait_ge(S["store"][1], CREDIT + TILES)
            for t in range(TILES):
                pool.indirect_dma_start(out=xs_dram, out_offset=bass.IndirectOffsetOnAxis(ap=slots[:, t:t + 1], axis=0),
                                        in_=x_all[:, t, 0:D], in_offset=None).then_inc(scattered, 16)
            for u in range(2):
                pool.wait_ge(Z["y_out"][u], CREDIT + 16 * (SLOT_TILES // 2))
            for t in range(TILES):
                if t >= 4:
                    pool.wait_ge(out_row, t - 3)
                pool.indirect_dma_start(out=y_rows(t), out_offset=None, in_=ys_dram,
                                        in_offset=bass.IndirectOffsetOnAxis(ap=slots[:, t:t + 1], axis=0)).then_inc(gathered[t % 4], 16)



def chunks(w, bias=None):
    n = w.shape[1]
    o = np.zeros((C + 1, 2, n), np.float32)
    o[:C, 0], o[:C, 1] = w[:C], w[C:]
    if bias is not None:
        o[C, 1] = bias
    return o.reshape(C + 1, 2 * n)


def kernel(**inputs):
    import concourse.bacc as bacc
    from concourse.bass_utils import run_bass_kernel_spmd

    a = {k: np.asarray(v) for k, v in inputs.items()}
    x = np.zeros((SEQS, T, D), np.float32)
    x[:, :(SEQ_IN + 1) // 2] = a["x"][:, ::2]

    wts = np.zeros((C + 1, NW), np.float32)

    def put(name, value):
        lo, hi = _W[name]
        wts[:value.shape[0], lo:hi] = value

    def by_expert(v):
        return v.reshape(v.shape[:-1] + (2, E3, HD3)).swapaxes(-3, -2).reshape(v.shape)

    put("a_qkv", chunks(a["L0_attn_W_qkv"]))
    put("feat", np.tile(a["L0_attn_proj_mat"].T, (HC, HC)))
    put("a_out", chunks(a["L0_attn_W_proj"], a["L0_attn_b_proj"]))
    put("f_qk", chunks(by_expert(a["L0_ffn_Wqk"]), by_expert(a["L0_ffn_bqk"])))
    put("f_v", chunks(a["L0_ffn_Wv"].transpose(1, 0, 2).reshape(D, D), a["L0_ffn_bv"].reshape(-1)))
    put("f_g1", chunks(a["L0_ffn_Wg1"], a["L0_ffn_bg1"]))
    put("f_g2", np.concatenate([a["L0_ffn_Wg2"], a["L0_ffn_bg2"][None]], 0))
    put("f_out", chunks(a["L0_ffn_Wp"], a["L0_ffn_bp"]))
    put("conv", np.concatenate([a["L0_ffn_conv_w"][:, 0, :], a["L0_ffn_conv_b"][:, None]], 1))
    put("l_qkv", chunks(a["L1_attn_w_qkv"].T, a["L1_attn_b_qkv"]))
    put("l_out", chunks(a["L1_attn_w_proj"].T, a["L1_attn_b_proj"]))
    put("m_g", chunks(a["L1_ffn_Wg"]))
    pos = np.zeros((P, P), np.float32)
    pos[:T, :T] = pos[T:, T:] = a["L0_ffn_pos_bias"]
    w1 = np.concatenate([chunks(a["L1_ffn_W1"][e], a["L1_ffn_b1"][e]) for e in range(EX)], 1)
    w2 = a["L1_ffn_W2"].reshape(EX, FT, P, D).transpose(2, 0, 1, 3).reshape(P, -1)

    arrays = {"x": x.reshape(TOKENS, D), "weights": wts, "consts": shape_constants(), "pos_bias": pos,
              "w1": w1, "w2": w2, "b2": a["L1_ffn_b2"].reshape(1, -1)}
    arrays = {f"in_{k}": np.ascontiguousarray(v) for k, v in arrays.items()}
    nc = bacc.Bacc("TRN2", target_bir_lowering=False, num_devices=1)
    aps = [nc.dram_tensor(k, v.shape, F32, kind="ExternalInput").ap() for k, v in arrays.items()]
    out = nc.dram_tensor("out", (TOKENS, D), F32, kind="ExternalOutput").ap()
    audio_tower(nc, *aps, out)
    got = run_bass_kernel_spmd(nc, [arrays], core_ids=[0])
    return got.results[0]["out"].reshape(SEQS, T, D)
```

```python
from contextlib import ExitStack

import numpy as np
import concourse.bass as bass
from concourse import mybir

F32 = mybir.dt.float32
BF16 = mybir.dt.bfloat16
I32 = mybir.dt.int32
U32 = mybir.dt.uint32
ALU = mybir.AluOpType
ACT = mybir.ActivationFunctionType
AX = mybir.AxisListType.X

SEQS, SEQ_IN, D = 32, 125, 192
T = 64
P = 128
TOKENS = SEQS * T
TILES = TOKENS // P
NU = 4
TURNS = TILES // NU
C = D // 2
H, HD = 12, 16
HC = H // 2
M = 44
FEPS = 1e-4
LNEPS = 1e-5
E3, HD3 = 3, 64
EX, FF = 8, 768
FT = FF // P
SLOT_TILES = (TOKENS + EX * (P - 1)) // P
SLOT_TILES += -SLOT_TILES % 4
BIG = -1e30

_W = {}
_n = 0
for _name, _cols in (("a_qkv", 2 * 3 * D), ("feat", HC * M), ("a_out", 2 * D), ("f_qk", 2 * 2 * D), ("f_v", 2 * D),
                     ("f_g1", 2 * 32), ("f_g2", E3), ("f_out", 2 * D), ("conv", 4), ("l_qkv", 2 * 3 * D),
                     ("l_out", 2 * D), ("m_g", 2 * EX)):
    _W[_name] = (_n, _n + _cols)
    _n += _cols
NW = _n
NW_A = _W["feat"][1]

_K = {}
_n = 0
for _name, _cols in (("ident", P), ("half", P), ("split", P), ("block", HC * M), ("diag", HC), ("causal", P),
                     ("kvmask", 68), ("cos", 2 * D), ("sin", 2 * D), ("triu", P), ("eidx", E3), ("eord", EX),
                     ("thr", TILES), ("slot", SLOT_TILES), ("eps", 3)):
    _K[_name] = (_n, _n + _cols)
    _n += _cols
NK = _n


def shape_constants():
    k = np.zeros((P, NK), np.float32)

    def put(name, rows, value):
        a, b = _K[name]
        k[:rows, a:b] = value

    put("ident", P, np.eye(P))
    seq = np.arange(P) // T
    put("half", 2, np.stack([seq == 0, seq == 1]))
    put("split", 2, BIG * np.stack([seq == 1, seq == 0]))
    blk = np.zeros((C, HC, M))
    for h in range(HC):
        blk[16 * h:16 * h + 16, h] = HD ** -0.25
    put("block", C, blk.reshape(C, -1))
    dg = np.zeros((C, HC))
    for h in range(HC):
        dg[16 * h:16 * h + 16, h] = 0.5 * HD ** -0.5
    put("diag", C, dg)
    q, s = np.arange(P)[:, None], np.arange(P)[None, :]
    put("causal", P, np.where((q // T == s // T) & (s <= q), 0.0, BIG))
    kv = np.zeros((2 * M, 2, 2, 17))
    for par in range(2):
        kv[M * par:M * par + M, :, par] = 1.0
    put("kvmask", 2 * M, kv.reshape(2 * M, -1))
    inv = (1.0 / np.float32(10000.0) ** (np.arange(0, HD, 2, dtype=np.float32) / np.float32(HD))).astype(np.float32)
    fr = (np.arange(T, dtype=np.float32)[:, None] * inv[None, :]).astype(np.float32)
    cos, sin = np.cos(fr.astype(np.float64)), np.sin(fr.astype(np.float64))
    cos, sin = np.tile(cos, (2, 1)), np.tile(sin, (2, 1))
    cos = np.concatenate([cos, cos], -1)
    sin = np.concatenate([-sin, sin], -1)
    scale = np.array([HD ** -0.5, 1.0])[None, :, None, None]
    put("cos", P, (cos[:, None, None, :] * scale * np.ones((1, 1, H, 1))).reshape(P, -1))
    put("sin", P, (sin[:, None, None, :] * scale * np.ones((1, 1, H, 1))).reshape(P, -1))
    put("triu", P, (q < s).astype(np.float32))
    put("eidx", P, np.arange(1, E3 + 1))
    put("eord", P, EX - np.arange(EX))
    put("thr", P, P * np.arange(TILES))
    put("slot", P, np.arange(SLOT_TILES))
    put("eps", P, np.array([LNEPS, -0.5, FEPS]))
    return k


def audio_tower(nc, x, weights, consts, pos_bias, w1, w2, b2, out):
    ctx = ExitStack()
    with ctx:
        def sb(name, shape, dt=F32):
            return ctx.enter_context(nc.sbuf_tensor(name, shape, dt))

        def each(name, shape, dt=F32):
            return [sb(f"{name}{u}", shape, dt) for u in range(NU)]

        def sem(name):
            return ctx.enter_context(nc.semaphore(name))

        def ev(name):
            return [sem(name)] * NU

        def ev_dma(name):
            return [sem(f"{name}_{u}") for u in range(NU)]

        xs_dram = nc.dram_tensor("sorted_x", (SLOT_TILES * P, D), F32, kind="Internal").ap()
        ys_dram = nc.dram_tensor("sorted_y", (SLOT_TILES * P, D), F32, kind="Internal").ap()

        W = sb("weights_sb", [C + 1, NW])
        K = sb("consts_sb", [P, NK])

        def wv(name, c=None, rows=C):
            a, b = _W[name]
            if c is not None:
                n = (b - a) // 2
                a, b = a + c * n, a + c * n + n
            return W[0:rows, a:b]

        def kc(name, rows=P):
            return K[0:rows, _K[name][0]:_K[name][1]]

        ident = kc("ident")
        feat = wv("feat")
        bf_ident = sb("bf_ident", [P, P], BF16)
        bf_causal = sb("bf_causal", [P, P], BF16)
        bf_half = sb("bf_half", [2, P], BF16)
        bf_split = sb("bf_split", [2, P], BF16)
        bias_mask = sb("bias_mask", [P, P])
        ones_row = sb("ones_row", [1, P])
        
        h_all = sb("h_all", [P, TILES, D])
        x_all = sb("x_all", [P, TILES, 2 * P])
        stash = sb("stash", [P, TILES * (H * M + HC * 68)])
        kd_all = stash[:, 0:TILES * H * M].rearrange("p (t n) -> p t n", t=TILES)
        vbd_all = stash[:, TILES * H * M:].rearrange("p (t n) -> p t n", t=TILES)
        w1_sb = stash[:, 0:EX * 2 * FF]
        b2_sb = W[0:1, 0:EX * D]
        kmx_all = sb("kmx_all", [P, TILES])
        kmax = sb("kmax", [P, 4])
        lg_all = sb("lg_all", [P, TILES, EX])

        actT = each("actT", [C + 1, 2 * P])
        xnT = each("xnT", [C + 1, 2 * P])
        rows = each("rows", [P, 3 * D])
        hs = [r[:, 0:D] for r in rows]
        xn = [r[:, D:2 * D] for r in rows]
        att = [r[:, 2 * D:3 * D] for r in rows]
        kvs = [r[0:2 * M, 0:HC * 68] for r in rows]
        stats = each("stats", [P, 16])
        small = each("small", [P, 64])
        big_b = each("big_b", [P, FF])
        big_c = each("big_c", [P, FF])
        shared = sb("shared", [P, NU * (FF + H * M + 6 * P + 2 * HC * 34)])

        def cut(start, n):
            return [shared[:, NU * start + u * n:NU * start + (u + 1) * n] for u in range(NU)]

        big_a = cut(0, FF)
        k1 = cut(FF, H * M)
        pad = cut(FF + H * M, 6 * P)
        vl = cut(FF + H * M + 6 * P, 2 * HC * 34)
        w2_sb = shared[:, 0:EX * FT * D]
        xin = [b[:, 0:D] for b in big_c]
        qe = [b[:, 0:H * M] for b in big_c]
        qc = [b[0:HD3, 3 * P:4 * P] for b in big_c]
        qkT = [b[0:C, 0:2 * P] for b in big_b]
        qksq = [b[0:C, 2 * P:4 * P] for b in big_b]
        zeros = pad[0][:, 0:D]
        vf = each("vf", [P, E3 * (HD3 + 1)])
        g1T = each("g1T", [33, P])

        rsm = sb("router_small", [P, 192])
        gate = sb("gate", [P, TILES])
        slots = sb("slots", [P, TILES], U32)
        tile_ex = sb("tile_ex", [P, SLOT_TILES], I32)

        ps = ctx.enter_context(nc.psum_tensor("ps", [P, 8, 512], F32))

        consts_in, wa_in, wb_in, moe_in = sem("consts_in"), sem("wa_in"), sem("wb_in"), sem("moe_in")
        w1_in, zero_out = sem("w1_in"), sem("zero_out")
        setup_v, setup_pe, ready, ready_p = sem("setup_v"), sem("setup_pe"), sem("ready"), sem("ready_p")
        x_in = ev_dma("x_in")
        S = {n: ev(n) for n in """
            xT_ps xT_sb sc_ps nmx p_sb pT_ps pT_sb px_ps hstore xstore kT_ps v_ps k_sb vbd dash_ps kd
            hrow mv var_eps rstd xnr xnT_ps xnT_sb attr attT_ps attT_sb pr_ps
            k1e k1 qT_ps q_sb kv_ps qd_ps kv_sb qe qx q1T_ps q1T_sb num_ps
            fqk_ps fv_ps g1_sb qf_sb vf_sb kf_sb conv gl_ps gs ge gp gep fs_ps nf fp_sb fpT_ps fpT_sb fo_ps
            lqk_ps lv_ps lqk_sb lv_a lv_d rope lT_ps lT_sb ls_half ls_ps pl px lpT_ps lpT_sb lo_ps store lg_ps lg
            """.split()}
        k_max, k_maxall, k_negmax = sem("k_max"), sem("k_maxall"), sem("k_negmax")
        vstep, pstep = sem("vstep"), sem("pstep")
        r_diff, r_exp, r_onehot, r_count, r_slots = (sem(n) for n in ("r_diff", "r_exp", "r_onehot", "r_count", "r_slots"))
        scattered, gathered, out_row, out_done = sem("scattered"), [sem(f"gathered{j}") for j in range(4)], sem("out_row"), sem("out_done")
        Z = {n: ev("m_" + n) for n in "xT_ps xT_sb h_ps h_sb hT_ps hT_sb y_ps y_sb".split()}
        Z.update({n: ev_dma("m_" + n) for n in ("x_in", "y_out")})
        block = ctx.enter_context(nc.Block())

        def bank(u, b):
            return ps[:, 2 * u + b, :]

        def banks(u, a, b):
            return ps[:, 2 * u + a:2 * u + b, :]

        def turn(eng, i):
            return [eng.snap(i * NU + (u + 1)) for u in range(NU)]

        CREDIT = NU

        def give_credit(eng, sems):
            for s in sems:
                eng.sem_inc(s, CREDIT)

        def stage_counts(eng, i):
            return [[[eng.snap(i * (3 * NU) + (before + NU * r + u + 1)) for u in range(NU)] for r in range(3)] for before in (0, TILES)]

        def v_rows(u, b, par):
            return bank(u, 1)[T * b:T * b + T, 0:D].rearrange("p (c r d) -> p c r d", c=HC, r=2)[:, :, par, :]

        def v_place(u, b, par):
            return vl[u][T * par:T * par + T, :].rearrange("p (b c r d) -> p b c r d", b=2, c=HC, r=2)[:, b, :, par, 0:HD]

        def features(pe, u):
            for half in range(2):
                pe.matmul(bank(u, half)[:, 0:HC * M], qkT[u][:, half * P:half * P + P], feat[:, :], start=True, stop=True)
            for half in range(2):
                last = pe.matmul(bank(u, 1)[:, 264 + HC * half:264 + HC * half + HC], qksq[u][:, half * P:half * P + P], kc("diag", C),
                                 start=True, stop=True)
            return last

        def y_rows(t):
            return hs[t % 4]

        def conv_w(k):
            return wv("conv", rows=HD3)[:, k:k + 1]

        @block.sync
        def _(sp):
            sp.dma_start(K[:, :], consts).then_inc(consts_in, 16)
            sp.dma_start(W[:, 0:NW_A], weights[:, 0:NW_A]).then_inc(wa_in, 16)
            xt = x.rearrange("(t p) d -> t p d", p=P)
            with sp.Fori(0, TURNS) as i:
                n1 = turn(sp, i)
                for u in range(NU):
                    sp.wait_ge(S["px_ps"][u], n1[u])
                    sp.dma_start(xin[u][:, :], xt[bass.ds(NU * i + u, 1)].rearrange("o p d -> (o p) d")).then_inc(x_in[u], 16)
            sp.wait_ge(S["kv_ps"][0], CREDIT + TILES)
            sp.dma_start(w1_sb[0:C + 1, :], w1).then_inc(w1_in, 16)
            sp.wait_ge(S["lg"][0], CREDIT + TILES)
            sp.dma_start(w2_sb, w2).then_inc(moe_in, 16)
            sp.dma_start(b2_sb, b2).then_inc(moe_in, 16)
            sp.wait_ge(scattered, 16 * TILES)
            xst, yst = (a.rearrange("(t p) d -> t p d", p=P) for a in (xs_dram, ys_dram))
            for u in range(NU):
                sp.dma_start(xn[u][:, :], xst[u]).then_inc(Z["x_in"][u], 16)
            with sp.Fori(0, SLOT_TILES // NU - 1) as i:
                n1 = turn(sp, i)
                for u in range(NU):
                    sp.wait_ge(Z["xT_ps"][u], n1[u])
                    sp.dma_start(xn[u][:, :], xst[bass.ds(NU * i + u + NU, 1)].rearrange("o p d -> (o p) d")).then_inc(Z["x_in"][u], 16)
                for u in range(NU):
                    sp.wait_ge(Z["y_sb"][u], n1[u] + CREDIT)
                    sp.dma_start(yst[bass.ds(NU * i + u, 1)].rearrange("o p d -> (o p) d"), att[u][:, :]).then_inc(Z["y_out"][u], 16)
            for u in range(NU):
                sp.wait_ge(Z["y_sb"][u], CREDIT + SLOT_TILES - NU + u + 1)
                sp.dma_start(yst[SLOT_TILES - NU + u], att[u][:, :]).then_inc(Z["y_out"][u], 16)
            ot = out.rearrange("(t p) d -> t p d", p=P)
            for t in range(0, TILES, 4):
                sp.wait_ge(out_row, t + 4)
                sp.dma_start(ot[t:t + 4].rearrange("t p d -> p t d"), h_all[:, t:t + 4, :]).then_inc(out_done, 16)
            sp.wait_ge(out_done, 16 * (TILES // 4))

        @block.scalar
        def _(act):
            act.dma_start(W[:, NW_A:NW], weights[:, NW_A:NW]).then_inc(wb_in, 16)
            act.dma_start(bias_mask[:, :], pos_bias).then_inc(wb_in, 16)
            act.wait_ge(ready, 1)
            act.wait_ge(ready_p, 1)
            act.dma_start(xs_dram.rearrange("(t p) d -> p t d", p=P),
                          zeros[:, :].unsqueeze(1).broadcast_to([P, SLOT_TILES, D])).then_inc(zero_out, 16)

            with act.Fori(0, TURNS) as i:
                n1 = turn(act, i)
                for u in range(NU):
                    act.wait_ge(S["xT_ps"][u], n1[u])
                    act.activation(big_a[u][0:C, 0:2 * P], bank(u, 0)[0:C, 0:2 * P], ACT.Copy).then_inc(S["xT_sb"][u], 1)
                for u in range(NU):
                    act.wait_ge(S["nmx"][u], n1[u])
                    act.activation(att[u][:, 0:P], bank(u, 1)[:, 0:P], ACT.Exp, scale=D ** -0.5, bias=small[u][:, 1:2],
                                   accum_out=small[u][:, 2:3]).then_inc(S["p_sb"][u], 1)
                for u in range(NU):
                    act.wait_ge(S["xnT_ps"][u], n1[u])
                    act.wait_ge(S["xstore"][u], n1[u])
                    act.activation(xnT[u][0:C, :], bank(u, 0)[0:C, 0:2 * P], ACT.Copy).then_inc(S["xnT_sb"][u], 1)
                for u in range(NU):
                    act.wait_ge(S["kT_ps"][u], n1[u])
                    act.activation(qkT[u][:, :], bank(u, 0)[0:C, 0:2 * P], ACT.Copy)
                    act.activation(qksq[u][:, :], bank(u, 0)[0:C, 0:2 * P], ACT.Square).then_inc(S["k_sb"][u], 1)

            act.wait_ge(k_negmax, 1)
            act.wait_ge(S["xstore"][0], CREDIT + TILES)
            with act.Fori(0, TURNS) as i:
                n1 = turn(act, i)
                m, l = stage_counts(act, i)
                for u in range(NU):
                    act.wait_ge(S["kv_ps"][u], n1[u])
                    act.activation(k1[u][:, :], kd_all[:, bass.ds(NU * i + u, 1), :].rearrange("p o n -> p (o n)"),
                                   ACT.Exp, bias=kmax[:, 2:3]).then_inc(S["k1e"][u], 1)
                for u in range(NU):
                    act.wait_ge(S["qT_ps"][u], n1[u])
                    act.activation(qkT[u][:, :], bank(u, 0)[0:C, 0:2 * P], ACT.Copy)
                    act.activation(qksq[u][:, :], bank(u, 0)[0:C, 0:2 * P], ACT.Square).then_inc(S["q_sb"][u], 1)
                for u in range(NU):
                    act.wait_ge(S["qe"][u], n1[u])
                    act.activation(qe[u][:, :], qe[u][:, :], ACT.Exp).then_inc(S["qx"][u], 1)
                for u in range(NU):
                    act.wait_ge(S["q1T_ps"][u], n1[u])
                    act.activation(big_a[u][0:2 * M, :].rearrange("p (b n) -> p b n", b=2), banks(u, 0, 2)[0:2 * M, :, 0:3 * P],
                                   ACT.Copy, bias=FEPS).then_inc(S["q1T_sb"][u], 1)

                def output_stage(r):
                    for u in range(NU):
                        act.wait_ge(S["attT_ps"][u], m[r][u])
                        act.activation(actT[u][0:C, :], bank(u, 1)[0:C, 0:2 * P], ACT.Copy).then_inc(S["attT_sb"][u], 1)
                    for u in range(NU):
                        act.wait_ge(S["xnT_ps"][u], l[r][u])
                        act.activation(xnT[u][0:C, :], bank(u, 0)[0:C, 0:2 * P], ACT.Copy).then_inc(S["xnT_sb"][u], 1)

                output_stage(0)
                for u in range(NU):
                    act.wait_ge(S["fqk_ps"][u], n1[u])
                    act.activation(g1T[u][0:32, :], bank(u, 0)[0:32, 3 * P:4 * P], ACT.Relu).then_inc(S["g1_sb"][u], 1)
                    act.activation(big_a[u][0:HD3, 0:3 * P], bank(u, 0)[0:HD3, 0:3 * P], ACT.Copy).then_inc(S["qf_sb"][u], 1)
                    act.wait_ge(S["fv_ps"][u], n1[u])
                    act.activation(vf[u][:, :].rearrange("p (e n) -> p e n", e=E3)[:, :, 0:HD3],
                                   bank(u, 1)[:, 0:D].rearrange("p (e n) -> p e n", e=E3), ACT.Copy).then_inc(S["vf_sb"][u], 1)
                for u in range(NU):
                    act.wait_ge(S["gs"][u], n1[u])
                    act.activation(small[u][:, 8:11], small[u][:, 4:7], ACT.Exp, accum_out=small[u][:, 11:12]).then_inc(S["ge"][u], 1)
                for u in range(NU):
                    act.wait_ge(S["gp"][u], n1[u])
                    act.activation(small[u][:, 16:19], small[u][:, 12:15], ACT.Exp).then_inc(S["gep"][u], 1)
                for u in range(NU):
                    act.wait_ge(S["nf"][u], n1[u])
                    for e in range(E3):
                        last = act.activation(big_b[u][:, e * P:e * P + P], bank(u, 0)[:, e * P:e * P + P], ACT.Exp,
                                              scale=HD3 ** -0.5, bias=small[u][:, 36 + e:37 + e])
                    last.then_inc(S["fp_sb"][u], 1)
                output_stage(1)
                for u in range(NU):
                    act.wait_ge(S["lqk_ps"][u], n1[u])
                    act.activation(big_a[u][:, 0:2 * D], bank(u, 0)[:, 0:2 * D], ACT.Copy).then_inc(S["lqk_sb"][u], 1)
                    act.wait_ge(S["lv_ps"][u], n1[u])
                    for par in range(2):
                        last = act.activation(v_place(u, 0, par), v_rows(u, 0, par), ACT.Copy)
                    last.then_inc(S["lv_a"][u], 1)
                for u in range(NU):
                    act.wait_ge(S["lT_ps"][u], n1[u])
                    act.activation(big_b[u][:, :].rearrange("p (b n) -> p b n", b=2), banks(u, 0, 2)[:, :, 0:3 * P],
                                   ACT.Copy).then_inc(S["lT_sb"][u], 1)
                for u in range(NU):
                    act.wait_ge(S["pl"][u], n1[u])
                    act.activation(big_c[u][:, :], big_c[u][:, :], ACT.Exp).then_inc(S["px"][u], 1)
                for u in range(NU):
                    act.wait_ge(S["lpT_ps"][u], n1[u])
                    act.activation(big_a[u][:, :].rearrange("p (b n) -> p b n", b=2), banks(u, 0, 2)[:, :, 0:3 * P],
                                   ACT.Copy).then_inc(S["lpT_sb"][u], 1)
                output_stage(2)

            act.wait_ge(r_diff, 1)
            act.activation(big_b[2][:, P:2 * P], big_b[2][:, 0:P], ACT.Exp).then_inc(r_exp, 1)

            with act.Fori(0, SLOT_TILES // NU) as i:
                n1 = turn(act, i)
                for u in range(NU):
                    act.wait_ge(Z["h_ps"][u], n1[u])
                    act.activation(big_b[u][:, :].rearrange("p (b n) -> p b n", b=2), banks(u, 0, 2)[:, :, 0:FF // 2],
                                   ACT.Silu).then_inc(Z["h_sb"][u], 1)

        @block.tensor
        def _(pe):
            pe.wait_ge(consts_in, 16)
            pe.wait_ge(wa_in, 16)
            pe.wait_ge(ready, 1)
            pe.wait_ge(ready_p, 1)

            def transposes(dst_bank, rows, src, cols, n, at=0, stride=P):
                for c in range(n):
                    last = pe.transpose(dst_bank[0:cols, at + stride * c:at + stride * c + rows], src[:, c * cols:(c + 1) * cols], ident)
                return last

            def project(dst, lhs, w, bias):
                pe.matmul(dst, lhs[0:C, 0:P], wv(w, 0), start=True, stop=False)
                k = C + 1 if bias else C
                return pe.matmul(dst, lhs[0:k, P:2 * P], wv(w, 1, k), start=False, stop=True)

            with pe.Fori(0, TURNS) as i:
                n1 = turn(pe, i)
                x_n = pe.snap(i * 16 + 16)
                for u in range(NU):
                    pe.wait_ge(x_in[u], x_n)
                    pe.wait_ge(S["kd"][u], n1[u])
                    transposes(bank(u, 0), P, xin[u], C, 2).then_inc(S["xT_ps"][u], 1)
                for u in range(NU):
                    pe.wait_ge(S["xT_sb"][u], n1[u])
                    for c in range(2):
                        xT = big_a[u][0:C, c * P:c * P + P]
                        pe.matmul(bank(u, 1)[:, 0:P], xT, xT, start=c == 0, stop=False)
                    pe.matmul(bank(u, 1)[:, 0:P], bf_half[:, :], bf_split[:, :], start=False, stop=True).then_inc(S["sc_ps"][u], 1)
                for u in range(NU):
                    pe.wait_ge(S["p_sb"][u], n1[u])
                    pe.transpose(bank(u, 0)[:, 2 * P:3 * P], att[u][:, 0:P], ident).then_inc(S["pT_ps"][u], 1)
                for u in range(NU):
                    pe.wait_ge(S["pT_sb"][u], n1[u])
                    pe.matmul(bank(u, 1)[:, P:P + D], big_b[u][:, 0:P], xin[u][:, :], start=True, stop=True).then_inc(S["px_ps"][u], 1)
                for u in range(NU):
                    pe.wait_ge(S["xnr"][u], n1[u])
                    transposes(bank(u, 0), P, xn[u], C, 2).then_inc(S["xnT_ps"][u], 1)
                for u in range(NU):
                    pe.wait_ge(S["xnT_sb"][u], n1[u])
                    for half in range(2):
                        for c in range(2):
                            last = pe.matmul(bank(u, 0)[0:C, half * P:half * P + P], wv("a_qkv", c)[:, D + half * C:D + half * C + C],
                                             xnT[u][0:C, c * P:c * P + P], start=c == 0, stop=c == 1)
                    last.then_inc(S["kT_ps"][u], 1)
                    for c in range(2):
                        last = pe.matmul(bank(u, 1)[:, 320:512], xnT[u][0:C, c * P:c * P + P], wv("a_qkv", c)[:, 2 * D:3 * D],
                                         start=c == 0, stop=c == 1)
                    last.then_inc(S["v_ps"][u], 1)
                for u in range(NU):
                    pe.wait_ge(S["k_sb"][u], n1[u])
                    pe.wait_ge(S["vbd"][u], n1[u])
                    features(pe, u).then_inc(S["dash_ps"][u], 1)

            pe.wait_ge(wb_in, 32)
            pe.wait_ge(ready, 2)
            pe.wait_ge(S["xstore"][0], CREDIT + TILES)
            with pe.Fori(0, TURNS) as i:
                n1 = turn(pe, i)
                m, l = stage_counts(pe, i)
                for u in range(NU):
                    pe.wait_ge(S["lg"][u], n1[u])
                    for half in range(2):
                        for c in range(2):
                            last = pe.matmul(bank(u, 0)[0:C, half * P:half * P + P], wv("a_qkv", c)[:, half * C:half * C + C],
                                             x_all[0:C, bass.ds(NU * i + u, 1), c * P:c * P + P].rearrange("p o n -> p (o n)"),
                                             start=c == 0, stop=c == 1)
                    last.then_inc(S["qT_ps"][u], 1)
                for u in range(NU):
                    pe.wait_ge(S["k1"][u], n1[u])
                    for c in range(HC):
                        last = pe.matmul(bank(u, 1)[0:2 * M, c * 68:c * 68 + 68], k1[u][:, c * 2 * M:(c + 1) * 2 * M],
                                         vbd_all[:, bass.ds(NU * i + u, 1), c * 68:c * 68 + 68].rearrange("p o n -> p (o n)"),
                                         start=True, stop=True)
                    last.then_inc(S["kv_ps"][u], 1)
                for u in range(NU):
                    pe.wait_ge(S["q_sb"][u], n1[u])
                    pe.wait_ge(S["kv_sb"][u], n1[u])
                    features(pe, u).then_inc(S["qd_ps"][u], 1)
                for u in range(NU):
                    pe.wait_ge(S["qx"][u], n1[u])
                    for b in range(2):
                        last = transposes(bank(u, b), P, qe[u][:, b * 6 * M:(b + 1) * 6 * M], 2 * M, 3)
                    last.then_inc(S["q1T_ps"][u], 1)
                for u in range(NU):
                    pe.wait_ge(S["q1T_sb"][u], n1[u])
                    for c in range(HC):
                        last = pe.matmul(bank(u, 0)[:, c * 68:c * 68 + 68], big_a[u][0:2 * M, c * P:c * P + P],
                                         kvs[u][:, c * 68:c * 68 + 68], start=True, stop=True)
                    last.then_inc(S["num_ps"][u], 1)

                def output_stage(r, w):
                    for u in range(NU):
                        pe.wait_ge(S["attr"][u], m[r][u])
                        transposes(bank(u, 1), P, att[u], C, 2).then_inc(S["attT_ps"][u], 1)
                    for u in range(NU):
                        pe.wait_ge(S["attT_sb"][u], m[r][u])
                        project(bank(u, 1)[:, 2 * P:2 * P + D], actT[u], w, True).then_inc(S["pr_ps"][u], 1)
                    for u in range(NU):
                        pe.wait_ge(S["xnr"][u], l[r][u])
                        transposes(bank(u, 0), P, xn[u], C, 2).then_inc(S["xnT_ps"][u], 1)

                output_stage(0, "a_out")
                for u in range(NU):
                    pe.wait_ge(S["xnT_sb"][u], l[0][u])
                    for c in range(2):
                        k = C + c
                        last = pe.matmul(bank(u, 0)[0:32, 3 * P:4 * P], wv("f_g1", c, k), xnT[u][0:k, c * P:c * P + P], start=c == 0, stop=c == 1)
                    for e in range(E3):
                        for c in range(2):
                            k = C + c
                            last = pe.matmul(bank(u, 0)[:, e * P:e * P + P], wv("f_qk", c, k)[:, e * P:e * P + P],
                                             xnT[u][0:k, c * P:c * P + P], start=c == 0, stop=c == 1)
                    last.then_inc(S["fqk_ps"][u], 1)
                    project(bank(u, 1)[:, 0:D], xnT[u], "f_v", True).then_inc(S["fv_ps"][u], 1)
                for u in range(NU):
                    pe.wait_ge(S["g1_sb"][u], n1[u])
                    pe.wait_ge(S["vf_sb"][u], n1[u])
                    pe.matmul(bank(u, 1)[:, D:D + E3], g1T[u][:, :], wv("f_g2", rows=33), start=True, stop=True).then_inc(S["gl_ps"][u], 1)
                for u in range(NU):
                    pe.wait_ge(S["qf_sb"][u], n1[u])
                    pe.wait_ge(S["kf_sb"][u], n1[u])
                    for e in (1, 2, 0):
                        if e == 0:
                            pe.wait_ge(S["conv"][u], n1[u])
                        q = qc[u][:, :] if e == 0 else big_a[u][0:HD3, e * P:e * P + P]
                        dst = bank(u, 0)[:, e * P:e * P + P]
                        pe.matmul(dst, q, big_a[u][0:HD3, (3 + e) * P:(4 + e) * P], start=True, stop=False)
                        if e == 2:
                            last = pe.matmul(dst, ident, bias_mask[:, :], start=False, stop=True)
                        else:
                            last = pe.matmul(dst, bf_ident[:, :], bf_causal[:, :], start=False, stop=True)
                    last.then_inc(S["fs_ps"][u], 1)
                for u in range(NU):
                    pe.wait_ge(S["fp_sb"][u], n1[u])
                    transposes(bank(u, 1), P, big_b[u], P, 3).then_inc(S["fpT_ps"][u], 1)
                for u in range(NU):
                    pe.wait_ge(S["fpT_sb"][u], n1[u])
                    for e in range(E3):
                        last = pe.matmul(bank(u, 0)[:, 65 * e:65 * e + 65], big_c[u][:, e * P:e * P + P], vf[u][:, 65 * e:65 * e + 65],
                                         start=True, stop=True)
                    last.then_inc(S["fo_ps"][u], 1)
                output_stage(1, "f_out")
                for u in range(NU):
                    pe.wait_ge(S["xnT_sb"][u], l[1][u])
                    for c in range(2):
                        k = C + c
                        last = pe.matmul(bank(u, 0)[:, 0:2 * D], xnT[u][0:k, c * P:c * P + P], wv("l_qkv", c, k)[:, 0:2 * D], start=c == 0, stop=c == 1)
                    last.then_inc(S["lqk_ps"][u], 1)
                    for c in range(2):
                        k = C + c
                        last = pe.matmul(bank(u, 1)[:, 0:D], xnT[u][0:k, c * P:c * P + P], wv("l_qkv", c, k)[:, 2 * D:3 * D], start=c == 0, stop=c == 1)
                    last.then_inc(S["lv_ps"][u], 1)
                for u in range(NU):
                    pe.wait_ge(S["rope"][u], n1[u])
                    pe.wait_ge(S["lv_a"][u], n1[u])
                    pe.wait_ge(S["lv_d"][u], n1[u])
                    for s in range(2):
                        last = transposes(bank(u, s), P, pad[u][:, s * 3 * P:(s + 1) * 3 * P], P, 3)
                    last.then_inc(S["lT_ps"][u], 1)
                for half in range(2):
                    for u in range(NU):
                        if half == 0:
                            pe.wait_ge(S["lT_sb"][u], n1[u])
                        else:
                            pe.wait_ge(S["ls_half"][u], n1[u])
                        for j in (half, 2 + half):
                            for g in range(3):
                                for b in range(2):
                                    q = big_b[u][32 * j:32 * j + 32, g * P + b * T:g * P + b * T + T]
                                    k = big_b[u][32 * j:32 * j + 32, (3 + g) * P + b * T:(3 + g) * P + b * T + T]
                                    at = (j % 2 * 3 + g) * T
                                    last = pe.matmul(bank(u, j // 2)[b * T:b * T + T, at:at + T], q, k, start=True, stop=True)
                        last.then_inc(S["ls_half" if half == 0 else "ls_ps"][u], 1)
                for u in range(NU):
                    pe.wait_ge(S["px"][u], n1[u])
                    for b in range(2):
                        last = transposes(bank(u, b), P, big_c[u][:, b * 3 * P:(b + 1) * 3 * P], P, 3)
                    last.then_inc(S["lpT_ps"][u], 1)
                for u in range(NU):
                    pe.wait_ge(S["lpT_sb"][u], n1[u])
                    for c in range(HC):
                        for b in range(2):
                            last = pe.matmul(bank(u, 0)[b * T:b * T + T, c * 34:c * 34 + 34], big_a[u][:, c * P + b * T:c * P + b * T + T],
                                             vl[u][:, (b * HC + c) * 34:(b * HC + c) * 34 + 34], start=True, stop=True)
                    last.then_inc(S["lo_ps"][u], 1)
                output_stage(2, "l_out")
                for u in range(NU):
                    pe.wait_ge(S["xnT_sb"][u], l[2][u])
                    project(bank(u, 1)[:, 0:EX], xnT[u], "m_g", False).then_inc(S["lg_ps"][u], 1)

            pe.wait_ge(r_onehot, 1)
            pe.matmul(bank(0, 0)[:, 0:P], kc("triu"), big_b[2][:, 4 * P:5 * P], start=True, stop=True)
            pe.matmul(bank(0, 1)[:, 0:P], big_b[3][:, 0:P], big_b[2][:, 4 * P:5 * P], start=True, stop=True).then_inc(r_count, 1)

            pe.wait_ge(r_slots, 2)
            pe.wait_ge(w1_in, 16)
            pe.wait_ge(moe_in, 32)
            with pe.Fori(0, SLOT_TILES // NU) as i:
                n1 = turn(pe, i)
                x_n = pe.snap(i * 16 + 16)
                expert = [pe.value_load(tile_ex[0:1, bass.ds(NU * i + u, 1)], min_val=0, max_val=EX - 1) for u in range(NU)]
                for u in range(NU):
                    pe.wait_ge(Z["x_in"][u], x_n)
                    transposes(bank(u, 0), P, xn[u], C, 2).then_inc(Z["xT_ps"][u], 1)
                for u in range(NU):
                    pe.wait_ge(Z["xT_sb"][u], n1[u])
                    pe.wait_ge(Z["y_sb"][u], n1[u])
                    for f in range(2):
                        for c in range(2):
                            k = C + c
                            last = pe.matmul(bank(u, f)[:, 0:FF // 2], xnT[u][0:k, c * P:c * P + P],
                                             w1_sb[0:k, bass.ds(expert[u] * (2 * FF) + (c * FF + f * (FF // 2)), FF // 2)], start=c == 0, stop=c == 1)
                    last.then_inc(Z["h_ps"][u], 1)
                for u in range(NU):
                    pe.wait_ge(Z["h_sb"][u], n1[u])
                    for b in range(2):
                        last = transposes(bank(u, b), P, big_b[u][:, b * 3 * P:(b + 1) * 3 * P], P, 3)
                    last.then_inc(Z["hT_ps"][u], 1)
                for u in range(NU):
                    pe.wait_ge(Z["hT_sb"][u], n1[u])
                    pe.matmul(bank(u, 1)[:, 0:D], ones_row[:, :], b2_sb[0:1, bass.ds(expert[u] * D, D)], start=True, stop=False)
                    for f in range(FT):
                        last = pe.matmul(bank(u, 1)[:, 0:D], big_c[u][:, f * P:f * P + P], w2_sb[:, bass.ds(expert[u] * (FT * D) + f * D, D)],
                                         start=False, stop=f == FT - 1)
                    last.then_inc(Z["y_ps"][u], 1)

        @block.vector
        def _(dve):
            count = [0]
            base = [0]

            def mark(ins):
                count[0] += 1
                ins.then_inc(vstep, 1)
                return count[0]

            def after(step):
                dve.wait_ge(vstep, base[0] + step)

            def loop_base(eng_i, before, per_turn):
                base[0] = dve.snap(eng_i * per_turn + before)
                count[0] = 0

            give_credit(dve, [S[n][0] for n in ("kd", "hstore", "xstore", "store", "lg", "px_ps", "kv_ps")])
            give_credit(dve, [Z["y_sb"][0], *Z["y_out"]])
            dve.memset(ones_row[:, :], 1.0)
            for u in range(NU):
                dve.memset(actT[u][C:C + 1, :], 1.0)
                dve.memset(xnT[u][C:C + 1, :], 1.0)
                dve.memset(g1T[u][32:33, :], 1.0)
                dve.memset(vf[u][:, :], 1.0)
            dve.wait_ge(consts_in, 16)
            dve.tensor_copy(bf_ident[:, :], ident)
            dve.tensor_copy(bf_causal[:, :], kc("causal"))
            dve.tensor_copy(bf_half[:, :], kc("half", 2))
            dve.tensor_copy(bf_split[:, :], kc("split", 2))
            dve.wait_ge(wa_in, 16)
            dve.tensor_tensor(feat[:, :], wv("feat"), kc("block", C), ALU.mult).then_inc(ready, 1)

            def layernorm(value, new_row):
                st = {}
                for s in range(NU + 3):
                    if s < NU:
                        new_row(s)
                    if 0 <= s - 1 < NU:
                        u = s - 1
                        dve.wait_ge(S["hrow"][u], value[u])
                        st[u] = mark(dve.bn_stats(stats[u][:, 0:6], hs[u][:, :]))
                    if 0 <= s - 2 < NU:
                        u = s - 2
                        after(st[u])
                        mark(dve.memset(stats[u][:, 15:16], 0.0))
                        dve.bn_aggr(stats[u][:, 8:10], stats[u][:, 0:6]).then_inc(S["mv"][u], 1)
                    if 0 <= s - 3 < NU:
                        u = s - 3
                        dve.wait_ge(S["rstd"][u], value[u])
                        dve.tensor_scalar(xn[u][:, :], hs[u][:, :], stats[u][:, 8:9], stats[u][:, 10:11],
                                          ALU.subtract, ALU.mult).then_inc(S["xnr"][u], 1)

            def minus_norms(u, dst, shift):
                return dve.tensor_tensor(dst.rearrange("p (b h n) -> p b h n", b=2, h=HC), dash(u),
                                         shift.rearrange("p (b h) -> p b h", b=2).unsqueeze(3).broadcast_to([P, 2, HC, M]), ALU.subtract)

            def dash(u):
                return banks(u, 0, 2)[:, :, 0:HC * M].rearrange("p b (h n) -> p b h n", h=HC)

            STEPS_A = 6 * NU
            with dve.Fori(0, TURNS) as i:
                n1 = turn(dve, i)
                loop_base(i, 0, STEPS_A)
                for u in range(NU):
                    dve.wait_ge(S["sc_ps"][u], n1[u])
                    a = mark(dve.reduce_max(small[u][:, 0:1], bank(u, 1)[:, 0:P], AX))
                    after(a)
                    dve.tensor_scalar(small[u][:, 1:2], small[u][:, 0:1], -D ** -0.5, None, ALU.mult).then_inc(S["nmx"][u], 1)
                for u in range(NU):
                    dve.wait_ge(S["pT_ps"][u], n1[u])
                    dve.tensor_copy(big_b[u][:, 0:P], bank(u, 0)[:, 2 * P:3 * P]).then_inc(S["pT_sb"][u], 1)
                r = []
                for u in range(NU):
                    dve.wait_ge(S["p_sb"][u], n1[u])
                    r.append(mark(dve.reciprocal(small[u][:, 3:4], small[u][:, 2:3])))

                def token_row(u):
                    dve.wait_ge(S["px_ps"][u], n1[u] + CREDIT)
                    dve.wait_ge(S["hstore"][u], n1[u])
                    after(r[u])
                    dve.tensor_scalar(hs[u][:, :], bank(u, 1)[:, P:P + D], small[u][:, 3:4], None, ALU.mult).then_inc(S["hrow"][u], 1)

                layernorm(n1, token_row)
                for u in range(NU):
                    dve.wait_ge(S["v_ps"][u], n1[u])
                    for b in range(2):
                        dst = vbd_all[T * b:T * b + T, bass.ds(NU * i + u, 1), :].rearrange("p o (c b r d) -> p (o c) b r d", c=HC, b=2, r=2)
                        last = dve.tensor_copy(dst[:, :, b, :, 0:HD], bank(u, 1)[T * b:T * b + T, 320:512].rearrange("p (c r d) -> p c r d", c=HC, r=2))
                    last.then_inc(S["vbd"][u], 1)
                for u in range(NU):
                    dve.wait_ge(S["dash_ps"][u], n1[u])
                    a = mark(dve.tensor_copy(small[u][:, 20:32], bank(u, 1)[:, 264:264 + H]))
                    b = mark(dve.tensor_reduce(kmx_all[:, bass.ds(NU * i + u, 1)], banks(u, 0, 2)[:, :, 0:HC * M], mybir.AxisListType.XY, ALU.max))
                    after(a)
                    minus_norms(u, kd_all[:, bass.ds(NU * i + u, 1), :].rearrange("p o n -> p (o n)"), small[u][:, 20:32]).then_inc(S["kd"][u], 1)
                assert count[0] == STEPS_A, count
            before = TURNS * STEPS_A
            base[0] = 0
            dve.wait_ge(vstep, before)
            dve.reduce_max(kmax[:, 0:1], kmx_all[:, :], AX).then_inc(k_max, 1)
            dve.wait_ge(k_maxall, 1)
            dve.tensor_scalar(kmax[:, 2:3], kmax[:, 1:2], -1.0, None, ALU.mult).then_inc(k_negmax, 1)
            dve.wait_ge(wb_in, 32)
            dve.scalar_tensor_tensor(out=bias_mask[:, :], in0=bias_mask[:, :], scalar=HD3 ** 0.5, in1=kc("causal"),
                                     op0=ALU.mult, op1=ALU.add).then_inc(ready, 1)

            dve.wait_ge(S["hstore"][0], CREDIT + TILES)
            STEPS_B = 25 * NU
            with dve.Fori(0, TURNS) as i:
                n1 = turn(dve, i)
                m, l = stage_counts(dve, i)
                loop_base(i, before, STEPS_B)
                for u in range(NU):
                    dve.wait_ge(S["kv_ps"][u], n1[u] + CREDIT)
                    dve.wait_ge(S["store"][u], n1[u])
                    dve.tensor_tensor(kvs[u][:, :].rearrange("p (c n) -> p c n", c=HC), bank(u, 1)[0:2 * M, 0:408].rearrange("p (c n) -> p c n", c=HC),
                                      kc("kvmask", 2 * M).unsqueeze(1).broadcast_to([2 * M, HC, 68]), ALU.mult).then_inc(S["kv_sb"][u], 1)
                for u in range(NU):
                    dve.wait_ge(S["qd_ps"][u], n1[u])
                    a = mark(dve.tensor_reduce(small[u][:, 20:32].rearrange("p (b h) -> p b h", b=2), dash(u), AX, ALU.max))
                    after(a)
                    a = mark(dve.tensor_tensor(small[u][:, 32:44], small[u][:, 20:32], bank(u, 1)[:, 264:264 + H], ALU.add))
                    after(a)
                    minus_norms(u, qe[u][:, :], small[u][:, 32:44]).then_inc(S["qe"][u], 1)
                for u in range(NU):
                    dve.wait_ge(S["num_ps"][u], n1[u])
                    num = bank(u, 0)[:, 0:408].rearrange("p (c b r d) -> p c b r d", c=HC, b=2, r=2)
                    z = small[u][:, 20:44].rearrange("p (c b r) -> p c b r", c=HC, b=2)
                    a = mark(dve.reciprocal(z, num[:, :, :, :, 16]))
                    after(a)
                    for b in range(2):
                        rows = slice(T * b, T * b + T)
                        last = dve.tensor_tensor(att[u][rows, :].rearrange("p (c r d) -> p c r d", c=HC, r=2), num[rows, :, b, :, 0:HD],
                                                 z[rows, :, b, :].unsqueeze(3).broadcast_to([T, HC, 2, HD]), ALU.mult)
                    last.then_inc(S["attr"][u], 1)

                def output_stage(r):

                    def row(u):
                        dve.wait_ge(S["pr_ps"][u], m[r][u])
                        if r == 0:
                            old = h_all[:, bass.ds(NU * i + u, 1), :].rearrange("p o d -> p (o d)")
                        else:
                            old = hs[u][:, :]
                        dve.tensor_tensor(hs[u][:, :], bank(u, 1)[:, 2 * P:2 * P + D], old, ALU.add).then_inc(S["hrow"][u], 1)

                    layernorm(l[r], row)

                output_stage(0)
                for u in range(NU):
                    dve.wait_ge(S["fqk_ps"][u], n1[u])
                    dve.tensor_copy(big_a[u][0:HD3, 3 * P:6 * P], bank(u, 0)[HD3:P, 0:3 * P]).then_inc(S["kf_sb"][u], 1)
                st = {}
                for u in range(NU):
                    dve.wait_ge(S["qf_sb"][u], n1[u])
                    q = big_a[u][0:HD3, 0:P]
                    q2, y2 = (a.rearrange("p (b t) -> p b t", b=2) for a in (q, qc[u][:, :]))
                    after(mark(dve.tensor_scalar(qc[u][:, :], q, conv_w(1), conv_w(3), ALU.mult, ALU.add)))
                    after(mark(dve.scalar_tensor_tensor(out=y2[:, :, 1:T], in0=q2[:, :, 0:T - 1], scalar=conv_w(0), in1=y2[:, :, 1:T],
                                                        op0=ALU.mult, op1=ALU.add)))
                    dve.scalar_tensor_tensor(out=y2[:, :, 0:T - 1], in0=q2[:, :, 1:T], scalar=conv_w(2), in1=y2[:, :, 0:T - 1],
                                             op0=ALU.mult, op1=ALU.add).then_inc(S["conv"][u], 1)
                for u in range(NU):
                    dve.wait_ge(S["gl_ps"][u], n1[u])
                    st[u] = mark(dve.reduce_max(small[u][:, 7:8], bank(u, 1)[:, D:D + E3], AX))
                for u in range(NU):
                    after(st[u])
                    dve.tensor_scalar(small[u][:, 4:7], bank(u, 1)[:, D:D + E3], small[u][:, 7:8], None, ALU.subtract).then_inc(S["gs"][u], 1)
                for u in range(NU):
                    dve.wait_ge(S["fs_ps"][u], n1[u])
                    st[u] = mark(dve.tensor_reduce(small[u][:, 33:36], bank(u, 0)[:, 0:3 * P].rearrange("p (e n) -> p e n", e=E3), AX, ALU.max))
                for u in range(NU):
                    after(st[u])
                    dve.tensor_scalar(small[u][:, 36:39], small[u][:, 33:36], -HD3 ** -0.5, None, ALU.mult).then_inc(S["nf"][u], 1)
                for u in range(NU):
                    dve.wait_ge(S["ge"][u], n1[u])
                    st[u] = mark(dve.reciprocal(small[u][:, 15:16], small[u][:, 11:12]))
                for u in range(NU):
                    after(st[u])
                    dve.tensor_scalar(small[u][:, 12:15], small[u][:, 8:11], small[u][:, 15:16], None, ALU.mult).then_inc(S["gp"][u], 1)
                for u in range(NU):
                    dve.wait_ge(S["gp"][u], n1[u])
                    st[u] = mark(dve.tensor_reduce(small[u][:, 40:41], small[u][:, 12:15], AX, ALU.min))
                for u in range(NU):
                    after(st[u])
                    st[u] = mark(dve.scalar_tensor_tensor(out=small[u][:, 41:44], in0=small[u][:, 12:15], scalar=small[u][:, 40:41], in1=kc("eidx"),
                                                          op0=ALU.is_equal, op1=ALU.mult))
                for u in range(NU):
                    after(st[u])
                    st[u] = mark(dve.reduce_max(small[u][:, 44:45], small[u][:, 41:44], AX))
                for u in range(NU):
                    after(st[u])
                    dve.wait_ge(S["gep"][u], n1[u])
                    st[u] = mark(dve.scalar_tensor_tensor(out=small[u][:, 46:49], in0=small[u][:, 41:44], scalar=small[u][:, 44:45],
                                                          in1=small[u][:, 16:19], op0=ALU.not_equal, op1=ALU.mult))
                for u in range(NU):
                    after(st[u])
                    st[u] = mark(dve.reduce_sum(small[u][:, 49:50], small[u][:, 46:49], AX))
                for u in range(NU):
                    after(st[u])
                    st[u] = mark(dve.reciprocal(small[u][:, 50:51], small[u][:, 49:50]))
                for u in range(NU):
                    after(st[u])
                    st[u] = mark(dve.tensor_scalar(small[u][:, 51:54], small[u][:, 46:49], small[u][:, 50:51], None, ALU.mult))
                weight_step = dict(st)
                for u in range(NU):
                    dve.wait_ge(S["fpT_ps"][u], n1[u])
                    dve.tensor_copy(big_c[u][:, 0:3 * P], bank(u, 1)[:, 0:3 * P]).then_inc(S["fpT_sb"][u], 1)
                for u in range(NU):
                    dve.wait_ge(S["fo_ps"][u], n1[u])
                    fo = bank(u, 0)[:, 0:195].rearrange("p (e n) -> p e n", e=E3)
                    a = mark(dve.reciprocal(small[u][:, 54:57], fo[:, :, HD3]))
                    after(a)
                    a = mark(dve.tensor_tensor(small[u][:, 57:60], small[u][:, 54:57], small[u][:, 51:54], ALU.mult))
                    after(a)
                    dve.tensor_tensor(att[u][:, :].rearrange("p (e n) -> p e n", e=E3), fo[:, :, 0:HD3],
                                      small[u][:, 57:60].unsqueeze(2).broadcast_to([P, E3, HD3]), ALU.mult).then_inc(S["attr"][u], 1)
                output_stage(1)
                for u in range(NU):
                    dve.wait_ge(S["lv_ps"][u], n1[u])
                    for par in range(2):
                        last = dve.tensor_copy(v_place(u, 1, par), v_rows(u, 1, par))
                    last.then_inc(S["lv_d"][u], 1)
                for u in range(NU):
                    dve.wait_ge(S["ls_ps"][u], n1[u])
                    sc = banks(u, 0, 2)[:, :, 0:6 * T].rearrange("p b (h n) -> p b h n", h=HC)
                    mx = small[u][:, 20:32].rearrange("p (b h) -> p b h", b=2)
                    a = mark(dve.tensor_reduce(mx, sc, AX, ALU.max))
                    after(a)
                    dve.tensor_tensor(big_c[u][:, :].rearrange("p (b h n) -> p b h n", b=2, h=HC), sc,
                                      mx.unsqueeze(3).broadcast_to([P, 2, HC, T]), ALU.subtract).then_inc(S["pl"][u], 1)
                for u in range(NU):
                    dve.wait_ge(S["lo_ps"][u], n1[u])
                    lo = bank(u, 0)[:, 0:204].rearrange("p (h d) -> p h d", h=H)
                    a = mark(dve.reciprocal(small[u][:, 20:32], lo[:, :, HD]))
                    after(a)
                    dve.tensor_tensor(att[u][:, :].rearrange("p (h d) -> p h d", h=H), lo[:, :, 0:HD],
                                      small[u][:, 20:32].unsqueeze(2).broadcast_to([P, H, HD]), ALU.mult).then_inc(S["attr"][u], 1)
                output_stage(2)
                for u in range(NU):
                    dve.wait_ge(S["lg_ps"][u], n1[u])
                    dve.tensor_copy(lg_all[:, bass.ds(NU * i + u, 1), :].rearrange("p o n -> p (o n)"), bank(u, 1)[:, 0:EX]).then_inc(S["lg"][u], 1)
                assert count[0] == STEPS_B, count

            base[0] = before + TURNS * STEPS_B
            count[0] = 0

            def step(ins):
                after(mark(ins))

            def te(t, k):
                return t[:, k * P:(k + 1) * P].rearrange("p (t e) -> p t e", t=TILES)

            def over_e(v):
                return v.unsqueeze(2).broadcast_to([P, TILES, EX])

            def over_t(v):
                return v.unsqueeze(1).broadcast_to([P, TILES, EX])

            dve.wait_ge(S["lg"][0], CREDIT + TILES)
            s16 = [rsm[:, 16 * k:16 * k + 16] for k in range(4)]
            step(dve.memset(big_b[3][:, 0:P], 1.0))
            step(dve.tensor_reduce(s16[0], lg_all[:, :, :], AX, ALU.max))
            dve.tensor_tensor(te(big_b[2], 0), lg_all[:, :, :], over_e(s16[0]), ALU.subtract).then_inc(r_diff, 1)
            dve.wait_ge(r_exp, 1)
            step(dve.tensor_reduce(s16[1], te(big_b[2], 1), AX, ALU.add))
            step(dve.reciprocal(gate[:, :], s16[1]))
            step(dve.tensor_reduce(s16[2], te(big_b[2], 1), AX, ALU.max))
            step(dve.tensor_tensor(te(big_b[2], 2), te(big_b[2], 1), over_e(s16[2]), ALU.is_equal))
            step(dve.tensor_tensor(te(big_b[2], 3), te(big_b[2], 2), over_t(kc("eord")), ALU.mult))
            step(dve.tensor_reduce(s16[3], te(big_b[2], 3), AX, ALU.max))
            dve.tensor_tensor(te(big_b[2], 4), te(big_b[2], 3), over_e(s16[3]), ALU.is_equal).then_inc(r_onehot, 1)
            dve.wait_ge(r_count, 1)
            step(dve.tensor_copy(big_b[0][:, 0:P], bank(0, 1)[:, 0:P]))
            src, k = te(big_b[0], 0), 0
            for sh in (1, 2, 4, 8):
                dst = te(big_b[0], k + 1)
                mark(dve.tensor_copy(dst[:, 0:sh, :], src[:, 0:sh, :]))
                step(dve.tensor_tensor(dst[:, sh:, :], src[:, sh:, :], src[:, :TILES - sh, :], ALU.add))
                src, k = dst, k + 1
            step(dve.tensor_tensor(te(big_b[0], 5), src, te(big_b[0], 0), ALU.subtract))
            filled = te(big_c[0], 0).rearrange("p t e -> p (t e)").rearrange("p (e t) -> p e t", e=EX)
            step(dve.tensor_tensor(filled, src[:, TILES - 1, :].unsqueeze(2).broadcast_to([P, EX, TILES]),
                                   kc("thr").unsqueeze(1).broadcast_to([P, EX, TILES]), ALU.is_gt))
            e8 = [rsm[:, 64 + 8 * k:72 + 8 * k] for k in range(8)]
            step(dve.tensor_reduce(e8[0], filled, AX, ALU.add))
            src = e8[0]
            for k, sh in enumerate((1, 2, 4)):
                mark(dve.tensor_copy(e8[k + 1][:, 0:sh], src[:, 0:sh]))
                step(dve.tensor_tensor(e8[k + 1][:, sh:], src[:, sh:], src[:, :EX - sh], ALU.add))
                src = e8[k + 1]
            step(dve.tensor_tensor(e8[4], src, e8[0], ALU.subtract))
            step(dve.tensor_scalar(e8[5], e8[4], float(P), None, ALU.mult))
            step(dve.tensor_tensor(te(big_c[0], 1), te(big_b[0], 5), bank(0, 0)[:, 0:P].rearrange("p (t e) -> p t e", t=TILES), ALU.add))
            step(dve.tensor_tensor(te(big_c[0], 2), te(big_c[0], 1), over_t(e8[5]), ALU.add))
            step(dve.tensor_tensor(te(big_c[0], 3), te(big_c[0], 2), te(big_b[2], 4), ALU.mult))
            step(dve.tensor_reduce(s16[0], te(big_c[0], 3), AX, ALU.add))
            dve.tensor_copy(slots[:, :], s16[0]).then_inc(r_slots, 1)
            past = big_b[1][:, 0:SLOT_TILES * EX].rearrange("p (s e) -> p s e", e=EX)
            step(dve.tensor_tensor(past, src.unsqueeze(1).broadcast_to([P, SLOT_TILES, EX]),
                                   kc("slot").unsqueeze(2).broadcast_to([P, SLOT_TILES, EX]), ALU.is_le))
            step(dve.tensor_reduce(rsm[:, 128:128 + SLOT_TILES], past, AX, ALU.add))
            step(dve.tensor_scalar(rsm[:, 160:160 + SLOT_TILES], rsm[:, 128:128 + SLOT_TILES], float(EX - 1), None, ALU.min))
            dve.tensor_copy(tile_ex[:, :], rsm[:, 160:160 + SLOT_TILES]).then_inc(r_slots, 1)

            with dve.Fori(0, SLOT_TILES // NU) as i:
                n1 = turn(dve, i)
                for u in range(NU):
                    dve.wait_ge(Z["xT_ps"][u], n1[u])
                    dve.tensor_copy(xnT[u][0:C, :], bank(u, 0)[0:C, 0:2 * P]).then_inc(Z["xT_sb"][u], 1)
                for u in range(NU):
                    dve.wait_ge(Z["hT_ps"][u], n1[u])
                    dve.tensor_copy(big_c[u][:, :].rearrange("p (b n) -> p b n", b=2), banks(u, 0, 2)[:, :, 0:3 * P]).then_inc(Z["hT_sb"][u], 1)
                for u in range(NU):
                    dve.wait_ge(Z["y_ps"][u], n1[u])
                    dve.wait_ge(Z["y_out"][u], i * 16 + CREDIT)
                    dve.tensor_copy(att[u][:, :], bank(u, 1)[:, 0:D]).then_inc(Z["y_sb"][u], 1)

            for t in range(TILES):
                dve.wait_ge(gathered[t % 4], 16 * (t // 4 + 1))
                dve.scalar_tensor_tensor(out=h_all[:, t, :], in0=y_rows(t), scalar=gate[:, t:t + 1], in1=h_all[:, t, :],
                                         op0=ALU.mult, op1=ALU.add).then_inc(out_row, 1)

        @block.gpsimd
        def _(pool):
            pool.wait_ge(consts_in, 16)
            pool.memset(vbd_all, 0.0).then_inc(pstep, 1)
            for u in range(NU):
                pool.memset(pad[u][:, :], 0.0).then_inc(pstep, 1)
                pool.memset(vl[u][:, :], 0.0).then_inc(pstep, 1)
            pool.wait_ge(pstep, 1 + 2 * NU)
            for b in range(2):
                v = vbd_all[T * b:T * b + T].rearrange("p t (c b r d) -> p (t c) b r d", c=HC, b=2, r=2)
                for par in range(2):
                    pool.memset(v[:, :, b, par, HD:HD + 1], 1.0)
            for u in range(NU):
                for par in range(2):
                    v = vl[u][T * par:T * par + T, :].rearrange("p (c r d) -> p c r d", c=2 * HC, r=2)
                    last = pool.memset(v[:, :, par, HD:HD + 1], 1.0)
            last.then_inc(ready_p, 1)

            def rstd(u, value):
                pool.wait_ge(S["mv"][u], value[u])
                pool.tensor_tensor(stats[u][:, 11:12], stats[u][:, 9:10], kc("eps")[:, 0:1], ALU.add).then_inc(S["var_eps"][u], 1)
                pool.wait_ge(S["var_eps"][u], value[u])
                pool.tensor_tensor(stats[u][:, 10:11], stats[u][:, 11:12], kc("eps")[:, 1:2], ALU.pow).then_inc(S["rstd"][u], 1)

            with pool.Fori(0, TURNS) as i:
                n1 = turn(pool, i)
                for u in range(NU):
                    rstd(u, n1)
                for u in range(NU):
                    pool.wait_ge(S["hrow"][u], n1[u])
                    pool.tensor_copy(h_all[:, bass.ds(NU * i + u, 1), :].rearrange("p o d -> p (o d)"), hs[u][:, :]).then_inc(S["hstore"][u], 1)
                for u in range(NU):
                    pool.wait_ge(S["xnT_sb"][u], n1[u])
                    pool.tensor_copy(x_all[0:C, bass.ds(NU * i + u, 1), :].rearrange("p o d -> p (o d)"), xnT[u][0:C, :]).then_inc(S["xstore"][u], 1)
            pool.wait_ge(k_max, 1)
            pool.partition_all_reduce(kmax[:, 1:2], kmax[:, 0:1], P, bass.bass_isa.ReduceOp.max).then_inc(k_maxall, 1)
            pool.wait_ge(zero_out, 16)
            before = 1 + 2 * NU

            ROPE_STEPS = NU
            with pool.Fori(0, TURNS) as i:
                n1 = turn(pool, i)
                m, l = stage_counts(pool, i)
                rbase = pool.snap(i * ROPE_STEPS + before)
                for u in range(NU):
                    pool.wait_ge(S["k1e"][u], n1[u])
                    pool.tensor_tensor(k1[u][:, :], k1[u][:, :], kc("eps")[:, 2:3].broadcast_to([P, H * M]), ALU.add).then_inc(S["k1"][u], 1)
                for u in range(NU):
                    rstd(u, l[0])
                for u in range(NU):
                    rstd(u, l[1])
                for u in range(NU):
                    pool.wait_ge(S["lqk_sb"][u], n1[u])
                    src = big_a[u][:, 0:2 * D].rearrange("p (h r d) -> p h r d", r=2, d=8)
                    sin = kc("sin").rearrange("p (h r d) -> p h r d", r=2, d=8)
                    sw = big_b[u][:, 0:2 * D].rearrange("p (h r d) -> p h r d", r=2, d=8)
                    for r in range(2):
                        pool.tensor_tensor(sw[:, :, r, :], src[:, :, 1 - r, :], sin[:, :, r, :], ALU.mult)
                    pool.tensor_tensor(big_b[u][:, 2 * D:4 * D], big_a[u][:, 0:2 * D], kc("cos"), ALU.mult).then_inc(pstep, 1)
                    pool.wait_ge(pstep, rbase + (1 + u))
                    for s in range(2):
                        dst = pad[u][:, s * 3 * P:(s + 1) * 3 * P].rearrange("p (g j n) -> p g j n", g=3, j=4)[:, :, :, 0:HD]
                        a, b = (big_b[u][:, o + s * D:o + (s + 1) * D].rearrange("p (j g d) -> p g j d", j=4, g=3) for o in (0, 2 * D))
                        last = pool.tensor_tensor(dst, a, b, ALU.add)
                    last.then_inc(S["rope"][u], 1)
                for u in range(NU):
                    rstd(u, l[2])
                for u in range(NU):
                    pool.wait_ge(S["xnr"][u], l[2][u])
                    pool.tensor_copy(h_all[:, bass.ds(NU * i + u, 1), :].rearrange("p o d -> p (o d)"), hs[u][:, :])
                    pool.tensor_copy(x_all[:, bass.ds(NU * i + u, 1), 0:D].rearrange("p o d -> p (o d)"), xn[u][:, :]).then_inc(S["store"][u], 1)

            pool.wait_ge(zero_out, 16)
            pool.wait_ge(r_slots, 1)
            pool.wait_ge(S["store"][1], CREDIT + TILES)
            for t in range(TILES):
                pool.indirect_dma_start(out=xs_dram, out_offset=bass.IndirectOffsetOnAxis(ap=slots[:, t:t + 1], axis=0),
                                        in_=x_all[:, t, 0:D], in_offset=None).then_inc(scattered, 16)
            for u in range(NU):
                pool.wait_ge(Z["y_out"][u], CREDIT + 16 * (SLOT_TILES // NU))
            for t in range(TILES):
                if t >= 4:
                    pool.wait_ge(out_row, t - 3)
                pool.indirect_dma_start(out=y_rows(t), out_offset=None, in_=ys_dram,
                                        in_offset=bass.IndirectOffsetOnAxis(ap=slots[:, t:t + 1], axis=0)).then_inc(gathered[t % 4], 16)



def chunks(w, bias=None):
    n = w.shape[1]
    o = np.zeros((C + 1, 2, n), np.float32)
    o[:C, 0], o[:C, 1] = w[:C], w[C:]
    if bias is not None:
        o[C, 1] = bias
    return o.reshape(C + 1, 2 * n)


def kernel(**inputs):
    import concourse.bacc as bacc
    from concourse.bass_utils import run_bass_kernel_spmd

    a = {k: np.asarray(v) for k, v in inputs.items()}
    x = np.zeros((SEQS, T, D), np.float32)
    x[:, :(SEQ_IN + 1) // 2] = a["x"][:, ::2]

    wts = np.zeros((C + 1, NW), np.float32)

    def put(name, value):
        lo, hi = _W[name]
        wts[:value.shape[0], lo:hi] = value

    def by_expert(v):
        return v.reshape(v.shape[:-1] + (2, E3, HD3)).swapaxes(-3, -2).reshape(v.shape)

    put("a_qkv", chunks(a["L0_attn_W_qkv"]))
    put("feat", np.tile(a["L0_attn_proj_mat"].T, (HC, HC)))
    put("a_out", chunks(a["L0_attn_W_proj"], a["L0_attn_b_proj"]))
    put("f_qk", chunks(by_expert(a["L0_ffn_Wqk"]), by_expert(a["L0_ffn_bqk"])))
    put("f_v", chunks(a["L0_ffn_Wv"].transpose(1, 0, 2).reshape(D, D), a["L0_ffn_bv"].reshape(-1)))
    put("f_g1", chunks(a["L0_ffn_Wg1"], a["L0_ffn_bg1"]))
    put("f_g2", np.concatenate([a["L0_ffn_Wg2"], a["L0_ffn_bg2"][None]], 0))
    put("f_out", chunks(a["L0_ffn_Wp"], a["L0_ffn_bp"]))
    put("conv", np.concatenate([a["L0_ffn_conv_w"][:, 0, :], a["L0_ffn_conv_b"][:, None]], 1))
    put("l_qkv", chunks(a["L1_attn_w_qkv"].T, a["L1_attn_b_qkv"]))
    put("l_out", chunks(a["L1_attn_w_proj"].T, a["L1_attn_b_proj"]))
    put("m_g", chunks(a["L1_ffn_Wg"]))
    pos = np.zeros((P, P), np.float32)
    pos[:T, :T] = pos[T:, T:] = a["L0_ffn_pos_bias"]
    w1 = np.concatenate([chunks(a["L1_ffn_W1"][e], a["L1_ffn_b1"][e]) for e in range(EX)], 1)
    w2 = a["L1_ffn_W2"].reshape(EX, FT, P, D).transpose(2, 0, 1, 3).reshape(P, -1)

    arrays = {"x": x.reshape(TOKENS, D), "weights": wts, "consts": shape_constants(), "pos_bias": pos,
              "w1": w1, "w2": w2, "b2": a["L1_ffn_b2"].reshape(1, -1)}
    arrays = {f"in_{k}": np.ascontiguousarray(v) for k, v in arrays.items()}
    nc = bacc.Bacc("TRN2", target_bir_lowering=False, num_devices=1)
    aps = [nc.dram_tensor(k, v.shape, F32, kind="ExternalInput").ap() for k, v in arrays.items()]
    out = nc.dram_tensor("out", (TOKENS, D), F32, kind="ExternalOutput").ap()
    audio_tower(nc, *aps, out)
    got = run_bass_kernel_spmd(nc, [arrays], core_ids=[0])
    return got.results[0]["out"].reshape(SEQS, T, D)
```

```python
from contextlib import ExitStack

import numpy as np
import concourse.bass as bass
from concourse import mybir

F32 = mybir.dt.float32
BF16 = mybir.dt.bfloat16
I32 = mybir.dt.int32
U32 = mybir.dt.uint32
ALU = mybir.AluOpType
ACT = mybir.ActivationFunctionType
AX = mybir.AxisListType.X

SEQS, SEQ_IN, D = 32, 125, 192
T = 64
P = 128
TOKENS = SEQS * T
TILES = TOKENS // P
NU = 4
TURNS = TILES // NU
C = D // 2
H, HD = 12, 16
HC = H // 2
M = 44
FEPS = 1e-4
LNEPS = 1e-5
E3, HD3 = 3, 64
EX, FF = 8, 768
FT = FF // P
SLOT_TILES = (TOKENS + EX * (P - 1)) // P
SLOT_TURNS = -(-SLOT_TILES // NU)
BIG = -1e30
REC = 2 * D + 2

_W = {}
_n = 0
for _name, _cols in (("a_qkv", 2 * 3 * D), ("feat", HC * M), ("a_out", 2 * D), ("f_qk", 2 * 2 * D), ("f_v", 2 * D),
                     ("f_g1", 2 * 32), ("f_g2", E3), ("f_out", 2 * D), ("conv", 4), ("l_qkv", 2 * 3 * D),
                     ("l_out", 2 * D), ("m_g", 2 * EX)):
    _W[_name] = (_n, _n + _cols)
    _n += _cols
NW = _n
NW_A = _W["feat"][1]

_K = {}
_n = 0
for _name, _cols in (("ident", P), ("half", P), ("split", P), ("causal", P), ("diag", HC), ("eps", 3), ("block", HC * M),
                     ("fold", T), ("headmask", 4 * T), ("kvmask", 68), ("cos", 2 * D), ("sin", 2 * D), ("triu", P), ("eidx", E3), ("eord", EX),
                     ("thr", TILES), ("slot", SLOT_TILES), ("ids", TILES), ("no_id", 1)):
    _K[_name] = (_n, _n + _cols)
    _n += _cols
NK = _n
NK_A = _K["block"][1]


def shape_constants():
    k = np.zeros((P, NK), np.float32)

    def put(name, rows, value):
        a, b = _K[name]
        k[:rows, a:b] = value

    put("ident", P, np.eye(P))
    seq = np.arange(P) // T
    put("fold", P, np.tile(np.eye(T), (2, 1)))
    put("headmask", P, np.kron(np.eye(4), np.ones((P // 4, T))))
    put("half", 2, np.stack([seq == 0, seq == 1]))
    put("split", 2, BIG * np.stack([seq == 1, seq == 0]))
    blk = np.zeros((C, HC, M))
    for h in range(HC):
        blk[16 * h:16 * h + 16, h] = HD ** -0.25
    put("block", C, blk.reshape(C, -1))
    dg = np.zeros((C, HC))
    for h in range(HC):
        dg[16 * h:16 * h + 16, h] = 0.5 * HD ** -0.5
    put("diag", C, dg)
    q, s = np.arange(P)[:, None], np.arange(P)[None, :]
    put("causal", P, np.where((q // T == s // T) & (s <= q), 0.0, BIG))
    kv = np.zeros((2 * M, 2, 2, 17))
    for par in range(2):
        kv[M * par:M * par + M, :, par] = 1.0
    put("kvmask", 2 * M, kv.reshape(2 * M, -1))
    inv = (1.0 / np.float32(10000.0) ** (np.arange(0, HD, 2, dtype=np.float32) / np.float32(HD))).astype(np.float32)
    fr = (np.arange(T, dtype=np.float32)[:, None] * inv[None, :]).astype(np.float32)
    cos, sin = np.cos(fr.astype(np.float64)), np.sin(fr.astype(np.float64))
    cos, sin = np.tile(cos, (2, 1)), np.tile(sin, (2, 1))
    cos = np.concatenate([cos, cos], -1)
    sin = np.concatenate([-sin, sin], -1)
    scale = np.array([HD ** -0.5, 1.0])[None, :, None, None]
    put("cos", P, (cos[:, None, None, :] * scale * np.ones((1, 1, H, 1))).reshape(P, -1))
    put("sin", P, (sin[:, None, None, :] * scale * np.ones((1, 1, H, 1))).reshape(P, -1))
    put("triu", P, (q < s).astype(np.float32))
    put("eidx", P, np.arange(1, E3 + 1))
    put("eord", P, EX - np.arange(EX))
    put("thr", P, P * np.arange(TILES))
    put("slot", P, np.arange(SLOT_TILES))
    put("ids", P, P * np.arange(TILES) + np.arange(P)[:, None])
    put("no_id", P, TOKENS + np.arange(P)[:, None])
    put("eps", P, np.array([LNEPS, -0.5, FEPS]))
    return k


def audio_tower(nc, x, weights, consts, pos_bias, w1, w2, b2, out):
    ctx = ExitStack()
    with ctx:
        def sb(name, shape, dt=F32):
            return ctx.enter_context(nc.sbuf_tensor(name, shape, dt))

        def each(name, shape, dt=F32):
            return [sb(f"{name}{u}", shape, dt) for u in range(NU)]

        def sem(name):
            return ctx.enter_context(nc.semaphore(name))

        def ev(name):
            return [sem(name)] * NU

        def ev_dma(name):
            return [sem(f"{name}_{u}") for u in range(NU)]

        sorted_dram = nc.dram_tensor("sorted", (SLOT_TILES * P, REC), F32, kind="Internal").ap()

        W = sb("weights_sb", [C + 1, NW])
        K = sb("consts_sb", [P, NK])

        def wv(name, c=None, rows=C):
            a, b = _W[name]
            if c is not None:
                n = (b - a) // 2
                a, b = a + c * n, a + c * n + n
            return W[0:rows, a:b]

        def kc(name, rows=P):
            return K[0:rows, _K[name][0]:_K[name][1]]

        ident = kc("ident")
        feat = wv("feat")
        bf_ident = sb("bf_ident", [P, P], BF16)
        bf_causal = sb("bf_causal", [P, P], BF16)
        bf_half = sb("bf_half", [2, P], BF16)
        bf_split = sb("bf_split", [2, P], BF16)
        bias_mask = sb("bias_mask", [P, P])
        all_tiles = sb("all_tiles", [P, TILES, 2 * P + D + 2])
        x_all = all_tiles[:, :, 0:2 * P]
        h_all = all_tiles[:, :, 2 * P:2 * P + D]
        records = all_tiles[:, :, 2 * P - D:]
        gate = records[:, :, 2 * D]
        stash = sb("stash", [P, TILES * (H * M + HC * 68)])
        kd_all = stash[:, 0:TILES * H * M].rearrange("p (t n) -> p t n", t=TILES)
        vbd_all = stash[:, TILES * H * M:].rearrange("p (t n) -> p t n", t=TILES)
        w1_sb = stash[:, 0:EX * 2 * FF]
        b2_sb = stash[:, EX * 2 * FF:EX * (2 * FF + D)]
        kmx_all = sb("kmx_all", [P, TILES])
        kmax = sb("kmax", [P, 4])
        lg_all = sb("lg_all", [P, TILES, EX])

        actT = each("actT", [C + 1, 2 * P])
        xnT = each("xnT", [C + 1, 2 * P])
        rows = each("rows", [P, 3 * D])
        hs = [r[:, 0:D] for r in rows]
        xn = [r[:, D:2 * D] for r in rows]
        att = [r[:, 2 * D:3 * D] for r in rows]
        kvs = [r[0:2 * M, 0:HC * 68] for r in rows]
        stats = each("stats", [P, 16])
        small_all = sb("small", [P, NU, 64])
        small = [small_all[:, u, :] for u in range(NU)]
        big_b = each("big_b", [P, FF])
        big_c = each("big_c", [P, FF])
        shared = sb("shared", [P, NU * (FF + H * M + 6 * P + 2 * HC * 34)])

        def cut(start, n):
            return [shared[:, NU * start + u * n:NU * start + (u + 1) * n] for u in range(NU)]

        big_a = cut(0, FF)
        k1 = cut(FF, H * M)
        pad = cut(FF + H * M, 6 * P)
        vl = cut(FF + H * M + 6 * P, 2 * HC * 34)
        w2_sb = shared[:, 0:EX * FT * D]
        xin = [b[:, 0:D] for b in big_c]
        qe = [b[:, 0:H * M] for b in big_c]
        qc = [b[0:HD3, 3 * P:4 * P] for b in big_c]
        qkT = [b[0:C, 0:2 * P] for b in big_b]
        qksq = [b[0:C, 2 * P:4 * P] for b in big_b]
        blank = pad[0][:, 0:REC]
        rest = [all_tiles[:, u, 0:D + 2] for u in range(NU)]
        token = each("token", [P, 1], U32)
        vf = each("vf", [P, E3 * (HD3 + 1)])
        g1T = each("g1T", [33, P])

        rsm = sb("router_small", [P, 192])
        slots = sb("slots", [P, TILES], U32)
        tile_ex = sb("tile_ex", [P, SLOT_TILES], I32)

        ps = ctx.enter_context(nc.psum_tensor("ps", [P, 8, 512], F32))

        consts_in, wa_in, wb_in, moe_in = sem("consts_in"), sem("wa_in"), sem("wb_in"), sem("moe_in")
        w1_in, b2_in, zero_out = sem("w1_in"), sem("b2_in"), sem("zero_out")
        ready, ready_p = sem("ready"), sem("ready_p")
        ZEROED, MASKS, VALUES, FEATURES, BIAS_MASK = 1, 2, 3, 4, 5
        x_in = ev_dma("x_in")
        S = {n: ev(n) for n in """
            xT_ps xT_sb sc_ps nmx p_sb pT_ps pT_sb px_ps hstore xstore kT_ps v_ps k_sb vbd dash_ps kd
            k1e k1 qT_ps q_sb q_sq kv_ps qd_ps kv_sb qe qx q1T_ps q1T_sb num_ps
            fqk_ps fv_ps g1_sb qf_sb vf_sb kf_sb conv gl_ps gs ge gp gep kept weights fs_ps nf fp_sb fpT_ps fpT_sb fo_ps
            lqk_ps lv_ps lqk_sb lv_a lv_d rot rot_c rope rope_d lT_ps lk_ps lT_sb lk_sb ls_ps pl px lpT_ps lpT_sb lo_ps store lg_ps lg
            """.split()}
        R = [{n: ev(f"{n}{r}") for n in "hrow mv var_eps rstd xnr xnT_ps xnT_sb attr attT_ps attT_sb pr_ps".split()} for r in range(3)]
        k_max, k_maxall, k_negmax = sem("k_max"), sem("k_maxall"), sem("k_negmax")
        vstep, values_zero = sem("vstep"), sem("values_zero")
        r_diff, r_exp, r_onehot, r_count, r_slots = (sem(n) for n in ("r_diff", "r_exp", "r_onehot", "r_count", "r_slots"))
        scattered = sem("scattered")
        Z = {n: ev("m_" + n) for n in "xT_ps xT_sb w1_sb h_ps h_sb y_ps y_bias y_sb".split()}
        Z.update({n: ev_dma("m_" + n) for n in ("x_in", "rest_in", "y_out")})
        block = ctx.enter_context(nc.Block())

        def bank(u, b):
            return ps[:, 2 * u + b, :]

        def banks(u, a, b):
            return ps[:, 2 * u + a:2 * u + b, :]

        def flat(u):
            return banks(u, 0, 2).rearrange("p b n -> p (b n)")

        def turn(eng, i):
            return [eng.snap(i * NU + (u + 1)) for u in range(NU)]

        CREDIT = NU

        def give_credit(eng, sems):
            for s in sems:
                eng.sem_inc(s, CREDIT)

        def pair(eng, base, k):
            count = (lambda v: v) if isinstance(base, int) else eng.snap
            return [((2 * k + j) % NU, base + (2 * k + j), count(base + (2 * k + j + 1))) for j in range(2)]

        def half_turns(eng, half, loop_entry=None):
            half(pair(eng, 0, 0), [], [])
            half(pair(eng, 0, 1), pair(eng, 0, 0), [])
            with eng.Fori(0, TURNS - 1) as i:
                if loop_entry:
                    loop_entry(i)
                base = i * NU
                for k in range(2):
                    half(pair(eng, base, k + 2), pair(eng, base, k + 1), pair(eng, base, k))
            if loop_entry:
                loop_entry(None)
            half([], pair(eng, TILES - NU, 1), pair(eng, TILES - NU, 0))
            half([], [], pair(eng, TILES - NU, 1))

        def slot_tiles(eng, i, ahead=0):
            base = i * NU
            tiles = [(u, base + (u + ahead)) for u in range(NU)]
            if isinstance(i, int):
                return [(u, t, t + 1) for u, t in tiles if t < SLOT_TILES]
            return [(u, t, eng.snap(t + 1)) for u, t in tiles]

        def slot_turns(eng, work):
            with eng.Fori(0, SLOT_TURNS - 1) as i:
                work(slot_tiles(eng, i))
            work(slot_tiles(eng, SLOT_TURNS - 1))

        def following_turns(eng, work, first=0):
            for i in range(first):
                work(slot_tiles(eng, i), slot_tiles(eng, i + 1))
            with eng.Fori(0, SLOT_TURNS - 2 - first) as i:
                work(slot_tiles(eng, i, NU * first), slot_tiles(eng, i, NU * (first + 1)))
            work(slot_tiles(eng, SLOT_TURNS - 2), slot_tiles(eng, SLOT_TURNS - 1))
            work(slot_tiles(eng, SLOT_TURNS - 1), [])

        def slot_rows(a, t):
            return a[bass.ds(t, 1)].rearrange("o p d -> (o p) d")

        def x_count(eng, u, t):
            count = t * (16 // NU) + (16 - u * (16 // NU))
            return count if isinstance(t, int) else eng.snap(count)

        def y_out_count(eng, u, t):
            count = t * (16 // NU) - u * (16 // NU)
            return count if isinstance(t, int) else eng.snap(count)

        def ln_counts(eng, tiles, r):
            return [n if r else n + TILES if isinstance(n, int) else eng.snap(t + (TILES + 1)) for u, t, n in tiles]

        def credited(eng, t):
            return t + (1 + CREDIT) if isinstance(t, int) else eng.snap(t + (1 + CREDIT))

        def w1_used(eng, t):
            return t + (CREDIT - 1) if isinstance(t, int) else eng.snap(t + (CREDIT - 1))

        def w1_expert(u, c):
            return big_b[2 * (u % 2) + c]

        def gates(tiles, at, n=E3):
            return small_all[:, tiles[0][0]:tiles[0][0] + 2, at:at + n]

        def tile(a, t):
            return a[:, bass.ds(t, 1), :].rearrange("p o n -> p (o n)")

        def v_rows(u, b, par):
            return bank(u, 1)[T * b:T * b + T, 0:D].rearrange("p (c r d) -> p c r d", c=HC, r=2)[:, :, par, :]

        def v_place(u, b, par):
            return vl[u][T * par:T * par + T, :].rearrange("p (b c r d) -> p b c r d", b=2, c=HC, r=2)[:, b, :, par, 0:HD]

        def rotated(u, b):
            rows = slice(T * b, T * b + T)
            dst = pad[u][rows, :].rearrange("p (h b d) -> p h b d", h=2 * H, b=2)[:, :, b, :]
            return (dst, *(big_b[u][rows, o:o + 2 * D].rearrange("p (h d) -> p h d", h=2 * H) for o in (0, 2 * D)))

        def features(pe, u):
            for half in range(2):
                pe.matmul(bank(u, half)[:, 0:HC * M], qkT[u][:, half * P:half * P + P], feat[:, :], start=True, stop=True)

        def norms(pe, u):
            for half in range(2):
                last = pe.matmul(bank(u, 1)[:, 264 + HC * half:264 + HC * half + HC], qksq[u][:, half * P:half * P + P], kc("diag", C),
                                 start=True, stop=True)
            return last

        def conv_w(k):
            return wv("conv", rows=HD3)[:, k:k + 1]

        @block.sync
        def _(sp):
            sp.dma_start(K[:, 0:NK_A], consts[:, 0:NK_A]).then_inc(consts_in, 16)
            xt = x.rearrange("(t p) d -> t p d", p=P)
            with sp.Fori(0, TURNS) as i:
                n1 = turn(sp, i)
                for u in range(NU):
                    sp.wait_ge(S["px_ps"][u], n1[u])
                    sp.dma_start(xin[u][:, :], xt[bass.ds(NU * i + u, 1)].rearrange("o p d -> (o p) d")).then_inc(x_in[u], 16)
            sp.wait_ge(S["kv_ps"][0], CREDIT + TILES)
            sp.dma_start(w1_sb[0:C + 1, :], w1).then_inc(w1_in, 16)
            sp.dma_start(b2_sb, b2.broadcast_to([P, EX * D])).then_inc(b2_in, 16)
            sp.wait_ge(S["lg"][0], CREDIT + TILES)
            sp.dma_start(w2_sb, w2).then_inc(moe_in, 16)
            sp.wait_ge(scattered, 16 * TILES)
            st = sorted_dram.rearrange("(t p) d -> t p d", p=P)

            def rest_in(tiles):
                for u, t, n in tiles:
                    sp.wait_ge(Z["y_sb"][u], n)
                    sp.dma_start(rest[u], slot_rows(st, t)[:, D:REC]).then_inc(Z["rest_in"][u], 16)

            def rows_in(tiles, following):
                for (u, t, n), (_, t_next, _) in zip(tiles, following):
                    sp.wait_ge(Z["xT_ps"][u], n)
                    sp.dma_start(xn[u][:, :], slot_rows(st, t_next)[:, 0:D]).then_inc(Z["x_in"][u], 16)

            for u in range(NU):
                sp.dma_start(xn[u][:, :], st[u][:, 0:D]).then_inc(Z["x_in"][u], 16)
            with sp.Fori(0, SLOT_TURNS - 2) as i:
                rest_in(slot_tiles(sp, i))
                rows_in(slot_tiles(sp, i), slot_tiles(sp, i, NU))
            rest_in(slot_tiles(sp, SLOT_TURNS - 2))
            rows_in(slot_tiles(sp, SLOT_TURNS - 2), slot_tiles(sp, SLOT_TURNS - 1))
            rest_in(slot_tiles(sp, SLOT_TURNS - 1))
            for u in range(NU):
                sp.wait_ge(Z["y_out"][u], 16 * ((SLOT_TILES - u + NU - 1) // NU))

        @block.scalar
        def _(act):
            for u in range(2):
                act.wait_ge(x_in[u], 16)
            act.dma_start(W[:, 0:NW_A], weights[:, 0:NW_A]).then_inc(wa_in, 16)
            act.dma_start(W[:, NW_A:NW], weights[:, NW_A:NW]).then_inc(wb_in, 16)
            act.dma_start(K[:, NK_A:NK], consts[:, NK_A:NK]).then_inc(wb_in, 16)
            act.dma_start(bias_mask[:, :], pos_bias).then_inc(wb_in, 16)

            def half_a(head, tail, _):
                for j in range(2):
                    for u, t, n in tail[j:j + 1]:
                        act.wait_ge(R[0]["xnT_ps"][u], n)
                        act.wait_ge(S["xstore"][u], n)
                        act.activation(xnT[u][0:C, :], bank(u, 0)[0:C, 0:2 * P], ACT.Copy).then_inc(R[0]["xnT_sb"][u], 1)
                act.wait_ge(ready_p, 1)
                for j in range(2):
                    for u, t, n in tail[j:j + 1]:
                        act.wait_ge(S["kT_ps"][u], n)
                        act.activation(qkT[u][:, :], bank(u, 0)[0:C, 0:2 * P], ACT.Copy)
                        act.activation(qksq[u][:, :], bank(u, 0)[0:C, 0:2 * P], ACT.Square).then_inc(S["k_sb"][u], 1)
                    if j == 0:
                        for u, t, n in head:
                            act.wait_ge(S["xT_ps"][u], n)
                            act.activation(big_a[u][0:C, 0:2 * P], bank(u, 0)[0:C, 0:2 * P], ACT.Copy).then_inc(S["xT_sb"][u], 1)
                    for u, t, n in tail[j:j + 1]:
                        act.wait_ge(S["v_ps"][u], n)
                        for b in range(2):
                            dst = vbd_all[T * b:T * b + T, bass.ds(t, 1), :].rearrange("p o (c b r d) -> p (o c) b r d", c=HC, b=2, r=2)
                            last = act.activation(dst[:, :, b, :, 0:HD], bank(u, 1)[T * b:T * b + T, 320:512].rearrange("p (c r d) -> p c r d", c=HC, r=2),
                                                  ACT.Copy)
                        last.then_inc(S["vbd"][u], 1)
                    if j == 0:
                        for u, t, n in head:
                            act.wait_ge(S["nmx"][u], n)
                            act.activation(att[u][:, 0:P], bank(u, 1)[:, 0:P], ACT.Exp, scale=D ** -0.5, bias=small[u][:, 1:2],
                                           accum_out=small[u][:, 2:3]).then_inc(S["p_sb"][u], 1)

            half_turns(act, half_a)

            act.wait_ge(S["xstore"][0], CREDIT + TILES)
            def half(head, tail, late):
                for u, t, n in head:
                    act.wait_ge(S["qT_ps"][u], n)
                    act.activation(qkT[u][:, :], bank(u, 0)[0:C, 0:2 * P], ACT.Copy).then_inc(S["q_sb"][u], 1)
                for j in range(2):
                    for u, t, n in head[j:j + 1]:
                        act.wait_ge(S["q_sb"][u], n)
                        act.activation(qksq[u][:, :], qkT[u][:, :], ACT.Square).then_inc(S["q_sq"][u], 1)
                    for u, t, n in tail[j:j + 1]:
                        act.wait_ge(S["fpT_ps"][u], n)
                        act.activation(big_c[u][:, 0:3 * P], bank(u, 1)[:, 0:3 * P], ACT.Copy).then_inc(S["fpT_sb"][u], 1)
                act.wait_ge(k_negmax, 1)
                for u, t, n in head:
                    act.wait_ge(S["kv_ps"][u], n)
                    act.activation(k1[u][:, :], tile(kd_all, t), ACT.Exp, bias=kmax[:, 2:3]).then_inc(S["k1e"][u], 1)
                attended(tail, 1)
                for u, t, n in head:
                    act.wait_ge(S["qe"][u], n)
                    act.activation(qe[u][:, :], qe[u][:, :], ACT.Exp).then_inc(S["qx"][u], 1)
                for u, t, n in head:
                    act.wait_ge(S["q1T_ps"][u], n)
                    act.activation(big_a[u][0:2 * M, :].rearrange("p (b n) -> p b n", b=2), banks(u, 0, 2)[0:2 * M, :, 0:3 * P],
                                   ACT.Copy, bias=FEPS).then_inc(S["q1T_sb"][u], 1)
                normalized(late, 2)
                normalized(tail, 1)
                for j in range(2):
                    for u, t, n in tail[j:j + 1]:
                        act.wait_ge(S["lqk_ps"][u], n)
                        act.activation(big_a[u][:, 0:2 * D], bank(u, 0)[:, 0:2 * D], ACT.Copy).then_inc(S["lqk_sb"][u], 1)
                        act.wait_ge(S["lv_ps"][u], n)
                        for par in range(2):
                            last = act.activation(v_place(u, 0, par), v_rows(u, 0, par), ACT.Copy)
                        last.then_inc(S["lv_a"][u], 1)
                    if j == 0:
                        attended(head, 0)
                for u, t, n in tail:
                    act.wait_ge(S["lT_ps"][u], n)
                    act.activation(big_b[u][:, 0:3 * P], bank(u, 0)[:, 0:3 * P], ACT.Copy).then_inc(S["lT_sb"][u], 1)
                normalized(head, 0)
                for j in range(2):
                    for u, t, n in head[j:j + 1]:
                        act.wait_ge(S["fqk_ps"][u], n)
                        act.activation(g1T[u][0:32, :], bank(u, 0)[0:32, 3 * P:4 * P], ACT.Relu).then_inc(S["g1_sb"][u], 1)
                        act.activation(big_a[u][0:HD3, 0:3 * P], bank(u, 0)[0:HD3, 0:3 * P], ACT.Copy).then_inc(S["qf_sb"][u], 1)
                        act.wait_ge(S["fv_ps"][u], n)
                        act.activation(vf[u][:, :].rearrange("p (e n) -> p e n", e=E3)[:, :, 0:HD3],
                                       bank(u, 1)[:, 0:D].rearrange("p (e n) -> p e n", e=E3), ACT.Copy).then_inc(S["vf_sb"][u], 1)
                    for u, t, n in tail[j:j + 1]:
                        act.wait_ge(S["pl"][u], n)
                        act.activation(big_c[u][:, :], big_c[u][:, :], ACT.Exp).then_inc(S["px"][u], 1)
                for u, t, n in tail:
                    act.wait_ge(S["lpT_ps"][u], n)
                    act.activation(big_a[u][:, :].rearrange("p (b n) -> p b n", b=2), banks(u, 0, 2)[:, :, 0:3 * P],
                                   ACT.Copy).then_inc(S["lpT_sb"][u], 1)
                if head:
                    act.wait_ge(S["gs"][0], head[1][2])
                    act.activation(gates(head, 8), gates(head, 4), ACT.Exp).then_inc(S["ge"][0], 2)
                    act.wait_ge(S["gp"][0], head[1][2])
                    act.activation(gates(head, 16), gates(head, 12), ACT.Exp).then_inc(S["gep"][0], 2)
                attended(tail, 2)
                for u, t, n in head:
                    act.wait_ge(S["nf"][u], n)
                    for e in range(E3):
                        last = act.activation(big_b[u][:, e * P:e * P + P], bank(u, 0)[:, e * P:e * P + P], ACT.Exp,
                                              scale=HD3 ** -0.5, bias=small[u][:, 36 + e:37 + e])
                    last.then_inc(S["fp_sb"][u], 1)

            def attended(tiles, r):
                for u, t, n in tiles:
                    act.wait_ge(R[r]["attT_ps"][u], n)
                    act.activation(actT[u][0:C, :], bank(u, 1)[0:C, 0:2 * P], ACT.Copy).then_inc(R[r]["attT_sb"][u], 1)

            def normalized(tiles, r):
                for (u, t, n), count in zip(tiles, ln_counts(act, tiles, r)):
                    act.wait_ge(R[r]["xnT_ps"][u], count)
                    act.activation(xnT[u][0:C, :], bank(u, 0)[0:C, 0:2 * P], ACT.Copy).then_inc(R[r]["xnT_sb"][u], 1)

            half_turns(act, half)

            act.wait_ge(r_diff, 1)
            act.activation(big_b[2][:, P:2 * P], big_b[2][:, 0:P], ACT.Exp).then_inc(r_exp, 1)

            act.wait_ge(w1_in, 16)
            act.wait_ge(r_slots, 2)
            def first_layer(u, t, n):
                expert = act.value_load(tile_ex[0:1, bass.ds(t, 1)], min_val=0, max_val=EX - 1)
                act.wait_ge(Z["h_ps"][u], w1_used(act, t))
                for c in range(2):
                    last = act.activation(w1_expert(u, c)[0:C + 1, :], w1_sb[0:C + 1, bass.ds(expert * (2 * FF) + c * FF, FF)], ACT.Copy)
                last.then_inc(Z["w1_sb"][u], 1)

            def experts(tiles):
                for tile in tiles[0:2]:
                    first_layer(*tile)
                for u, t, n in tiles:
                    if u + 2 < len(tiles):
                        first_layer(*tiles[u + 2])
                    act.wait_ge(Z["h_ps"][u], credited(act, t))
                    act.activation(big_c[u][:, :].rearrange("p (b n) -> p b n", b=2), banks(u, 0, 2)[:, :, 0:3 * P],
                                   ACT.Silu).then_inc(Z["h_sb"][u], 1)

            slot_turns(act, experts)

        @block.tensor
        def _(pe):
            pe.wait_ge(consts_in, 16)

            def transposes(dst_bank, rows, src, cols, n, at=0, stride=P):
                for c in range(n):
                    last = pe.transpose(dst_bank[0:cols, at + stride * c:at + stride * c + rows], src[:, c * cols:(c + 1) * cols], ident)
                return last

            def project(dst, lhs, w, bias):
                pe.matmul(dst, lhs[0:C, 0:P], wv(w, 0), start=True, stop=False)
                k = C + 1 if bias else C
                return pe.matmul(dst, lhs[0:k, P:2 * P], wv(w, 1, k), start=False, stop=True)

            def half_a(head, tail, _):
                for u, t, n in tail:
                    pe.wait_ge(R[0]["xnr"][u], n)
                    transposes(bank(u, 0), P, xn[u], C, 2).then_inc(R[0]["xnT_ps"][u], 1)
                pe.wait_ge(wa_in, 16)
                for j in range(2):
                    for u, t, n in tail[j:j + 1]:
                        pe.wait_ge(R[0]["xnT_sb"][u], n)
                        for half in range(2):
                            for c in range(2):
                                last = pe.matmul(bank(u, 0)[0:C, half * P:half * P + P], wv("a_qkv", c)[:, D + half * C:D + half * C + C],
                                                 xnT[u][0:C, c * P:c * P + P], start=c == 0, stop=c == 1)
                        last.then_inc(S["kT_ps"][u], 1)
                        for c in range(2):
                            last = pe.matmul(bank(u, 1)[:, 320:512], xnT[u][0:C, c * P:c * P + P], wv("a_qkv", c)[:, 2 * D:3 * D],
                                             start=c == 0, stop=c == 1)
                        last.then_inc(S["v_ps"][u], 1)
                    if j == 0:
                        for u, t, n in head:
                            pe.wait_ge(x_in[u], x_count(pe, u, t))
                            pe.wait_ge(S["kd"][u], n)
                            transposes(bank(u, 0), P, xin[u], C, 2).then_inc(S["xT_ps"][u], 1)
                        pe.wait_ge(ready, MASKS)
                        for u, t, n in head:
                            pe.wait_ge(S["xT_sb"][u], n)
                            for c in range(2):
                                xT = big_a[u][0:C, c * P:c * P + P]
                                pe.matmul(bank(u, 1)[:, 0:P], xT, xT, start=c == 0, stop=False)
                            pe.matmul(bank(u, 1)[:, 0:P], bf_half[:, :], bf_split[:, :], start=False, stop=True).then_inc(S["sc_ps"][u], 1)
                for u, t, n in head:
                    pe.wait_ge(S["p_sb"][u], n)
                    pe.transpose(bank(u, 0)[:, 2 * P:3 * P], att[u][:, 0:P], ident).then_inc(S["pT_ps"][u], 1)
                pe.wait_ge(ready, FEATURES)
                for u, t, n in head:
                    pe.wait_ge(S["pT_sb"][u], n)
                    pe.matmul(bank(u, 1)[:, P:P + D], big_b[u][:, 0:P], xin[u][:, :], start=True, stop=True).then_inc(S["px_ps"][u], 1)
                for u, t, n in tail:
                    pe.wait_ge(S["k_sb"][u], n)
                    pe.wait_ge(S["vbd"][u], n)
                    features(pe, u)
                    norms(pe, u).then_inc(S["dash_ps"][u], 1)

            half_turns(pe, half_a)

            pe.wait_ge(wb_in, 48)
            pe.wait_ge(ready, BIAS_MASK)
            pe.wait_ge(ready_p, 3)
            pe.wait_ge(S["xstore"][0], CREDIT + TILES)
            def half(head, tail, late):
                for u, t, n in head:
                    for half in range(2):
                        for c in range(2):
                            last = pe.matmul(bank(u, 0)[0:C, half * P:half * P + P], wv("a_qkv", c)[:, half * C:half * C + C],
                                             tile(x_all, t)[0:C, c * P:c * P + P], start=c == 0, stop=c == 1)
                    last.then_inc(S["qT_ps"][u], 1)
                for u, t, n in tail:
                    pe.wait_ge(S["fp_sb"][u], n)
                    transposes(bank(u, 1), P, big_b[u], P, 3).then_inc(S["fpT_ps"][u], 1)
                for j in range(2):
                    for u, t, n in head[j:j + 1]:
                        pe.wait_ge(S["q_sb"][u], n)
                        for u_late, t_late, n_late in late[j:j + 1]:
                            pe.wait_ge(R[2]["hrow"][u_late], n_late)
                        features(pe, u)
                        pe.wait_ge(S["q_sq"][u], n)
                        norms(pe, u).then_inc(S["qd_ps"][u], 1)
                    if j == 0:
                        for u, t, n in tail:
                            pe.wait_ge(S["fpT_sb"][u], n)
                            for e in range(E3):
                                last = pe.matmul(bank(u, 0)[:, 65 * e:65 * e + 65], big_c[u][:, e * P:e * P + P], vf[u][:, 65 * e:65 * e + 65],
                                                 start=True, stop=True)
                            last.then_inc(S["fo_ps"][u], 1)
                attention_transposed(tail, 1)
                projected(tail, 1, "f_out")
                for u, t, n in head:
                    pe.wait_ge(S["qx"][u], n)
                    for b in range(2):
                        last = transposes(bank(u, b), P, qe[u][:, b * 6 * M:(b + 1) * 6 * M], 2 * M, 3)
                    last.then_inc(S["q1T_ps"][u], 1)
                if late:
                    for u, t, n in head:
                        pe.wait_ge(S["q1T_sb"][u], n)
                layernorm_transposed(late, 2)
                for u, t, n in head:
                    pe.wait_ge(S["q1T_sb"][u], n)
                    pe.wait_ge(S["k1"][u], n)
                    for c in range(HC):
                        last = pe.matmul(bank(u, 1)[0:2 * M, c * 68:c * 68 + 68], k1[u][:, c * 2 * M:(c + 1) * 2 * M],
                                         tile(vbd_all, t)[:, c * 68:c * 68 + 68], start=True, stop=True)
                    last.then_inc(S["kv_ps"][u], 1)
                layernorm_transposed(tail, 1)
                for u, t, n in head:
                    pe.wait_ge(S["kv_sb"][u], n)
                    for u_late, t_late, n_late in late:
                        if u_late == u:
                            pe.wait_ge(R[2]["xnT_sb"][u], n_late)
                    for c in range(HC):
                        last = pe.matmul(bank(u, 0)[:, c * 68:c * 68 + 68], big_a[u][0:2 * M, c * P:c * P + P],
                                         kvs[u][:, c * 68:c * 68 + 68], start=True, stop=True)
                    last.then_inc(S["num_ps"][u], 1)
                for j in range(2):
                    for u, t, n in tail[j:j + 1]:
                        pe.wait_ge(R[1]["xnT_sb"][u], n)
                        for c in range(2):
                            k = C + c
                            last = pe.matmul(bank(u, 0)[:, 0:2 * D], xnT[u][0:k, c * P:c * P + P], wv("l_qkv", c, k)[:, 0:2 * D], start=c == 0, stop=c == 1)
                        last.then_inc(S["lqk_ps"][u], 1)
                        for c in range(2):
                            k = C + c
                            last = pe.matmul(bank(u, 1)[:, 0:D], xnT[u][0:k, c * P:c * P + P], wv("l_qkv", c, k)[:, 2 * D:3 * D], start=c == 0, stop=c == 1)
                        last.then_inc(S["lv_ps"][u], 1)
                    if j == 0:
                        attention_transposed(head, 0)
                for u, t, n in late:
                    for u_head, t_head, n_head in head:
                        if u_head == u:
                            pe.wait_ge(R[0]["attT_sb"][u], n_head)
                    pe.wait_ge(R[2]["xnT_sb"][u], n)
                    project(bank(u, 1)[:, 3 * P + T:3 * P + T + EX], xnT[u], "m_g", False).then_inc(S["lg_ps"][u], 1)
                projected(head, 0, "a_out")
                for u, t, n in tail:
                    pe.wait_ge(S["rope"][u], n)
                    pe.wait_ge(S["rope_d"][u], n)
                    pe.wait_ge(S["lv_a"][u], n)
                    pe.wait_ge(S["lv_d"][u], n)
                    transposes(bank(u, 0), P, pad[u][:, 0:3 * P], P, 3).then_inc(S["lT_ps"][u], 1)
                    for g in range(3):
                        last = pe.matmul(bank(u, 1)[:, g * T:g * T + T], pad[u][:, (3 + g) * P:(4 + g) * P], kc("fold"), start=True, stop=True)
                    last.then_inc(S["lk_ps"][u], 1)
                layernorm_transposed(head, 0)
                counts = ln_counts(pe, head, 0)
                for j in range(2):
                    for (u, t, n), count in zip(head[j:j + 1], counts[j:j + 1]):
                        pe.wait_ge(R[0]["xnT_sb"][u], count)
                        for c in range(2):
                            k = C + c
                            last = pe.matmul(bank(u, 0)[0:32, 3 * P:4 * P], wv("f_g1", c, k), xnT[u][0:k, c * P:c * P + P], start=c == 0, stop=c == 1)
                        for e in range(E3):
                            for c in range(2):
                                k = C + c
                                last = pe.matmul(bank(u, 0)[:, e * P:e * P + P], wv("f_qk", c, k)[:, e * P:e * P + P],
                                                 xnT[u][0:k, c * P:c * P + P], start=c == 0, stop=c == 1)
                        last.then_inc(S["fqk_ps"][u], 1)
                        project(bank(u, 1)[:, 0:D], xnT[u], "f_v", True).then_inc(S["fv_ps"][u], 1)
                    for u, t, n in tail if j == 0 else []:
                        pe.wait_ge(S["lT_sb"][u], n)
                        pe.wait_ge(S["lk_sb"][u], n)
                        for g in range(3):
                            last = pe.matmul(flat(u)[:, g * 4 * T:(g + 1) * 4 * T], big_b[u][:, g * P:g * P + P], big_c[u][:, g * 4 * T:(g + 1) * 4 * T],
                                             start=True, stop=True)
                        last.then_inc(S["ls_ps"][u], 1)
                for u, t, n in tail:
                    pe.wait_ge(S["px"][u], n)
                    for b in range(2):
                        last = transposes(bank(u, b), P, big_c[u][:, b * 3 * P:(b + 1) * 3 * P], P, 3)
                    last.then_inc(S["lpT_ps"][u], 1)
                for j, (u, t, n) in enumerate(head):
                    pe.wait_ge(S["g1_sb"][u], n)
                    pe.wait_ge(S["vf_sb"][u], n)
                    pe.matmul(bank(head[0][0], 1)[:, D + E3 * j:D + E3 * j + E3], g1T[u][:, :], wv("f_g2", rows=33),
                              start=True, stop=True).then_inc(S["gl_ps"][u], 1)
                for u, t, n in tail:
                    pe.wait_ge(S["lpT_sb"][u], n)
                    for c in range(HC):
                        for b in range(2):
                            last = pe.matmul(bank(u, 0)[b * T:b * T + T, c * 34:c * 34 + 34], big_a[u][:, c * P + b * T:c * P + b * T + T],
                                             vl[u][:, (b * HC + c) * 34:(b * HC + c) * 34 + 34], start=True, stop=True)
                    last.then_inc(S["lo_ps"][u], 1)
                for j in range(2):
                    for u, t, n in head[j:j + 1]:
                        pe.wait_ge(S["qf_sb"][u], n)
                        pe.wait_ge(S["kf_sb"][u], n)
                        for e in (1, 2, 0):
                            if e == 0:
                                pe.wait_ge(S["conv"][u], n)
                            q = qc[u][:, :] if e == 0 else big_a[u][0:HD3, e * P:e * P + P]
                            dst = bank(u, 0)[:, e * P:e * P + P]
                            pe.matmul(dst, q, big_a[u][0:HD3, (3 + e) * P:(4 + e) * P], start=True, stop=False)
                            if e == 2:
                                last = pe.matmul(dst, ident, bias_mask[:, :], start=False, stop=True)
                            else:
                                last = pe.matmul(dst, bf_ident[:, :], bf_causal[:, :], start=False, stop=True)
                        last.then_inc(S["fs_ps"][u], 1)
                    if j == 0:
                        attention_transposed(tail, 2)
                projected(tail, 2, "l_out")

            def attention_transposed(tiles, r):
                for u, t, n in tiles:
                    pe.wait_ge(R[r]["attr"][u], n)
                    transposes(bank(u, 1), P, att[u], C, 2).then_inc(R[r]["attT_ps"][u], 1)

            def projected(tiles, r, w):
                for u, t, n in tiles:
                    pe.wait_ge(R[r]["attT_sb"][u], n)
                    project(bank(u, 1)[:, 2 * P:2 * P + D], actT[u], w, True).then_inc(R[r]["pr_ps"][u], 1)

            def layernorm_transposed(tiles, r):
                for (u, t, n), count in zip(tiles, ln_counts(pe, tiles, r)):
                    pe.wait_ge(R[r]["xnr"][u], count)
                    transposes(bank(u, 0), P, xn[u], C, 2).then_inc(R[r]["xnT_ps"][u], 1)

            half_turns(pe, half)

            pe.wait_ge(r_onehot, 1)
            pe.matmul(bank(0, 0)[:, 0:P], kc("triu"), big_b[2][:, 4 * P:5 * P], start=True, stop=True)
            pe.matmul(bank(0, 1)[:, 0:P], big_b[3][:, 0:P], big_b[2][:, 4 * P:5 * P], start=True, stop=True).then_inc(r_count, 1)

            pe.wait_ge(r_slots, 2)
            pe.wait_ge(moe_in, 16)
            def rows_transposed(tiles, before=[]):
                for j, (u, t, n) in enumerate(tiles):
                    for u_before, t_before, n_before in before[j:j + 1]:
                        pe.wait_ge(Z["h_sb"][u], n_before)
                    pe.wait_ge(Z["x_in"][u], x_count(pe, u, t))
                    transposes(bank(u, 0), P, xn[u], C, 2).then_inc(Z["xT_ps"][u], 1)

            def second_layer(tiles):
                for u, t, n in tiles:
                    expert = pe.value_load(tile_ex[0:1, bass.ds(t, 1)], min_val=0, max_val=EX - 1)
                    pe.wait_ge(Z["h_sb"][u], n)
                    for f in range(FT):
                        last = pe.matmul(bank(u, 1)[:, 0:D], big_c[u][:, f * P:f * P + P], w2_sb[:, bass.ds(expert * (FT * D) + f * D, D)],
                                         start=f == 0, stop=f == FT - 1)
                    last.then_inc(Z["y_ps"][u], 1)

            def experts(tiles, following):
                for u, t, n in tiles:
                    pe.wait_ge(Z["xT_sb"][u], n)
                    pe.wait_ge(Z["y_sb"][u], n)
                    pe.wait_ge(Z["w1_sb"][u], n)
                    for f in range(FT):
                        for c in range(2):
                            k = C + c
                            last = pe.matmul(bank(u, f // 3)[:, f % 3 * P:f % 3 * P + P],
                                             w1_expert(u, c)[0:k, f * P:f * P + P], xnT[u][0:k, c * P:c * P + P],
                                             start=c == 0, stop=c == 1)
                    last.then_inc(Z["h_ps"][u], 1)
                second_layer(tiles[0:2])
                rows_transposed(following, tiles)
                second_layer(tiles[2:])

            rows_transposed(slot_tiles(pe, 0))
            following_turns(pe, experts)

        @block.vector
        def _(dve):
            count = [0]
            base = [0]

            def mark(ins):
                count[0] += 1
                ins.then_inc(vstep, 1)
                return count[0]

            def after(step):
                dve.wait_ge(vstep, base[0] + step)

            give_credit(dve, [S[n][0] for n in ("kd", "hstore", "xstore", "store", "lg", "px_ps", "kv_ps")])
            give_credit(dve, [Z["y_sb"][0], Z["h_ps"][0]])
            for u in range(NU):
                last = dve.memset(pad[u][:, :], 0.0)
            last.then_inc(ready, 1)
            dve.wait_ge(consts_in, 16)
            dve.tensor_copy(bf_ident[:, :], ident)
            dve.tensor_copy(bf_causal[:, :], kc("causal"))
            dve.tensor_copy(bf_half[:, :], kc("half", 2))
            dve.tensor_copy(bf_split[:, :], kc("split", 2)).then_inc(ready, 1)
            for u in range(NU):
                last = dve.memset(vl[u][:, :], 0.0)
            last.then_inc(ready, 1)
            for u in range(NU):
                dve.memset(vf[u][:, :], 1.0)
            dve.wait_ge(ready, VALUES)
            for u in range(NU):
                for par in range(2):
                    v = vl[u][T * par:T * par + T, :].rearrange("p (c r d) -> p c r d", c=2 * HC, r=2)
                    dve.memset(v[:, :, par, HD:HD + 1], 1.0)
            dve.wait_ge(wa_in, 16)
            dve.tensor_tensor(feat[:, :], wv("feat"), kc("block", C), ALU.mult).then_inc(ready, 1)

            def layernorm(tiles, r, new_row):
                if not tiles:
                    return

                def statistics(u, value):
                    dve.wait_ge(R[r]["hrow"][u], value)
                    return mark(dve.bn_stats(stats[u][:, 0:6], hs[u][:, :]))

                def aggregate(u, step):
                    after(step)
                    mark(dve.memset(stats[u][:, 15:16], 0.0))
                    dve.bn_aggr(stats[u][:, 8:10], stats[u][:, 0:6]).then_inc(R[r]["mv"][u], 1)

                def normalize(u, value):
                    dve.wait_ge(R[r]["rstd"][u], value)
                    dve.tensor_scalar(xn[u][:, :], hs[u][:, :], stats[u][:, 8:9], stats[u][:, 10:11],
                                      ALU.subtract, ALU.mult).then_inc(R[r]["xnr"][u], 1)

                new_row(tiles[0][0])
                for j, (u, value) in enumerate(tiles):
                    step = statistics(u, value)
                    if j + 1 < len(tiles):
                        new_row(tiles[j + 1][0])
                    aggregate(u, step)
                    if j >= 1:
                        normalize(*tiles[j - 1])
                normalize(*tiles[-1])

            def minus_norms(u, dst, shift):
                return dve.tensor_tensor(dst.rearrange("p (b h n) -> p b h n", b=2, h=HC), dash(u),
                                         shift.rearrange("p (b h) -> p b h", b=2).unsqueeze(3).broadcast_to([P, 2, HC, M]), ALU.subtract)

            def dash(u):
                return banks(u, 0, 2)[:, :, 0:HC * M].rearrange("p b (h n) -> p b h n", h=HC)

            def half_a(head, tail, _):
                for u, t, n in head:
                    dve.wait_ge(S["sc_ps"][u], n)
                    after(mark(dve.reduce_max(small[u][:, 0:1], bank(u, 1)[:, 0:P], AX)))
                    dve.tensor_scalar(small[u][:, 1:2], small[u][:, 0:1], -D ** -0.5, None, ALU.mult).then_inc(S["nmx"][u], 1)
                for u, t, n in head:
                    dve.wait_ge(S["pT_ps"][u], n)
                    dve.tensor_copy(big_b[u][:, 0:P], bank(u, 0)[:, 2 * P:3 * P]).then_inc(S["pT_sb"][u], 1)
                r = {}
                for u, t, n in head:
                    dve.wait_ge(S["p_sb"][u], n)
                    r[u] = mark(dve.reciprocal(small[u][:, 3:4], small[u][:, 2:3]))
                index = {u: (t, n) for u, t, n in head}

                def token_row(u):
                    t, n = index[u]
                    dve.wait_ge(S["px_ps"][u], credited(dve, t))
                    dve.wait_ge(S["hstore"][u], n)
                    after(r[u])
                    dve.tensor_scalar(hs[u][:, :], bank(u, 1)[:, P:P + D], small[u][:, 3:4], None, ALU.mult).then_inc(R[0]["hrow"][u], 1)

                layernorm([(u, n) for u, t, n in head], 0, token_row)
                for u, t, n in tail:
                    dve.wait_ge(S["dash_ps"][u], n)
                    a = mark(dve.tensor_copy(small[u][:, 20:32], bank(u, 1)[:, 264:264 + H]))
                    mark(dve.tensor_reduce(kmx_all[:, bass.ds(t, 1)], banks(u, 0, 2)[:, :, 0:HC * M], mybir.AxisListType.XY, ALU.max))
                    after(a)
                    minus_norms(u, tile(kd_all, t), small[u][:, 20:32]).then_inc(S["kd"][u], 1)

            steps = [0]

            def count_steps(half, in_head, in_tail, in_late):
                per_turn = 2 * (in_head + in_tail + in_late)
                start = []

                def counted(head, tail, late):
                    base[0], count[0] = steps[0], 0
                    half(head, tail, late)
                    assert count[0] == bool(head) * in_head + bool(tail) * in_tail + bool(late) * in_late, count
                    steps[0] = steps[0] + count[0]

                def loop_entry(i):
                    if i is None:
                        steps[0] = start[0] + (TURNS - 1) * per_turn
                    else:
                        start.append(steps[0])
                        steps[0] = dve.snap(i * per_turn + start[0])

                half_turns(dve, counted, loop_entry)

            count_steps(half_a, (2 + 2) * 2, 2 * 2, 0)
            dve.wait_ge(wb_in, 48)
            dve.scalar_tensor_tensor(out=bias_mask[:, :], in0=bias_mask[:, :], scalar=HD3 ** 0.5, in1=kc("causal"),
                                     op0=ALU.mult, op1=ALU.add).then_inc(ready, 1)
            dve.wait_ge(vstep, steps[0])
            dve.reduce_max(kmax[:, 0:1], kmx_all[:, :], AX).then_inc(k_max, 1)
            dve.wait_ge(k_maxall, 1)
            dve.tensor_scalar(kmax[:, 2:3], kmax[:, 1:2], -1.0, None, ALU.mult).then_inc(k_negmax, 1)

            dve.wait_ge(S["hstore"][0], CREDIT + TILES)
            def half(head, tail, late):
                output_stage(late, 2)
                for j in range(2):
                    for u, t, n in head[j:j + 1]:
                        dve.wait_ge(S["qd_ps"][u], n)
                        a = mark(dve.tensor_reduce(small[u][:, 20:32].rearrange("p (b h) -> p b h", b=2), dash(u), AX, ALU.max))
                        after(a)
                        a = mark(dve.tensor_tensor(small[u][:, 20:32], small[u][:, 20:32], bank(u, 1)[:, 264:264 + H], ALU.add))
                        after(a)
                        minus_norms(u, qe[u][:, :], small[u][:, 20:32]).then_inc(S["qe"][u], 1)
                    for u, t, n in tail if j == 0 else []:
                        dve.wait_ge(S["fo_ps"][u], n)
                        fo = bank(u, 0)[:, 0:195].rearrange("p (e n) -> p e n", e=E3)
                        dve.wait_ge(S["weights"][u], n)
                        a = mark(dve.reciprocal(small[u][:, 54:57], fo[:, :, HD3]))
                        after(a)
                        a = mark(dve.tensor_tensor(small[u][:, 57:60], small[u][:, 54:57], small[u][:, 51:54], ALU.mult))
                        after(a)
                        dve.tensor_tensor(att[u][:, :].rearrange("p (e n) -> p e n", e=E3), fo[:, :, 0:HD3],
                                          small[u][:, 57:60].unsqueeze(2).broadcast_to([P, E3, HD3]), ALU.mult).then_inc(R[1]["attr"][u], 1)
                output_stage(tail, 1)
                for u, t, n in head:
                    dve.wait_ge(S["kv_ps"][u], credited(dve, t))
                    dve.wait_ge(S["store"][u], n)
                    dve.tensor_tensor(kvs[u][:, :].rearrange("p (c n) -> p c n", c=HC), bank(u, 1)[0:2 * M, 0:408].rearrange("p (c n) -> p c n", c=HC),
                                      kc("kvmask", 2 * M).unsqueeze(1).broadcast_to([2 * M, HC, 68]), ALU.mult).then_inc(S["kv_sb"][u], 1)
                for u, t, n in head:
                    dve.wait_ge(S["num_ps"][u], n)
                    num = bank(u, 0)[:, 0:408].rearrange("p (c b r d) -> p c b r d", c=HC, b=2, r=2)
                    z = small[u][:, 8:32].rearrange("p (c b r) -> p c b r", c=HC, b=2)
                    a = mark(dve.reciprocal(z, num[:, :, :, :, 16]))
                    after(a)
                    for b in range(2):
                        rows = slice(T * b, T * b + T)
                        last = dve.tensor_tensor(att[u][rows, :].rearrange("p (c r d) -> p c r d", c=HC, r=2), num[rows, :, b, :, 0:HD],
                                                 z[rows, :, b, :].unsqueeze(3).broadcast_to([T, HC, 2, HD]), ALU.mult)
                    last.then_inc(R[0]["attr"][u], 1)
                for u, t, n in tail:
                    dve.wait_ge(S["lqk_sb"][u], n)
                    dve.tensor_tensor(big_b[u][:, 2 * D:4 * D], big_a[u][:, 0:2 * D], kc("cos"), ALU.mult).then_inc(S["rot_c"][u], 1)
                    dve.wait_ge(S["lv_ps"][u], n)
                    for par in range(2):
                        last = dve.tensor_copy(v_place(u, 1, par), v_rows(u, 1, par))
                    last.then_inc(S["lv_d"][u], 1)
                for u, t, n in tail:
                    dve.wait_ge(S["rot_c"][u], n)
                    dve.wait_ge(S["rot"][u], n)
                    dve.tensor_tensor(*rotated(u, 1), ALU.add).then_inc(S["rope_d"][u], 1)
                output_stage(head, 0, late)
                for u, t, n in tail:
                    dve.wait_ge(S["lk_ps"][u], n)
                    dve.tensor_tensor(big_c[u][:, :].rearrange("p (g j n) -> p g j n", g=3, j=4),
                                      bank(u, 1)[:, 0:3 * T].rearrange("p (g n) -> p g n", g=3).unsqueeze(2).broadcast_to([P, 3, 4, T]),
                                      kc("headmask").rearrange("p (j n) -> p j n", j=4).unsqueeze(1).broadcast_to([P, 3, 4, T]),
                                      ALU.mult).then_inc(S["lk_sb"][u], 1)
                for j in range(2):
                    for u, t, n in head[j:j + 1]:
                        dve.wait_ge(S["fqk_ps"][u], n)
                        dve.tensor_copy(big_a[u][0:HD3, 3 * P:6 * P], bank(u, 0)[HD3:P, 0:3 * P]).then_inc(S["kf_sb"][u], 1)
                        dve.wait_ge(S["qf_sb"][u], n)
                        q = big_a[u][0:HD3, 0:P]
                        q2, y2 = (a.rearrange("p (b t) -> p b t", b=2) for a in (q, qc[u][:, :]))
                        after(mark(dve.tensor_scalar(qc[u][:, :], q, conv_w(1), conv_w(3), ALU.mult, ALU.add)))
                        after(mark(dve.scalar_tensor_tensor(out=y2[:, :, 1:T], in0=q2[:, :, 0:T - 1], scalar=conv_w(0), in1=y2[:, :, 1:T],
                                                            op0=ALU.mult, op1=ALU.add)))
                        dve.scalar_tensor_tensor(out=y2[:, :, 0:T - 1], in0=q2[:, :, 1:T], scalar=conv_w(2), in1=y2[:, :, 0:T - 1],
                                                 op0=ALU.mult, op1=ALU.add).then_inc(S["conv"][u], 1)
                    for u, t, n in tail if j == 0 else []:
                        dve.wait_ge(S["ls_ps"][u], n)
                        sc = flat(u)[:, 0:H * T].rearrange("p (h n) -> p h n", h=H)
                        a = mark(dve.tensor_reduce(small[u][:, 20:32], sc, AX, ALU.max))
                        after(a)
                        dve.tensor_tensor(big_c[u][:, :].rearrange("p (h n) -> p h n", h=H), sc,
                                          small[u][:, 20:32].unsqueeze(2).broadcast_to([P, H, T]), ALU.subtract).then_inc(S["pl"][u], 1)
                if head:
                    gl = bank(head[0][0], 1)[:, D:D + 2 * E3].rearrange("p (u e) -> p u e", e=E3)
                    dve.wait_ge(S["gl_ps"][0], head[1][2])
                    after(mark(dve.tensor_reduce(gates(head, 7, 1), gl, AX, ALU.max)))
                    dve.tensor_tensor(gates(head, 4), gl, to3(head, 7), ALU.subtract).then_inc(S["gs"][0], 2)
                    dve.wait_ge(S["ge"][0], head[1][2])
                    after(mark(dve.tensor_reduce(gates(head, 11, 1), gates(head, 8), AX, ALU.add)))
                    after(mark(dve.reciprocal(gates(head, 15, 1), gates(head, 11, 1))))
                    dve.tensor_tensor(gates(head, 12), gates(head, 8), to3(head, 15), ALU.mult).then_inc(S["gp"][0], 2)
                for u, t, n in tail:
                    dve.wait_ge(S["lo_ps"][u], n)
                    lo = bank(u, 0)[:, 0:204].rearrange("p (h d) -> p h d", h=H)
                    a = mark(dve.reciprocal(small[u][:, 20:32], lo[:, :, HD]))
                    after(a)
                    dve.tensor_tensor(att[u][:, :].rearrange("p (h d) -> p h d", h=H), lo[:, :, 0:HD],
                                      small[u][:, 20:32].unsqueeze(2).broadcast_to([P, H, HD]), ALU.mult).then_inc(R[2]["attr"][u], 1)
                for j in range(2):
                    for u, t, n in head[j:j + 1]:
                        dve.wait_ge(S["fs_ps"][u], n)
                        after(mark(dve.tensor_reduce(small[u][:, 33:36], bank(u, 0)[:, 0:3 * P].rearrange("p (e n) -> p e n", e=E3), AX, ALU.max)))
                        dve.tensor_scalar(small[u][:, 36:39], small[u][:, 33:36], -HD3 ** -0.5, None, ALU.mult).then_inc(S["nf"][u], 1)
                    if head and j == 0:
                        dve.wait_ge(S["gp"][0], head[1][2])
                        after(mark(dve.tensor_reduce(gates(head, 40, 1), gates(head, 12), AX, ALU.min)))
                        after(mark(dve.tensor_tensor(gates(head, 41), gates(head, 12), to3(head, 40), ALU.is_equal)))
                        after(mark(dve.tensor_tensor(gates(head, 45), gates(head, 41), kc("eidx").unsqueeze(1).broadcast_to([P, 2, E3]), ALU.mult)))
                        after(mark(dve.tensor_reduce(gates(head, 44, 1), gates(head, 45), AX, ALU.max)))
                        dve.tensor_tensor(gates(head, 41), gates(head, 45), to3(head, 44), ALU.not_equal).then_inc(S["kept"][0], 2)
                if head:
                    dve.wait_ge(S["gep"][0], head[1][2])
                    dve.wait_ge(S["kept"][0], head[1][2])
                    after(mark(dve.tensor_tensor(gates(head, 48), gates(head, 41), gates(head, 16), ALU.mult)))
                    after(mark(dve.tensor_reduce(gates(head, 60, 1), gates(head, 48), AX, ALU.add)))
                    after(mark(dve.reciprocal(gates(head, 61, 1), gates(head, 60, 1))))
                    dve.tensor_tensor(gates(head, 51), gates(head, 48), to3(head, 61), ALU.mult).then_inc(S["weights"][0], 2)

            def router_logits(late):
                for u, t, n in late:
                    dve.wait_ge(S["lg_ps"][u], n)
                    dve.tensor_copy(tile(lg_all, t), bank(u, 1)[:, 3 * P + T:3 * P + T + EX]).then_inc(S["lg"][u], 1)

            def output_stage(tiles, r, late=[]):
                if not tiles:
                    router_logits(late)
                index = {u: (t, n) for u, t, n in tiles}

                def row(u):
                    t, n = index[u]
                    dve.wait_ge(R[r]["pr_ps"][u], n)
                    old = hs[u][:, :] if r else tile(h_all, t)
                    dve.tensor_tensor(hs[u][:, :], bank(u, 1)[:, 2 * P:2 * P + D], old, ALU.add).then_inc(R[r]["hrow"][u], 1)
                    router_logits([x for x in late if x[0] == u])

                layernorm([(u, v) for (u, t, n), v in zip(tiles, ln_counts(dve, tiles, r))], r, row)

            def to3(tiles, at):
                return gates(tiles, at, 1).broadcast_to([P, 2, E3])

            count_steps(half, (2 + 1 + 2 + 2 + 1) * 2 + 10, (2 + 2 + 1 + 1) * 2, 2 * 2)

            base[0] = steps[0]
            count[0] = 0

            def step(ins):
                after(mark(ins))

            def te(t, k):
                return t[:, k * P:(k + 1) * P].rearrange("p (t e) -> p t e", t=TILES)

            def over_e(v):
                return v.unsqueeze(2).broadcast_to([P, TILES, EX])

            def over_t(v):
                return v.unsqueeze(1).broadcast_to([P, TILES, EX])

            dve.wait_ge(S["lg"][0], CREDIT + TILES)
            s16 = [rsm[:, 16 * k:16 * k + 16] for k in range(4)]
            mark(dve.memset(big_b[3][:, 0:P], 1.0))
            step(dve.tensor_reduce(s16[0], lg_all[:, :, :], AX, ALU.max))
            dve.tensor_tensor(te(big_b[2], 0), lg_all[:, :, :], over_e(s16[0]), ALU.subtract).then_inc(r_diff, 1)
            mark(dve.tensor_copy(records[:, :, 2 * D + 1], kc("ids")))
            dve.wait_ge(r_exp, 1)
            step(dve.tensor_reduce(s16[2], te(big_b[2], 1), AX, ALU.max))
            step(dve.tensor_tensor(te(big_b[2], 2), te(big_b[2], 1), over_e(s16[2]), ALU.is_equal))
            step(dve.tensor_tensor(te(big_b[2], 3), te(big_b[2], 2), over_t(kc("eord")), ALU.mult))
            step(dve.tensor_reduce(s16[3], te(big_b[2], 3), AX, ALU.max))
            dve.tensor_tensor(te(big_b[2], 4), te(big_b[2], 3), over_e(s16[3]), ALU.is_equal).then_inc(r_onehot, 1)
            step(dve.tensor_reduce(s16[1], te(big_b[2], 1), AX, ALU.add))
            mark(dve.reciprocal(gate, s16[1]))
            dve.wait_ge(r_count, 1)
            step(dve.tensor_copy(big_b[0][:, 0:P], bank(0, 1)[:, 0:P]))
            src, k = te(big_b[0], 0), 0
            for sh in (1, 2, 4, 8):
                dst = te(big_b[0], k + 1)
                mark(dve.tensor_copy(dst[:, 0:sh, :], src[:, 0:sh, :]))
                step(dve.tensor_tensor(dst[:, sh:, :], src[:, sh:, :], src[:, :TILES - sh, :], ALU.add))
                src, k = dst, k + 1
            step(dve.tensor_tensor(te(big_b[0], 5), src, te(big_b[0], 0), ALU.subtract))
            filled = te(big_c[0], 0).rearrange("p t e -> p (t e)").rearrange("p (e t) -> p e t", e=EX)
            step(dve.tensor_tensor(filled, src[:, TILES - 1, :].unsqueeze(2).broadcast_to([P, EX, TILES]),
                                   kc("thr").unsqueeze(1).broadcast_to([P, EX, TILES]), ALU.is_gt))
            e8 = [rsm[:, 64 + 8 * k:72 + 8 * k] for k in range(8)]
            step(dve.tensor_reduce(e8[0], filled, AX, ALU.add))
            src = e8[0]
            for k, sh in enumerate((1, 2, 4)):
                mark(dve.tensor_copy(e8[k + 1][:, 0:sh], src[:, 0:sh]))
                step(dve.tensor_tensor(e8[k + 1][:, sh:], src[:, sh:], src[:, :EX - sh], ALU.add))
                src = e8[k + 1]
            step(dve.tensor_tensor(e8[4], src, e8[0], ALU.subtract))
            step(dve.tensor_scalar(e8[5], e8[4], float(P), None, ALU.mult))
            step(dve.tensor_tensor(te(big_c[0], 1), te(big_b[0], 5), bank(0, 0)[:, 0:P].rearrange("p (t e) -> p t e", t=TILES), ALU.add))
            step(dve.tensor_tensor(te(big_c[0], 2), te(big_c[0], 1), over_t(e8[5]), ALU.add))
            step(dve.tensor_tensor(te(big_c[0], 3), te(big_c[0], 2), te(big_b[2], 4), ALU.mult))
            step(dve.tensor_reduce(s16[0], te(big_c[0], 3), AX, ALU.add))
            dve.tensor_copy(slots[:, :], s16[0]).then_inc(r_slots, 1)
            past = big_b[1][:, 0:SLOT_TILES * EX].rearrange("p (s e) -> p s e", e=EX)
            step(dve.tensor_tensor(past, src.unsqueeze(1).broadcast_to([P, SLOT_TILES, EX]),
                                   kc("slot").unsqueeze(2).broadcast_to([P, SLOT_TILES, EX]), ALU.is_le))
            step(dve.tensor_reduce(rsm[:, 128:128 + SLOT_TILES], past, AX, ALU.add))
            step(dve.tensor_scalar(rsm[:, 160:160 + SLOT_TILES], rsm[:, 128:128 + SLOT_TILES], float(EX - 1), None, ALU.min))
            dve.tensor_copy(tile_ex[:, :], rsm[:, 160:160 + SLOT_TILES]).then_inc(r_slots, 1)

            dve.wait_ge(r_slots, 2)
            dve.wait_ge(b2_in, 16)
            def rows_transposed(tiles):
                for u, t, n in tiles:
                    dve.wait_ge(Z["xT_ps"][u], n)
                    dve.tensor_copy(xnT[u][0:C, :], bank(u, 0)[0:C, 0:2 * P]).then_inc(Z["xT_sb"][u], 1)

            def rows_made(tiles):
                for u, t, n in tiles:
                    expert = dve.value_load(tile_ex[0:1, bass.ds(t, 1)], min_val=0, max_val=EX - 1)
                    dve.wait_ge(Z["y_ps"][u], n)
                    if not isinstance(t, int) or t >= NU:
                        dve.wait_ge(Z["y_out"][u], y_out_count(dve, u, t))
                    dve.wait_ge(Z["rest_in"][u], x_count(dve, u, t))
                    dve.tensor_copy(token[u][:, :], rest[u][:, D + 1:D + 2])
                    dve.tensor_tensor(att[u][:, :], bank(u, 1)[:, 0:D], b2_sb[:, bass.ds(expert * D, D)], ALU.add).then_inc(Z["y_bias"][u], 1)
                    dve.wait_ge(Z["y_bias"][u], n)
                    dve.scalar_tensor_tensor(out=att[u][:, :], in0=att[u][:, :], scalar=rest[u][:, D:D + 1], in1=rest[u][:, 0:D],
                                             op0=ALU.mult, op1=ALU.add).then_inc(Z["y_sb"][u], 1)

            def experts(tiles, following):
                rows_made(tiles[0:2])
                rows_transposed(following)
                rows_made(tiles[2:])

            rows_transposed(slot_tiles(dve, 0))
            following_turns(dve, experts, 1)

        @block.gpsimd
        def _(pool):
            pool.memset(vbd_all, 0.0).then_inc(values_zero, 1)
            pool.wait_ge(values_zero, 1)
            for b in range(2):
                v = vbd_all[T * b:T * b + T].rearrange("p t (c b r d) -> p (t c) b r d", c=HC, b=2, r=2)
                for par in range(2):
                    last = pool.memset(v[:, :, b, par, HD:HD + 1], 1.0)
            last.then_inc(ready_p, 1)
            pool.wait_ge(ready_p, 1)
            for u in range(NU):
                pool.memset(actT[u][C:C + 1, :], 1.0)
                last = pool.memset(xnT[u][C:C + 1, :], 1.0)
            last.then_inc(ready_p, 1)
            pool.wait_ge(ready_p, 2)
            for u in range(NU):
                last = pool.memset(g1T[u][32:33, :], 1.0)
            last.then_inc(ready_p, 1)
            pool.wait_ge(ready_p, 3)
            pool.wait_ge(ready, ZEROED)
            pool.wait_ge(wb_in, 48)
            pool.tensor_copy(blank[:, REC - 1:REC], kc("no_id")).then_inc(ready_p, 1)
            pool.wait_ge(ready_p, 4)
            pool.dma_start(sorted_dram.rearrange("(t p) d -> p t d", p=P),
                           blank.unsqueeze(1).broadcast_to([P, SLOT_TILES, REC])).then_inc(zero_out, 16)
            pool.wait_ge(consts_in, 16)

            def rstd(u, value, r):
                pool.wait_ge(R[r]["mv"][u], value)
                pool.tensor_tensor(stats[u][:, 11:12], stats[u][:, 9:10], kc("eps")[:, 0:1], ALU.add).then_inc(R[r]["var_eps"][u], 1)
                pool.wait_ge(R[r]["var_eps"][u], value)
                pool.tensor_tensor(stats[u][:, 10:11], stats[u][:, 11:12], kc("eps")[:, 1:2], ALU.pow).then_inc(R[r]["rstd"][u], 1)

            def half_a(head, tail, _):
                for u, t, n in tail:
                    pool.wait_ge(R[0]["xnT_sb"][u], n)
                    pool.tensor_copy(tile(x_all, t)[0:C, :], xnT[u][0:C, :]).then_inc(S["xstore"][u], 1)
                for u, t, n in head:
                    rstd(u, n, 0)
                for u, t, n in head:
                    pool.wait_ge(R[0]["hrow"][u], n)
                    pool.tensor_copy(tile(h_all, t), hs[u][:, :]).then_inc(S["hstore"][u], 1)

            half_turns(pool, half_a)
            pool.wait_ge(k_max, 1)
            pool.partition_all_reduce(kmax[:, 1:2], kmax[:, 0:1], P, bass.bass_isa.ReduceOp.max).then_inc(k_maxall, 1)
            pool.wait_ge(zero_out, 16)
            pool.memset(blank[:, REC - 1:REC], 0.0)
            def half(head, tail, late):
                statistics(late, 2)
                for u, t, n in late:
                    pool.wait_ge(R[2]["xnr"][u], n)
                    pool.tensor_copy(tile(h_all, t), hs[u][:, :])
                    pool.tensor_copy(tile(records, t)[:, 0:D], xn[u][:, :]).then_inc(S["store"][u], 1)
                for u, t, n in head:
                    pool.wait_ge(S["k1e"][u], n)
                    pool.tensor_tensor(k1[u][:, :], k1[u][:, :], kc("eps")[:, 2:3].broadcast_to([P, H * M]), ALU.add).then_inc(S["k1"][u], 1)
                statistics(tail, 1)
                for u, t, n in tail:
                    pool.wait_ge(S["lqk_sb"][u], n)
                    src = big_a[u][:, 0:2 * D].rearrange("p (h r d) -> p h r d", r=2, d=8)
                    sin = kc("sin").rearrange("p (h r d) -> p h r d", r=2, d=8)
                    sw = big_b[u][:, 0:2 * D].rearrange("p (h r d) -> p h r d", r=2, d=8)
                    for r in range(2):
                        last = pool.tensor_tensor(sw[:, :, r, :], src[:, :, 1 - r, :], sin[:, :, r, :], ALU.mult)
                    last.then_inc(S["rot"][u], 1)
                    pool.wait_ge(S["rot"][u], n)
                    pool.wait_ge(S["rot_c"][u], n)
                    pool.tensor_tensor(*rotated(u, 0), ALU.add).then_inc(S["rope"][u], 1)
                statistics(head, 0)

            def statistics(tiles, r):
                for (u, t, n), value in zip(tiles, ln_counts(pool, tiles, r)):
                    rstd(u, value, r)

            half_turns(pool, half)

            pool.wait_ge(zero_out, 16)
            pool.wait_ge(r_slots, 1)
            pool.wait_ge(S["store"][1], CREDIT + TILES)
            for t in range(TILES):
                pool.indirect_dma_start(out=sorted_dram, out_offset=bass.IndirectOffsetOnAxis(ap=slots[:, t:t + 1], axis=0),
                                        in_=records[:, t, :], in_offset=None).then_inc(scattered, 16)

            bound = pool.to_reg(TOKENS - 1)

            def rows_out(tiles):
                for u, t, n in tiles:
                    pool.wait_ge(Z["y_sb"][u], credited(pool, t))
                    pool.tensor_tensor(lg_all.rearrange("p t e -> p (t e)")[:, bass.ds(t, 1)], kc("eps")[:, 0:1], kc("eps")[:, 0:1], ALU.add)
                    pool.indirect_dma_start(out=out, out_offset=bass.IndirectOffsetOnAxis(ap=token[u][:, :], axis=0),
                                            in_=att[u][:, :], in_offset=None, bounds_check=bound, oob_is_err=False).then_inc(Z["y_out"][u], 16)

            slot_turns(pool, rows_out)


def chunks(w, bias=None):
    n = w.shape[1]
    o = np.zeros((C + 1, 2, n), np.float32)
    o[:C, 0], o[:C, 1] = w[:C], w[C:]
    if bias is not None:
        o[C, 1] = bias
    return o.reshape(C + 1, 2 * n)


def kernel(**inputs):
    import concourse.bacc as bacc
    from concourse.bass_utils import run_bass_kernel_spmd

    a = {k: np.asarray(v) for k, v in inputs.items()}
    x = np.zeros((SEQS, T, D), np.float32)
    x[:, :(SEQ_IN + 1) // 2] = a["x"][:, ::2]

    wts = np.zeros((C + 1, NW), np.float32)

    def put(name, value):
        lo, hi = _W[name]
        wts[:value.shape[0], lo:hi] = value

    def by_expert(v):
        return v.reshape(v.shape[:-1] + (2, E3, HD3)).swapaxes(-3, -2).reshape(v.shape)

    put("a_qkv", chunks(a["L0_attn_W_qkv"]))
    put("feat", np.tile(a["L0_attn_proj_mat"].T, (HC, HC)))
    put("a_out", chunks(a["L0_attn_W_proj"], a["L0_attn_b_proj"]))
    put("f_qk", chunks(by_expert(a["L0_ffn_Wqk"]), by_expert(a["L0_ffn_bqk"])))
    put("f_v", chunks(a["L0_ffn_Wv"].transpose(1, 0, 2).reshape(D, D), a["L0_ffn_bv"].reshape(-1)))
    put("f_g1", chunks(a["L0_ffn_Wg1"], a["L0_ffn_bg1"]))
    put("f_g2", np.concatenate([a["L0_ffn_Wg2"], a["L0_ffn_bg2"][None]], 0))
    put("f_out", chunks(a["L0_ffn_Wp"], a["L0_ffn_bp"]))
    put("conv", np.concatenate([a["L0_ffn_conv_w"][:, 0, :], a["L0_ffn_conv_b"][:, None]], 1))
    put("l_qkv", chunks(a["L1_attn_w_qkv"].T, a["L1_attn_b_qkv"]))
    put("l_out", chunks(a["L1_attn_w_proj"].T, a["L1_attn_b_proj"]))
    put("m_g", chunks(a["L1_ffn_Wg"]))
    pos = np.zeros((P, P), np.float32)
    pos[:T, :T] = pos[T:, T:] = a["L0_ffn_pos_bias"]
    w1 = np.concatenate([chunks(a["L1_ffn_W1"][e], a["L1_ffn_b1"][e]) for e in range(EX)], 1)
    w2 = a["L1_ffn_W2"].reshape(EX, FT, P, D).transpose(2, 0, 1, 3).reshape(P, -1)

    arrays = {"x": x.reshape(TOKENS, D), "weights": wts, "consts": shape_constants(), "pos_bias": pos,
              "w1": w1, "w2": w2, "b2": a["L1_ffn_b2"].reshape(1, -1)}
    arrays = {f"in_{k}": np.ascontiguousarray(v) for k, v in arrays.items()}
    nc = bacc.Bacc("TRN2", target_bir_lowering=False, num_devices=1)
    aps = [nc.dram_tensor(k, v.shape, F32, kind="ExternalInput").ap() for k, v in arrays.items()]
    out = nc.dram_tensor("out", (TOKENS, D), F32, kind="ExternalOutput").ap()
    audio_tower(nc, *aps, out)
    got = run_bass_kernel_spmd(nc, [arrays], core_ids=[0])
    return got.results[0]["out"].reshape(SEQS, T, D)
```
